# Optimizing a Trainium2 kernel written in Bass

```python
import numpy as np
import jax
import jax.numpy as jnp

def _softmax(x, axis=-1):
    return jax.nn.softmax(x, axis=axis)

def _gelu(x):
    return jax.nn.gelu(x, approximate=True)

def _silu(x):
    return jax.nn.silu(x)

def _sigmoid(x):
    return jax.nn.sigmoid(x)

def _layernorm(x, axis=-1, eps=1e-05):
    m = jnp.mean(x, axis=axis, keepdims=True)
    v = jnp.var(x, axis=axis, keepdims=True)
    return (x - m) / jnp.sqrt(v + eps)

def _scatter_add(tgt, idx, src, axis=0):
    return tgt.at[idx].add(src)

def _segment_sum(src, seg, n):
    return jax.ops.segment_sum(src, seg, n)
kernel_name = 'mk_decoder_postln_d2_seqx_r8_e2c3ec'

def setup_inputs(seed: int=0):
    np.random.seed(seed)
    _w = jnp.asarray

    def _rec_inputs():
        import jax
        import jax.numpy as jnp
        _rk = jax.random.key(seed)
        x = -0.0002928 + 1 * jax.random.normal(jax.random.fold_in(_rk, 1), (8, 100, 128), jnp.float32)
        _lenS = 100 - jax.random.randint(jax.random.fold_in(_rk, 7), (8,), 0, max(1, 100 // 4) + 1, jnp.int32)
        _lenS2 = 1444 - jax.random.randint(jax.random.fold_in(_rk, 8), (8,), 0, max(1, 1444 // 4) + 1, jnp.int32)
        _ctx_1024P = jax.random.normal(jax.random.fold_in(_rk, 11), (8, 16, 128), jnp.float32)
        _ctx_1024c = jax.random.dirichlet(jax.random.fold_in(_rk, 511), 0.3 * jnp.ones((16,), jnp.float32), (8, 1444))
        _ctx_1024t = jnp.einsum('bsk,bkd->bsd', _ctx_1024c, _ctx_1024P)
        _ctx_1024t = _ctx_1024t * jax.lax.rsqrt(jnp.mean(jnp.square(_ctx_1024t)) + 1e-12) * 0.953939
        ctx_1024 = -1.39393e-06 + 0.999914 * (_ctx_1024t + 0.3 * jax.random.normal(jax.random.fold_in(_rk, 611), (8, 1444, 128), jnp.float32))
        return (x, ctx_1024)
    x, ctx_1024 = _rec_inputs()

    def _L0_attn_setup():
        import jax, jax.numpy as jnp
        import numpy as np
        import math
        B = 2
        L = 256
        D_MODEL = 128
        D_STATE = 16
        D_CONV = 4
        D_INNER = 2 * D_MODEL
        DT_RANK = math.ceil(D_MODEL / 16)
        DT_MIN, DT_MAX = (0.001, 0.1)

        def _dt_bias(k):
            dt = jnp.exp(jax.random.uniform(k, (D_INNER,)) * (math.log(DT_MAX) - math.log(DT_MIN)) + math.log(DT_MIN))
            dt = jnp.clip(dt, 0.0001, None)
            return (dt + jnp.log(-jnp.expm1(-dt))).astype(jnp.float32)

        def _causal_conv(x, w, b):
            out = jax.lax.conv_general_dilated(x, w[:, None, :], (1,), [(D_CONV - 1, 0)], dimension_numbers=('NCH', 'OIH', 'NCH'), feature_group_count=D_INNER)
            return out + b[None, :, None]

        def _selective_scan(u, dt, A, Bm, Cm, Dp, z):
            h0 = jnp.zeros((u.shape[0], u.shape[1], A.shape[1]), u.dtype)

            def step(h, inp):
                dt_l, u_l, B_l, C_l = inp
                h = jnp.exp(dt_l[..., None] * A) * h + (dt_l * u_l)[..., None] * B_l[:, None, :]
                return (h, jnp.einsum('bdn,bn->bd', h, C_l))
            xs = tuple((jnp.moveaxis(a, -1, 0) for a in (dt, u, Bm, Cm)))
            _, ys = jax.lax.scan(step, h0, xs)
            y = jnp.moveaxis(ys, 0, -1) + Dp[None, :, None] * u
            return y * jax.nn.silu(z)

        def _mamba_dir(xz, conv_w, conv_b, x_proj_w, dt_proj_w, dt_proj_b, A_log, Dp):
            x, z = jnp.split(xz, 2, axis=1)
            x = jax.nn.silu(_causal_conv(x, conv_w, conv_b))
            x_dbl = jnp.einsum('bdl,ed->bel', x, x_proj_w)
            dtv = x_dbl[:, :DT_RANK]
            Bm = x_dbl[:, DT_RANK:DT_RANK + D_STATE]
            Cm = x_dbl[:, DT_RANK + D_STATE:]
            dtv = jax.nn.softplus(jnp.einsum('brl,dr->bdl', dtv, dt_proj_w) + dt_proj_b[None, :, None])
            return _selective_scan(x, dtv, -jnp.exp(A_log), Bm, Cm, Dp, z)
        key = jax.random.key(seed)
        ks = jax.random.split(key, 14)
        nrm = lambda k, shape, s: (jax.random.normal(k, shape) * s).astype(jnp.float32)
        dt_std = DT_RANK ** (-0.5)
        A_log = jnp.log(jnp.broadcast_to(jnp.arange(1, D_STATE + 1, dtype=jnp.float32), (D_INNER, D_STATE)))
        return {'hidden_states': jax.random.normal(ks[0], (B, L, D_MODEL), dtype=jnp.float32), 'in_proj_w': nrm(ks[1], (2 * D_INNER, D_MODEL), D_MODEL ** (-0.5)), 'conv_w': nrm(ks[2], (D_INNER, D_CONV), 0.5), 'conv_b': nrm(ks[3], (D_INNER,), 0.1), 'x_proj_w': nrm(ks[4], (DT_RANK + 2 * D_STATE, D_INNER), D_INNER ** (-0.5)), 'dt_proj_w': jax.random.uniform(ks[5], (D_INNER, DT_RANK), minval=-dt_std, maxval=dt_std).astype(jnp.float32), 'dt_proj_b': _dt_bias(ks[6]), 'A_log': A_log, 'D': jnp.ones((D_INNER,), jnp.float32), 'conv_wb': nrm(ks[7], (D_INNER, D_CONV), 0.5), 'conv_bb': nrm(ks[8], (D_INNER,), 0.1), 'x_proj_wb': nrm(ks[9], (DT_RANK + 2 * D_STATE, D_INNER), D_INNER ** (-0.5)), 'dt_proj_wb': jax.random.uniform(ks[10], (D_INNER, DT_RANK), minval=-dt_std, maxval=dt_std).astype(jnp.float32), 'dt_proj_bb': _dt_bias(ks[11]), 'A_b_log': A_log, 'D_b': jnp.ones((D_INNER,), jnp.float32), 'out_proj_w': nrm(ks[12], (D_MODEL, D_INNER), D_INNER ** (-0.5))}
    _L0_attn_all = _L0_attn_setup()
    _L0_attn_in = {k: v for k, v in _L0_attn_all.items() if k in ('in_proj_w', 'conv_w', 'conv_b', 'x_proj_w', 'dt_proj_w', 'dt_proj_b', 'A_log', 'D', 'conv_wb', 'conv_bb', 'x_proj_wb', 'dt_proj_wb', 'dt_proj_bb', 'A_b_log', 'D_b', 'out_proj_w')}
    del _L0_attn_all

    def _L0_xattn_setup():
        import jax, jax.numpy as jnp
        import numpy as np
        D_MODEL = 128
        NUM_HEAD = 16
        HEAD_DIM = D_MODEL // NUM_HEAD
        D_OUT = 128
        B, S = (2, 256)
        key = jax.random.key(seed)
        ks = jax.random.split(key, 11)
        s = 0.02
        return {'Q': jax.random.normal(ks[0], (B, S, D_MODEL), jnp.float32), 'K': jax.random.normal(ks[1], (B, S, D_MODEL), jnp.float32), 'V': jax.random.normal(ks[2], (B, S, D_MODEL), jnp.float32), 'Wq': jax.random.normal(ks[3], (D_MODEL, D_MODEL), jnp.float32) * s, 'bq': jnp.zeros((D_MODEL,), jnp.float32), 'Wk': jax.random.normal(ks[4], (D_MODEL, D_MODEL), jnp.float32) * s, 'bk': jnp.zeros((D_MODEL,), jnp.float32), 'Wv': jax.random.normal(ks[5], (D_MODEL, D_MODEL), jnp.float32) * s, 'bv': jnp.zeros((D_MODEL,), jnp.float32), 'Wo': jax.random.normal(ks[6], (D_MODEL, D_OUT), jnp.float32) * s, 'bo': jnp.zeros((D_OUT,), jnp.float32)}
    _L0_xattn_all = _L0_xattn_setup()
    _L0_xattn_in = {k: v for k, v in _L0_xattn_all.items() if k in ('Wq', 'bq', 'Wk', 'bk', 'Wv', 'bv', 'Wo', 'bo')}
    del _L0_xattn_all

    def _L0_ffn_setup():
        import jax, jax.numpy as jnp
        import numpy as np
        B, N, D = (4, 256, 128)
        SPARSITY = 0.01
        key = jax.random.key(seed)
        k1, k2, k3 = jax.random.split(key, 3)
        x = jax.random.normal(k1, (B, N, D), dtype=jnp.float32)
        spatial = jax.random.normal(k2, (D, D), dtype=jnp.float32) * 0.02
        freq = jnp.fft.fft(spatial, axis=-1)
        k = int(D * SPARSITY)
        mag = jnp.abs(freq)
        kth = jax.lax.top_k(mag, k)[0][:, -1:]
        w_sparse = jnp.where(mag >= kth, freq, 0.0 + 0j)
        bias = jax.random.normal(k3, (D,), dtype=jnp.float32) * 0.01
        return {'x': x, 'w_freq_real': jnp.real(w_sparse).astype(jnp.float32), 'w_freq_imag': jnp.imag(w_sparse).astype(jnp.float32), 'bias': bias}
    _L0_ffn_all = _L0_ffn_setup()
    _L0_ffn_in = {k: v for k, v in _L0_ffn_all.items() if k in ('w_freq_real', 'w_freq_imag', 'bias')}
    del _L0_ffn_all

    def _L1_attn_setup():
        import jax, jax.numpy as jnp
        import numpy as np
        D_MODEL = 128
        NHEAD = 16
        NUM_KV_HEADS = 4
        HEAD_DIM = D_MODEL // NHEAD
        NUM_GROUPS = NHEAD // NUM_KV_HEADS
        SCALE = float(np.sqrt(HEAD_DIM))
        B, L = (1, 512)
        key = jax.random.key(seed)
        ks = jax.random.split(key, 9)
        s = 0.02
        kv_dim = NUM_KV_HEADS * HEAD_DIM
        return {'x': jax.random.normal(ks[0], (B, L, D_MODEL), dtype=jnp.float32), 'Wq': jax.random.normal(ks[1], (D_MODEL, D_MODEL), dtype=jnp.float32) * s, 'bq': jnp.zeros((D_MODEL,), dtype=jnp.float32), 'Wk': jax.random.normal(ks[2], (D_MODEL, kv_dim), dtype=jnp.float32) * s, 'bk': jnp.zeros((kv_dim,), dtype=jnp.float32), 'Wv': jax.random.normal(ks[3], (D_MODEL, kv_dim), dtype=jnp.float32) * s, 'bv': jnp.zeros((kv_dim,), dtype=jnp.float32), 'Wo': jax.random.normal(ks[4], (D_MODEL, D_MODEL), dtype=jnp.float32) * s, 'bo': jnp.zeros((D_MODEL,), dtype=jnp.float32)}
    _L1_attn_all = _L1_attn_setup()
    _L1_attn_in = {k: v for k, v in _L1_attn_all.items() if k in ('Wq', 'bq', 'Wk', 'bk', 'Wv', 'bv', 'Wo', 'bo')}
    del _L1_attn_all

    def _L1_xattn_setup():
        import jax, jax.numpy as jnp
        import numpy as np
        QUERY_DIM = 128
        CONTEXT_DIM = 128
        HEADS = 8
        DIM_HEAD = 64
        INNER = HEADS * DIM_HEAD
        SCALE = DIM_HEAD ** (-0.5)
        key = jax.random.key(seed)
        ks = jax.random.split(key, 7)
        B, N, M = (2, 256, 256)
        x = jax.random.normal(ks[0], (B, N, QUERY_DIM), dtype=jnp.float32)
        context = jax.random.normal(ks[1], (B, M, CONTEXT_DIM), dtype=jnp.float32)
        Wq = jax.random.normal(ks[2], (QUERY_DIM, INNER), dtype=jnp.float32) * QUERY_DIM ** (-0.5)
        Wk = jax.random.normal(ks[3], (CONTEXT_DIM, INNER), dtype=jnp.float32) * CONTEXT_DIM ** (-0.5)
        Wv = jax.random.normal(ks[4], (CONTEXT_DIM, INNER), dtype=jnp.float32) * CONTEXT_DIM ** (-0.5)
        Wo = jax.random.normal(ks[5], (INNER, QUERY_DIM), dtype=jnp.float32) * INNER ** (-0.5)
        bo = jax.random.normal(ks[6], (QUERY_DIM,), dtype=jnp.float32) * 0.01
        return {'x': x, 'context': context, 'Wq': Wq, 'Wk': Wk, 'Wv': Wv, 'Wo': Wo, 'bo': bo}
    _L1_xattn_all = _L1_xattn_setup()
    _L1_xattn_in = {k: v for k, v in _L1_xattn_all.items() if k in ('Wq', 'Wk', 'Wv', 'Wo', 'bo')}
    del _L1_xattn_all

    def _L1_ffn_setup():
        import jax, jax.numpy as jnp
        import numpy as np
        B, T, D, E, H = (4, 256, 128, 4, 8)
        EPS = 1e-05

        def _uniform(k, shape, bound):
            return jax.random.uniform(k, shape, jnp.float32, -bound, bound)

        def _layernorm(x, w, b):
            mu = jnp.mean(x, axis=-1, keepdims=True)
            var = jnp.mean(jnp.square(x - mu), axis=-1, keepdims=True)
            return (x - mu) * jax.lax.rsqrt(var + EPS) * w + b
        key = jax.random.key(seed)
        ks = jax.random.split(key, 12)
        wb = np.sqrt(6.0 / D) / np.sqrt(6.0)
        wb = 1.0 / np.sqrt(D)
        return {'x': jax.random.normal(ks[0], (B, T, D), jnp.float32), 'router_prob': jax.random.uniform(ks[1], (B, T, E), jnp.float32), 'norm_w': jnp.ones((D,), jnp.float32), 'norm_b': jnp.zeros((D,), jnp.float32), 'q_w': _uniform(ks[2], (D, D), wb), 'q_b': _uniform(ks[3], (D,), wb), 'k_w': _uniform(ks[4], (D, D), wb), 'k_b': _uniform(ks[5], (D,), wb), 'v_w': _uniform(ks[6], (D, D), wb), 'v_b': _uniform(ks[7], (D,), wb), 'o_w': _uniform(ks[8], (D, D), wb), 'o_b': _uniform(ks[9], (D,), wb)}
    _L1_ffn_all = _L1_ffn_setup()
    _L1_ffn_in = {k: v for k, v in _L1_ffn_all.items() if k in ('router_prob', 'norm_w', 'norm_b', 'q_w', 'q_b', 'k_w', 'k_b', 'v_w', 'v_b', 'o_w', 'o_b')}
    del _L1_ffn_all
    return {'x': x, 'ctx_1024': ctx_1024, 'L0_attn_in_proj_w': _L0_attn_in['in_proj_w'], 'L0_attn_conv_w': _L0_attn_in['conv_w'], 'L0_attn_conv_b': _L0_attn_in['conv_b'], 'L0_attn_x_proj_w': _L0_attn_in['x_proj_w'], 'L0_attn_dt_proj_w': _L0_attn_in['dt_proj_w'], 'L0_attn_dt_proj_b': _L0_attn_in['dt_proj_b'], 'L0_attn_A_log': _L0_attn_in['A_log'], 'L0_attn_D': _L0_attn_in['D'], 'L0_attn_conv_wb': _L0_attn_in['conv_wb'], 'L0_attn_conv_bb': _L0_attn_in['conv_bb'], 'L0_attn_x_proj_wb': _L0_attn_in['x_proj_wb'], 'L0_attn_dt_proj_wb': _L0_attn_in['dt_proj_wb'], 'L0_attn_dt_proj_bb': _L0_attn_in['dt_proj_bb'], 'L0_attn_A_b_log': _L0_attn_in['A_b_log'], 'L0_attn_D_b': _L0_attn_in['D_b'], 'L0_attn_out_proj_w': _L0_attn_in['out_proj_w'], 'L0_xattn_Wq': _L0_xattn_in['Wq'], 'L0_xattn_bq': _L0_xattn_in['bq'], 'L0_xattn_Wk': _L0_xattn_in['Wk'], 'L0_xattn_bk': _L0_xattn_in['bk'], 'L0_xattn_Wv': _L0_xattn_in['Wv'], 'L0_xattn_bv': _L0_xattn_in['bv'], 'L0_xattn_Wo': _L0_xattn_in['Wo'], 'L0_xattn_bo': _L0_xattn_in['bo'], 'L0_ffn_w_freq_real': _L0_ffn_in['w_freq_real'], 'L0_ffn_w_freq_imag': _L0_ffn_in['w_freq_imag'], 'L0_ffn_bias': _L0_ffn_in['bias'], 'L1_attn_Wq': _L1_attn_in['Wq'], 'L1_attn_bq': _L1_attn_in['bq'], 'L1_attn_Wk': _L1_attn_in['Wk'], 'L1_attn_bk': _L1_attn_in['bk'], 'L1_attn_Wv': _L1_attn_in['Wv'], 'L1_attn_bv': _L1_attn_in['bv'], 'L1_attn_Wo': _L1_attn_in['Wo'], 'L1_attn_bo': _L1_attn_in['bo'], 'L1_xattn_Wq': _L1_xattn_in['Wq'], 'L1_xattn_Wk': _L1_xattn_in['Wk'], 'L1_xattn_Wv': _L1_xattn_in['Wv'], 'L1_xattn_Wo': _L1_xattn_in['Wo'], 'L1_xattn_bo': _L1_xattn_in['bo'], 'L1_ffn_router_prob': _L1_ffn_in['router_prob'], 'L1_ffn_norm_w': _L1_ffn_in['norm_w'], 'L1_ffn_norm_b': _L1_ffn_in['norm_b'], 'L1_ffn_q_w': _L1_ffn_in['q_w'], 'L1_ffn_q_b': _L1_ffn_in['q_b'], 'L1_ffn_k_w': _L1_ffn_in['k_w'], 'L1_ffn_k_b': _L1_ffn_in['k_b'], 'L1_ffn_v_w': _L1_ffn_in['v_w'], 'L1_ffn_v_b': _L1_ffn_in['v_b'], 'L1_ffn_o_w': _L1_ffn_in['o_w'], 'L1_ffn_o_b': _L1_ffn_in['o_b']}

def reference(x, ctx_1024, L0_attn_in_proj_w, L0_attn_conv_w, L0_attn_conv_b, L0_attn_x_proj_w, L0_attn_dt_proj_w, L0_attn_dt_proj_b, L0_attn_A_log, L0_attn_D, L0_attn_conv_wb, L0_attn_conv_bb, L0_attn_x_proj_wb, L0_attn_dt_proj_wb, L0_attn_dt_proj_bb, L0_attn_A_b_log, L0_attn_D_b, L0_attn_out_proj_w, L0_xattn_Wq, L0_xattn_bq, L0_xattn_Wk, L0_xattn_bk, L0_xattn_Wv, L0_xattn_bv, L0_xattn_Wo, L0_xattn_bo, L0_ffn_w_freq_real, L0_ffn_w_freq_imag, L0_ffn_bias, L1_attn_Wq, L1_attn_bq, L1_attn_Wk, L1_attn_bk, L1_attn_Wv, L1_attn_bv, L1_attn_Wo, L1_attn_bo, L1_xattn_Wq, L1_xattn_Wk, L1_xattn_Wv, L1_xattn_Wo, L1_xattn_bo, L1_ffn_router_prob, L1_ffn_norm_w, L1_ffn_norm_b, L1_ffn_q_w, L1_ffn_q_b, L1_ffn_k_w, L1_ffn_k_b, L1_ffn_v_w, L1_ffn_v_b, L1_ffn_o_w, L1_ffn_o_b):
    import jax
    import jax.numpy as jnp

    def _L0_attn_ref(hidden_states, in_proj_w, conv_w, conv_b, x_proj_w, dt_proj_w, dt_proj_b, A_log, D, conv_wb, conv_bb, x_proj_wb, dt_proj_wb, dt_proj_bb, A_b_log, D_b, out_proj_w):
        import jax, jax.numpy as jnp
        import numpy as np
        import math
        B = 2
        L = 256
        D_MODEL = 128
        D_STATE = 16
        D_CONV = 4
        D_INNER = 2 * D_MODEL
        DT_RANK = math.ceil(D_MODEL / 16)
        DT_MIN, DT_MAX = (0.001, 0.1)

        def _dt_bias(k):
            dt = jnp.exp(jax.random.uniform(k, (D_INNER,)) * (math.log(DT_MAX) - math.log(DT_MIN)) + math.log(DT_MIN))
            dt = jnp.clip(dt, 0.0001, None)
            return (dt + jnp.log(-jnp.expm1(-dt))).astype(jnp.float32)

        def _causal_conv(x, w, b):
            out = jax.lax.conv_general_dilated(x, w[:, None, :], (1,), [(D_CONV - 1, 0)], dimension_numbers=('NCH', 'OIH', 'NCH'), feature_group_count=D_INNER)
            return out + b[None, :, None]

        def _selective_scan(u, dt, A, Bm, Cm, Dp, z):
            h0 = jnp.zeros((u.shape[0], u.shape[1], A.shape[1]), u.dtype)

            def step(h, inp):
                dt_l, u_l, B_l, C_l = inp
                h = jnp.exp(dt_l[..., None] * A) * h + (dt_l * u_l)[..., None] * B_l[:, None, :]
                return (h, jnp.einsum('bdn,bn->bd', h, C_l))
            xs = tuple((jnp.moveaxis(a, -1, 0) for a in (dt, u, Bm, Cm)))
            _, ys = jax.lax.scan(step, h0, xs)
            y = jnp.moveaxis(ys, 0, -1) + Dp[None, :, None] * u
            return y * jax.nn.silu(z)

        def _mamba_dir(xz, conv_w, conv_b, x_proj_w, dt_proj_w, dt_proj_b, A_log, Dp):
            x, z = jnp.split(xz, 2, axis=1)
            x = jax.nn.silu(_causal_conv(x, conv_w, conv_b))
            x_dbl = jnp.einsum('bdl,ed->bel', x, x_proj_w)
            dtv = x_dbl[:, :DT_RANK]
            Bm = x_dbl[:, DT_RANK:DT_RANK + D_STATE]
            Cm = x_dbl[:, DT_RANK + D_STATE:]
            dtv = jax.nn.softplus(jnp.einsum('brl,dr->bdl', dtv, dt_proj_w) + dt_proj_b[None, :, None])
            return _selective_scan(x, dtv, -jnp.exp(A_log), Bm, Cm, Dp, z)
        xz = jnp.einsum('bld,ed->bel', hidden_states, in_proj_w)
        out_f = _mamba_dir(xz, conv_w, conv_b, x_proj_w, dt_proj_w, dt_proj_b, A_log, D)
        out_b = _mamba_dir(xz[..., ::-1], conv_wb, conv_bb, x_proj_wb, dt_proj_wb, dt_proj_bb, A_b_log, D_b)
        y = out_f + out_b[..., ::-1]
        return jnp.einsum('bdl,od->blo', y, out_proj_w)

    def _L0_xattn_ref(Q, K, V, Wq, bq, Wk, bk, Wv, bv, Wo, bo):
        import jax, jax.numpy as jnp
        import numpy as np
        D_MODEL = 128
        NUM_HEAD = 16
        HEAD_DIM = D_MODEL // NUM_HEAD
        D_OUT = 128
        B, S = (2, 256)
        T = jnp.asarray(HEAD_DIM, Q.dtype) ** 0.5
        b = Q.shape[0]
        q = (Q @ Wq + bq) / T
        k = K @ Wk + bk
        v = V @ Wv + bv
        q = q.reshape(b, -1, NUM_HEAD, HEAD_DIM)
        k = k.reshape(b, -1, NUM_HEAD, HEAD_DIM)
        v = v.reshape(b, -1, NUM_HEAD, HEAD_DIM)
        scores = jnp.einsum('bqhd,bkhd->bhqk', q, k)
        attn = jax.nn.softmax(scores, axis=-1)
        out = jnp.einsum('bhqk,bkhd->bqhd', attn, v).reshape(b, -1, D_MODEL)
        return out @ Wo + bo

    def _L0_ffn_ref(x, w_freq_real, w_freq_imag, bias):
        import jax, jax.numpy as jnp
        import numpy as np
        B, N, D = (4, 256, 128)
        SPARSITY = 0.01
        w = jax.lax.complex(w_freq_real, w_freq_imag)
        x_freq = jnp.fft.fft(x, axis=-1)
        y_freq = jnp.einsum('bnd,do->bno', x_freq, w)
        y = jnp.real(jnp.fft.ifft(y_freq, axis=-1))
        return y + bias

    def _L1_attn_ref(x, Wq, bq, Wk, bk, Wv, bv, Wo, bo):
        import jax, jax.numpy as jnp
        import numpy as np
        D_MODEL = 128
        NHEAD = 16
        NUM_KV_HEADS = 4
        HEAD_DIM = D_MODEL // NHEAD
        NUM_GROUPS = NHEAD // NUM_KV_HEADS
        SCALE = float(np.sqrt(HEAD_DIM))
        B, L = (1, 512)
        Bsz, Ls, D = x.shape
        Q = (x @ Wq + bq).reshape(Bsz, Ls, NUM_KV_HEADS, NUM_GROUPS, HEAD_DIM)
        K = (x @ Wk + bk).reshape(Bsz, Ls, NUM_KV_HEADS, HEAD_DIM)
        V = (x @ Wv + bv).reshape(Bsz, Ls, NUM_KV_HEADS, HEAD_DIM)
        scores = jnp.einsum('bqkgd,blkd->bkgql', Q, K) / SCALE
        attn = jax.nn.softmax(scores, axis=-1)
        out = jnp.einsum('bkgql,blkd->bqkgd', attn, V)
        out = out.reshape(Bsz, Ls, D)
        return out @ Wo + bo

    def _L1_xattn_ref(x, context, Wq, Wk, Wv, Wo, bo):
        import jax, jax.numpy as jnp
        import numpy as np
        QUERY_DIM = 128
        CONTEXT_DIM = 128
        HEADS = 8
        DIM_HEAD = 64
        INNER = HEADS * DIM_HEAD
        SCALE = DIM_HEAD ** (-0.5)
        B, N, _ = x.shape
        M = context.shape[1]
        q = (x @ Wq).reshape(B, N, HEADS, DIM_HEAD)
        k = (context @ Wk).reshape(B, M, HEADS, DIM_HEAD)
        v = (context @ Wv).reshape(B, M, HEADS, DIM_HEAD)
        sim = jnp.einsum('bihd,bjhd->bhij', q.astype(jnp.float32), k.astype(jnp.float32)) * SCALE
        attn = jax.nn.softmax(sim, axis=-1).astype(v.dtype)
        out = jnp.einsum('bhij,bjhd->bihd', attn, v).reshape(B, N, INNER)
        return out @ Wo + bo

    def _L1_ffn_ref(x, router_prob, norm_w, norm_b, q_w, q_b, k_w, k_b, v_w, v_b, o_w, o_b):
        import jax, jax.numpy as jnp
        import numpy as np
        B, T, D, E, H = (4, 256, 128, 4, 8)
        EPS = 1e-05

        def _uniform(k, shape, bound):
            return jax.random.uniform(k, shape, jnp.float32, -bound, bound)

        def _layernorm(x, w, b):
            mu = jnp.mean(x, axis=-1, keepdims=True)
            var = jnp.mean(jnp.square(x - mu), axis=-1, keepdims=True)
            return (x - mu) * jax.lax.rsqrt(var + EPS) * w + b
        e_cnt = router_prob.shape[2]
        b, t, d = x.shape
        n = t // e_cnt
        h = H
        scale = d ** (-0.5)
        qs, ks_, vs = ([], [], [])
        for e in range(e_cnt):
            xe = x[:, e * n:(e + 1) * n, :]
            xn = _layernorm(xe, norm_w, norm_b)
            m = d // 2 ** e
            xm = xn[..., :m]
            qs.append(jnp.einsum('bnm,dm->bnd', xm, q_w[:, :m]) + q_b)
            ks_.append(jnp.einsum('bnm,dm->bnd', xm, k_w[:, :m]) + k_b)
            vs.append(jnp.einsum('bnm,dm->bnd', xm, v_w[:, :m]) + v_b)
        q = jnp.concatenate(qs, axis=1)
        k = jnp.concatenate(ks_, axis=1)
        v = jnp.concatenate(vs, axis=1)
        dh = d // h
        q = q.reshape(b, t, h, dh).transpose(0, 2, 1, 3)
        k = k.reshape(b, t, h, dh).transpose(0, 2, 1, 3)
        v = v.reshape(b, t, h, dh).transpose(0, 2, 1, 3)
        attn = jnp.einsum('bhqd,bhkd->bhqk', q, k) * scale
        attn = jax.nn.softmax(attn, axis=-1)
        attn_out = jnp.einsum('bhqk,bhkd->bhqd', attn, v)
        attn_out = attn_out.transpose(0, 2, 1, 3).reshape(b, t, d)
        outs = []
        for e in range(e_cnt):
            sl = slice(e * n, (e + 1) * n)
            m = d // 2 ** e
            xm = attn_out[:, sl, :m]
            out = jnp.einsum('bnm,om->bno', xm, o_w[:m, :m]) + o_b[:m]
            pad = d - m
            if pad:
                out = jnp.pad(out, ((0, 0), (0, 0), (0, pad)))
            outs.append(out + x[:, sl, :])
        return jnp.concatenate(outs, axis=1)
    x = _layernorm(x + _L0_attn_ref(x, L0_attn_in_proj_w, L0_attn_conv_w, L0_attn_conv_b, L0_attn_x_proj_w, L0_attn_dt_proj_w, L0_attn_dt_proj_b, L0_attn_A_log, L0_attn_D, L0_attn_conv_wb, L0_attn_conv_bb, L0_attn_x_proj_wb, L0_attn_dt_proj_wb, L0_attn_dt_proj_bb, L0_attn_A_b_log, L0_attn_D_b, L0_attn_out_proj_w), axis=-1)
    x = _layernorm(x + _L0_xattn_ref(x, ctx_1024, ctx_1024, L0_xattn_Wq, L0_xattn_bq, L0_xattn_Wk, L0_xattn_bk, L0_xattn_Wv, L0_xattn_bv, L0_xattn_Wo, L0_xattn_bo), axis=-1)
    x = _layernorm(x + _L0_ffn_ref(x, L0_ffn_w_freq_real, L0_ffn_w_freq_imag, L0_ffn_bias), axis=-1)
    x = _layernorm(x + _L1_attn_ref(x, L1_attn_Wq, L1_attn_bq, L1_attn_Wk, L1_attn_bk, L1_attn_Wv, L1_attn_bv, L1_attn_Wo, L1_attn_bo), axis=-1)
    x = _layernorm(x + _L1_xattn_ref(x, ctx_1024, L1_xattn_Wq, L1_xattn_Wk, L1_xattn_Wv, L1_xattn_Wo, L1_xattn_bo), axis=-1)
    x = _layernorm(x + _L1_ffn_ref(x, L1_ffn_router_prob, L1_ffn_norm_w, L1_ffn_norm_b, L1_ffn_q_w, L1_ffn_q_b, L1_ffn_k_w, L1_ffn_k_b, L1_ffn_v_w, L1_ffn_v_b, L1_ffn_o_w, L1_ffn_o_b), axis=-1)
    return x

_drawn_inputs = setup_inputs


def setup_inputs(seed=0):
    import zlib

    import numpy as np

    out = dict(_drawn_inputs(seed))
    spreads = {'L0_attn_D': (1.0, 0.2),
     'L0_attn_D_b': (1.0, 0.2),
     'L0_xattn_bq': (0.0, 0.8),
     'L0_xattn_bk': (0.0, 2.0),
     'L0_xattn_bv': (0.0, 0.381),
     'L0_xattn_bo': (0.0, 0.1),
     'L1_attn_bq': (0.0, 0.8),
     'L1_attn_bk': (0.0, 2.0),
     'L1_attn_bv': (0.0, 0.402),
     'L1_attn_bo': (0.0, 0.1),
     'L1_ffn_norm_w': (1.0, 0.6),
     'L1_ffn_norm_b': (0.0, 0.8)}
    factors = {'L0_attn_dt_proj_wb': 3.65,
     'L0_xattn_Wq': 8.0,
     'L0_xattn_Wk': 8.0,
     'L0_ffn_bias': 6.911,
     'L1_attn_Wq': 8.0,
     'L1_attn_Wk': 8.0,
     'L1_attn_Wv': 8.0,
     'L1_attn_Wo': 2.745,
     'L1_xattn_bo': 5.962,
     'L1_ffn_q_w': 8.0,
     'L1_ffn_q_b': 23.026,
     'L1_ffn_k_w': 8.0,
     'L1_ffn_k_b': 64.0,
     'L1_ffn_v_b': 6.88,
     'L1_ffn_o_b': 3.009}
    for name, (base, spread) in spreads.items():
        noise = np.random.default_rng([zlib.crc32(name.encode()), seed]).standard_normal(out[name].shape)
        drawn = base * np.exp(spread * noise) if base else spread * noise
        out[name] = jnp.asarray(drawn.astype(out[name].dtype))
    for name, factor in factors.items():
        out[name] = (out[name] * factor).astype(out[name].dtype)
    return out
```

```python
from contextlib import ExitStack

import numpy as np

import concourse.bass as bass
from concourse import mybir

F32 = mybir.dt.float32
BF16 = mybir.dt.bfloat16
ALU = mybir.AluOpType
ACT = mybir.ActivationFunctionType
X_AXIS = mybir.AxisListType.X

D = 128
B, L = 8, 100
T = B * L
HT = T // 2
S = 1444
NST, DR, NC = 16, 8, 4
KT = 12
KC = [(0, 512), (512, 512), (1024, 420)]
KLAST = S - 128 * (KT - 1)
EPS = 1e-5
TWO_ONES = float(np.array([0x3F803F80], np.uint32).view(np.float32)[0])
CHUNK = 512
STAGE5_HIGH = 25000
SHIFTED = 96
TERMS = [(0, 0), (0, 1), (0, 2), (1, 0), (1, 1), (2, 0)]


def build(nc, a):
    with ExitStack() as ctx:
        def sb(name, shape, dt=F32):
            return ctx.enter_context(nc.sbuf_tensor(name, shape, dt))

        def sem(name):
            return ctx.enter_context(nc.semaphore(name))

        X_ = [sb("x_even", [128, T]), sb("x_odd", [128, T])]
        X = [x[:, :] for x in X_]
        Z = sb("residual", [128, T])[:, :]
        CEN = sb("centred", [128, T])[:, :]
        SQ = sb("square_then_rstd", [128, T])[:, :]
        CT = [sb("ctxT0", [128, S]), sb("ctxT1", [128, S])]

        wts = {}
        for name in W_RESIDENT:
            if name not in MAMBA_ONLY:
                wts[name] = sb("w_" + name, list(W_RESIDENT[name][1]))
        ARENA_W = 39600
        arena = sb("arena", [128, ARENA_W])
        PS = ctx.enter_context(nc.psum_tensor("ps", [128, 8, 512], F32))

        def carve(at):
            pos = [at]

            def f32(n):
                pos[0] += n
                assert pos[0] <= ARENA_W, pos[0]
                return arena[:, pos[0] - n:pos[0]]

            def b16(n):
                return f32((n + 1) // 2).bitcast(BF16)
            return f32, b16

        def two(v):
            return v.rearrange("p (j n) -> p j n", j=2)

        def half(v, j):
            return v[:, j * HT:(j + 1) * HT]

        ld = {g: sem("ld_" + g) for g in LOADS}
        z_ready, mean_ready, cent_ready, sq_ready = sem("z_ready"), sem("mean_ready"), sem("cent_ready"), sem("sq_ready")
        var_ready, ln_ready, rstd_ready, x_ready = sem("var_ready"), sem("ln_ready"), sem("rstd_ready"), sem("x_ready")
        op_done = sem("op_done")
        out_stored = sem("out_stored")
        ctx_ld = [sem("ctx_loaded0"), sem("ctx_loaded1")]

        def pe_ln(n, src, ready, count):
            for j in range(2):
                nc.tensor.wait_ge(ready, count + j + 1)
                nc.tensor.matmul(PS[:, j, 0:HT], wts["ones_d"][:, :], half(src, j), start=True, stop=True).then_inc(mean_ready, 1)
            for j in range(2):
                nc.tensor.wait_ge(sq_ready, 2 * (n - 1) + j + 1)
                nc.tensor.matmul(PS[:, 2 + j, 0:HT], wts["ones_d"][:, :], half(SQ, j), start=True, stop=True).then_inc(var_ready, 1)

        def dve_ln(n, src, dst, ready):
            for j in range(2):
                nc.vector.wait_ge(mean_ready, 2 * (n - 1) + j + 1)
                nc.vector.tensor_tensor(half(CEN, j), half(src, j), PS[:, j, 0:HT], ALU.subtract).then_inc(cent_ready, 1)
            for j in range(2):
                nc.vector.wait_ge(rstd_ready, 2 * (n - 1) + j + 1)
                nc.vector.tensor_tensor(half(dst, j), half(CEN, j), half(SQ, j), ALU.mult).then_inc(ready, 1)

        def act_ln(k):
            for j in range(2):
                nc.scalar.wait_ge(cent_ready, 2 * (k - 1) + j + 1)
                nc.scalar.activation(half(SQ, j), half(CEN, j), ACT.Square).then_inc(sq_ready, 1)
            for j in range(2):
                nc.scalar.wait_ge(var_ready, 2 * (k - 1) + j + 1)
                nc.scalar.activation(half(SQ, j), PS[:, 2 + j, 0:HT], ACT.Ln, bias=wts["eps"][:, 0:1]).then_inc(ln_ready, 1)
                nc.scalar.wait_ge(ln_ready, 2 * (k - 1) + j + 1)
                nc.scalar.activation(half(SQ, j), half(SQ, j), ACT.Exp, scale=-0.5).then_inc(rstd_ready, 1)

        def dve_residual(k, bias):
            for j in range(2):
                nc.vector.wait_ge(op_done, 2 * (k - 1) + j + 1)
                if bias is None:
                    ins = nc.vector.tensor_tensor(half(Z, j), PS[:, 4 + j, 0:HT], half(X[(k - 1) % 2], j), ALU.add)
                else:
                    ins = nc.vector.scalar_tensor_tensor(out=half(Z, j), in0=PS[:, 4 + j, 0:HT], scalar=bias,
                                                         in1=half(X[(k - 1) % 2], j), op0=ALU.add, op1=ALU.add)
                ins.then_inc(z_ready, 1)

        def pe_x(k):
            nc.tensor.wait_ge(x_ready, 2 * k)

        f32, b16 = carve(0)
        PADW = L + 2 * (NC - 1)
        XP = [f32(B * PADW).rearrange("p (b l) -> p b l", b=B) for _ in range(2)]
        SZ = [f32(T) for _ in range(2)]
        CACC = [[f32(T) for _ in range(2)] for _ in range(2)]
        U = [[f32(T) for _ in range(2)] for _ in range(2)]
        DT = [[f32(T) for _ in range(2)] for _ in range(2)]
        DTU = [[f32(T) for _ in range(2)] for _ in range(2)]
        DEC = [[f32(T) for _ in range(2)] for _ in range(2)]
        WIN = [[f32(T) for _ in range(2)] for _ in range(2)]
        BSB = [f32(T) for _ in range(2)]
        H = [f32(T) for _ in range(2)]
        G = [f32(T) for _ in range(2)]
        BC = [b16(T) for _ in range(2)]
        R1 = f32(T)
        DTR = [f32(T) for _ in range(2)]
        SEL = b16(2 * NST * 128).rearrange("p (n m) -> p n m", n=2 * NST)
        ANEG = f32(2 * 2 * NST)
        DIAG = [[f32(128) for _ in range(2)] for _ in range(2)]
        YZ = [f32(T) for _ in range(2)]
        for name in MAMBA_ONLY:
            shape = W_RESIDENT[name][1]
            v = f32(int(np.prod(shape[1:])))
            if len(shape) == 3:
                v = v.rearrange("p (i n) -> p i n", i=shape[1])
            if len(shape) == 4:
                v = v.rearrange("p (i j n) -> p i j n", i=shape[1], j=shape[2])
            wts[name] = v

        inproj, xp_ready, pads, sz_ready = sem("inproj"), sem("xp_ready"), sem("pads_zero"), sem("sz_ready")
        tap0, conv_dve, u_ready = sem("tap0"), sem("conv_dve"), sem("u_ready")
        xproj, bc_hi, bc_r1, bc_mid, bc_ready, dtr_ready = sem("xproj"), sem("bc_hi"), sem("bc_r1"), sem("bc_mid"), sem("bc_ready"), sem("dtr_ready")
        dtproj, sp_act, relu_ready, dt_ready, dtu_ready = sem("dtproj"), sem("sp_act"), sem("relu_ready"), sem("dt_ready"), sem("dtu_ready")
        sel_ready, aexp, aneg, diag_ready = sem("sel_ready"), sem("aexp"), sem("aneg"), sem("diag_ready")
        dec_zeroed, b_copied = sem("dec_zeroed"), sem("b_copied")
        dec_ready, win_ready, scanned, g_ready = sem("dec_ready"), sem("win_ready"), sem("scanned"), sem("g_ready")
        b_ready, c_ready, y_added, yz_ready = sem("b_bcast"), sem("c_bcast"), sem("y_added"), sem("yz_ready")

        def pe_mamba():
            nc.tensor.wait_ge(ld["mamba"], 16 * LOADS["mamba"])
            for e in range(4):
                for j in range(2):
                    m = nc.tensor.matmul(PS[:, 2 * e + j, 0:HT], wts["w_in"][:, e * 128:(e + 1) * 128], half(X[0], j), start=True, stop=True)
                m.then_inc(inproj, 1)
            for d in range(2):
                if d == 0:
                    nc.tensor.wait_ge(xp_ready, 2)
                nc.tensor.wait_ge(u_ready, 2 * d + 2)
                for j in range(2):
                    for h in range(2):
                        m = nc.tensor.matmul(PS[:, 2 * d + j, 0:HT], wts["w_xp"][:, d, h, :], half(U[d][h], j), start=(h == 0), stop=(h == 1))
                m.then_inc(xproj, 1)
            nc.tensor.wait_ge(sz_ready, 2)
            for d in range(2):
                nc.tensor.wait_ge(dtr_ready, d + 1)
                for h in range(2):
                    if d == 1:
                        nc.tensor.wait_ge(relu_ready, h + 1)
                    for j in range(2):
                        m = nc.tensor.matmul(PS[:, 4 + 2 * h + j, 0:HT], wts["w_dt"][32:32 + DR, d, h * 128:(h + 1) * 128],
                                             DTR[d][32:32 + DR, j * HT:(j + 1) * HT], start=True, stop=True)
                    m.then_inc(dtproj, 1)
            nc.tensor.wait_ge(diag_ready, 4)
            for h in range(2):
                nc.tensor.wait_ge(relu_ready, 2 + h + 1)
                for d in range(2):
                    for j in range(2):
                        m = nc.tensor.matmul(PS[:, 4 + 2 * h + j, 0:HT], DIAG[d][h], half(U[d][h], j), start=(d == 0), stop=False, skip_group_check=True)
                m.then_inc(y_added, 1)
            nc.tensor.wait_ge(sel_ready, 1)

            def bcast(bank, which, d, done):
                for j in range(2):
                    m = nc.tensor.matmul(PS[:, bank + j, 0:HT], which, BC[d][:, j * HT:(j + 1) * HT], start=True, stop=True)
                m.then_inc(done, 1)

            def sel(n, c):
                return SEL_FLAT[:, bass.ds(n * 128 + c * NST * 128, 128)] if not isinstance(n, int) else SEL[:, n + c * NST, :]

            def add_y(m_, h, last):
                nc.tensor.wait_ge(g_ready, 2 * m_ + h + 3)
                for j in range(2):
                    m = nc.tensor.matmul(PS[:, 4 + 2 * h + j, 0:HT], wts["ident"][:, :], half(G[h], j), start=False, stop=last, skip_group_check=True)
                m.then_inc(y_added, 1)

            nc.tensor.wait_ge(bc_ready, 2)
            bcast(0, sel(0, 0), 0, b_ready)
            bcast(2, sel(0, 1), 0, c_ready)
            nc.tensor.wait_ge(b_copied, 1)
            bcast(0, sel(1, 0), 0, b_ready)

            def state(n, d, ahead, after):
                m_ = n + d * NST
                if ahead:
                    nc.tensor.wait_ge(b_copied, m_ + 2)
                    bcast(0, sel(ahead[0], 0), ahead[1], b_ready)
                last = after is None
                add_y(m_, 0, last)
                if after:
                    nc.tensor.wait_ge(g_ready, 2 * m_ + 4)
                    bcast(2, sel(after[0], 1), after[1], c_ready)
                add_y(m_, 1, last)
            for d in range(2):
                with nc.tensor.Fori(0, NST - 2) as n:
                    state(n, d, (n + 2, d), (n + 1, d))
                state(NST - 2, d, None if d else (0, 1), (NST - 1, d))
                state(NST - 1, d, None if d else (1, 1), None if d else (0, 1))
            nc.tensor.wait_ge(yz_ready, 2)
            for j in range(2):
                for h in range(2):
                    m = nc.tensor.matmul(PS[:, 4 + j, 0:HT], wts["w_out"][:, h, :], half(YZ[h], j), start=(h == 0), stop=(h == 1))
                m.then_inc(op_done, 1)

        SEL_FLAT = SEL.rearrange("p n m -> p (n m)")

        def interior(h):
            return XP[h][:, :, NC - 1:NC - 1 + L]

        def tap(d, h, k):
            at = k if d == 0 else 2 * (NC - 1) - k
            return XP[h][:, :, at:at + L]

        def by_batch(v):
            return v.rearrange("p (b l) -> p b l", b=B)

        def act_mamba():
            nc.scalar.wait_ge(ld["mamba"], 16 * LOADS["mamba"])
            for h in range(2):
                nc.scalar.wait_ge(inproj, h + 1)
                nc.scalar.wait_ge(pads, 2)
                for j in range(2):
                    i = nc.scalar.activation(interior(h)[:, 4 * j:4 * j + 4, :], PS[:, 2 * h + j, 0:HT].rearrange("p (b l) -> p b l", b=4), ACT.Copy)
                i.then_inc(xp_ready, 1)
            for h in range(2):
                nc.scalar.wait_ge(inproj, 2 + h + 1)
                nc.scalar.activation(two(SZ[h]), PS[:, 4 + 2 * h:6 + 2 * h, 0:HT], ACT.Silu).then_inc(sz_ready, 1)
            nc.scalar.wait_ge(xp_ready, 2)
            for d in range(2):
                for h in range(2):
                    nc.scalar.activation(by_batch(CACC[d][h]), tap(d, h, 0), ACT.Identity,
                                         bias=wts["conv_b"][:, 2 * d + h:2 * d + h + 1], scale=wts["conv_w"][:, 4 * (2 * d + h):4 * (2 * d + h) + 1]).then_inc(tap0, 1)
            nc.scalar.activation(SEL, wts["sel32"][:, :].unsqueeze(2).broadcast_to([128, 2 * NST, 128]), ACT.Copy).then_inc(sel_ready, 1)
            for d in range(2):
                for h in range(2):
                    nc.scalar.wait_ge(conv_dve, (2 * d + h + 1) * (NC - 1))
                    nc.scalar.activation(U[d][h], CACC[d][h], ACT.Silu).then_inc(u_ready, 1)
            nc.scalar.preload_act_table_set("natural_log_exp_and_others")
            nc.scalar.activation(ANEG, wts["a_log"][:, :], ACT.Exp).then_inc(aexp, 1)
            for d in range(2):
                nc.scalar.wait_ge(xproj, d + 1)
                nc.scalar.activation(two(BC[d]), PS[:, 2 * d:2 * d + 2, 0:HT], ACT.Copy).then_inc(bc_hi, 1)
                nc.scalar.activation(two(DTR[d])[32:32 + DR], PS[32:32 + DR, 2 * d:2 * d + 2, 0:HT], ACT.Copy).then_inc(dtr_ready, 1)
            for d in range(2):
                for h in range(2):
                    n = 2 * d + h
                    v = CACC[d][h]
                    nc.scalar.wait_ge(dtproj, n + 1)
                    nc.scalar.activation(two(v), PS[:, 4 + 2 * h:6 + 2 * h, 0:HT], ACT.Abs, bias=wts["dt_b"][:, n:n + 1]).then_inc(sp_act, 1)
                    nc.scalar.wait_ge(sp_act, 3 * n + 1)
                    nc.scalar.activation(v, v, ACT.Exp, scale=-1.0).then_inc(sp_act, 1)
                    nc.scalar.wait_ge(sp_act, 3 * n + 2)
                    nc.scalar.activation(v, v, ACT.Ln, bias=wts["one"][:, 0:1]).then_inc(sp_act, 1)
            nc.scalar.wait_ge(aneg, 1)

            def copy_b(m_, k):
                nc.scalar.wait_ge(b_ready, m_ + 1)
                if not isinstance(m_, int) or m_ > 1:
                    nc.scalar.wait_ge(win_ready, 2 * m_ - 2)
                nc.scalar.activation(two(BSB[k]), PS[:, 0:2, 0:HT], ACT.Copy).then_inc(b_copied, 1)

            def decay(n, d, k, copy):
                m_ = n + d * NST
                cols = (1, L) if d == 0 else (0, L - 1)
                for h in range(2):
                    nc.scalar.wait_ge(scanned, 2 * m_ + h + 3)
                    nc.scalar.activation(by_batch(DEC[d][h])[:, :, cols[0]:cols[1]], by_batch(DT[d][h])[:, :, cols[0]:cols[1]], ACT.Exp,
                                         scale=ANEG[:, bass.ds(n + (2 * d + h) * NST, 1)]).then_inc(dec_ready, 1)
                if copy:
                    copy_b(m_ + 2, k)
            for k in range(2):
                copy_b(k, k)
            nc.scalar.wait_ge(dec_zeroed, 4)
            nc.scalar.wait_ge(dt_ready, 4)
            for d in range(2):
                with nc.scalar.Fori(0, NST // 2 - d) as pair:
                    for k in range(2):
                        decay(pair * 2 + k, d, k, True)
            for k in range(2):
                decay(NST - 2 + k, 1, k, False)

        def pool_mamba():
            nc.gpsimd.wait_ge(dtu_ready, 4)
            for d in range(2):
                with nc.gpsimd.Fori(0, NST // 2) as pair:
                    for k in range(2):
                        m_ = pair * 2 + (k + d * NST)
                        nc.gpsimd.wait_ge(b_copied, m_ + 1)
                        for h in range(2):
                            nc.gpsimd.wait_ge(scanned, 2 * m_ + h + 1)
                            nc.gpsimd.tensor_tensor(WIN[k][h], DTU[d][h], BSB[k], ALU.mult).then_inc(win_ready, 1)

        def dve_mamba():
            for h in range(2):
                nc.vector.memset(XP[h], 0.0).then_inc(pads, 1)
            for d in range(2):
                for h in range(2):
                    nc.vector.memset(by_batch(DEC[d][h])[:, :, (0 if d == 0 else L - 1):(1 if d == 0 else L)], 0.0).then_inc(dec_zeroed, 1)
            nc.vector.wait_ge(ld["mamba"], 16 * LOADS["mamba"])
            for d in range(2):
                for h in range(2):
                    nc.vector.tensor_scalar(DIAG[d][h], wts["ident"][:, :], wts["d_skip"][:, 2 * d + h:2 * d + h + 1], None, ALU.mult).then_inc(diag_ready, 1)
            for d in range(2):
                for h in range(2):
                    n = 2 * d + h
                    nc.vector.wait_ge(tap0, n + 1)
                    for k in range(1, NC):
                        if k > 1:
                            nc.vector.wait_ge(conv_dve, (NC - 1) * n + k - 1)
                        c = by_batch(CACC[d][h])
                        nc.vector.scalar_tensor_tensor(out=c, in0=tap(d, h, k), scalar=wts["conv_w"][:, 4 * n + k:4 * n + k + 1],
                                                       in1=c, op0=ALU.mult, op1=ALU.add).then_inc(conv_dve, 1)
            nc.vector.wait_ge(aexp, 1)
            nc.vector.tensor_scalar(ANEG, ANEG, -1.0, None, ALU.mult).then_inc(aneg, 1)
            for d in range(2):
                nc.vector.wait_ge(bc_hi, d + 1)
                nc.vector.wait_ge(dtr_ready, d + 1)
                if d == 1:
                    nc.vector.wait_ge(bc_ready, 1)
                nc.vector.tensor_tensor(two(R1)[64:128], PS[64:128, 2 * d:2 * d + 2, 0:HT], two(BC[d])[64:128], ALU.subtract).then_inc(bc_r1, 1)
                nc.vector.wait_ge(bc_r1, d + 1)
                nc.vector.tensor_copy(BC[d][64:128], R1[64:128]).then_inc(bc_mid, 1)
                nc.vector.wait_ge(bc_mid, d + 1)
                nc.vector.tensor_tensor(BC[d][96:128], R1[96:128], BC[d][96:128], ALU.subtract).then_inc(bc_ready, 1)
            for d in range(2):
                for h in range(2):
                    n = 2 * d + h
                    nc.vector.wait_ge(sp_act, 3 * n + 1)
                    nc.vector.tensor_scalar(two(DT[d][h]), PS[:, 4 + 2 * h:6 + 2 * h, 0:HT], wts["dt_b"][:, n:n + 1], 0.0, ALU.add, ALU.max).then_inc(relu_ready, 1)
                    nc.vector.wait_ge(sp_act, 3 * n + 3)
                    nc.vector.wait_ge(relu_ready, n + 1)
                    nc.vector.tensor_tensor(DT[d][h], DT[d][h], CACC[d][h], ALU.add).then_inc(dt_ready, 1)
                    nc.vector.wait_ge(dt_ready, n + 1)
                    nc.vector.tensor_tensor(DTU[d][h], DT[d][h], U[d][h], ALU.mult).then_inc(dtu_ready, 1)
            for d in range(2):
                with nc.vector.Fori(0, NST // 2) as pair:
                    for k in range(2):
                        m_ = pair * 2 + (k + d * NST)
                        for h in range(2):
                            nc.vector.wait_ge(dec_ready, 2 * m_ + h + 1)
                            nc.vector.wait_ge(win_ready, 2 * m_ + h + 1)
                            nc.vector.wait_ge(g_ready, 2 * m_ + h + 1)
                            if d == 0:
                                i = nc.vector.tensor_tensor_scan(H[h], DEC[d][h], WIN[k][h], 0.0, ALU.mult, ALU.add)
                            else:
                                i = nc.vector.tensor_tensor_scan(H[h][:, ::-1], DEC[d][h][:, ::-1], WIN[k][h][:, ::-1], 0.0, ALU.mult, ALU.add)
                            i.then_inc(scanned, 1)
                        nc.vector.wait_ge(c_ready, m_ + 1)
                        for h in range(2):
                            nc.vector.wait_ge(y_added, 2 * m_ + h + 1)
                            nc.vector.wait_ge(scanned, 2 * m_ + h + 5)
                            nc.vector.tensor_tensor(two(G[h]), two(H[h]), PS[:, 2:4, 0:HT], ALU.mult).then_inc(g_ready, 1)
            nc.vector.wait_ge(y_added, 2 + 4 * NST)
            nc.vector.wait_ge(sz_ready, 2)
            for h in range(2):
                nc.vector.tensor_tensor(two(YZ[h]), two(SZ[h]), PS[:, 4 + 2 * h:6 + 2 * h, 0:HT], ALU.mult).then_inc(yz_ready, 1)
            dve_residual(1, None)

        f32, b16 = carve(0)
        KST = [b16(8 * S).rearrange("p (g n) -> p g n", g=8) for _ in range(2)]
        VA = [f32(KT * 256).rearrange("p (t g n) -> p t g n", t=KT, g=8) for _ in range(2)]
        PT = [f32(16 * L) for _ in range(2)]
        K32, KR = f32(S), f32(S)
        KH = [b16(S) for _ in range(2)]
        KP = [None, b16(S), b16(S)]
        QM = [b16(16 * L) for _ in range(2)]
        QS = [b16(16 * L) for _ in range(2)]
        ONE_ROW = b16(S)
        Q32, QR = f32(T), f32(T)
        QP = [b16(T) for _ in range(3)]
        ACC0 = f32(4 * T).rearrange("p (i n) -> p i n", i=4)
        AS, RD = f32(HT), f32(HT)
        TILES = -(-16 * L // 128)
        TLAST = 16 * L - 128 * (TILES - 1)
        MX, MXC = f32(TILES * 3).rearrange("p (t c) -> p t c", c=3), f32(TILES)
        MB = b16(128)
        DH0 = 8.0 ** -0.5
        QDMA = 16 * 2 * len(TERMS)
        UNITS = 4 * KT
        MAXU = 3 * TILES
        JOBS = {2: dict(V0=(0, 0), V1=(1, 0), V2=(0, 1), K0=(1, 1), K1=(0, 2), K2=(1, 2), M=(0, 3), D=(1, 3)),
                1: dict(V0=(0, 0), V1=(1, 0), V2=(0, 1), M=(1, 1), D=(0, 2)),
                0: dict(D=(1, -2))}
        PRO = 5
        V_AT, K_AT, M_AT, MAX_KT = (0, 1, 2), (3, 4, 5), 10, 10

        q_mm, q_cut, q_hi, qp_st, qs_zero = sem("q_mm"), sem("q_cut"), sem("q_hi"), sem("q_parts_stored"), sem("stack_zero")
        qs_ld, mrow_ld = sem("qs_loaded"), sem("mrow_loaded")
        qm_ready, run_max, ones_ld = sem("qm_ready"), sem("run_max"), sem("ones_loaded")
        kp_st = [sem(f"kp_stored{c}") for c in range(3)]
        kst_ld = [[sem(f"kst_loaded{u}_{c}") for c in range(3)] for u in range(2)]
        k_high, one_row = sem("k_high"), sem("one_row")
        k_mm, k_cut, v_mm, va_init = sem("k_mm"), sem("k_cut"), sem("v_mm"), sem("va_init")
        job_free = [sem("job_free0"), sem("job_free1")]
        unit_done, exp_done, pt_free, acc_free = sem("unit_done"), sem("exp_done"), sem("pt_free"), sem("acc_free")
        mx_mm, mx_read, mxc_ready, mt_mm = sem("mx_mm"), sem("mx_read"), sem("mxc_ready"), sem("mt_mm")
        den_mm, rd_ready, accn_ready = sem("den_mm"), sem("rd_ready"), sem("accn_ready")

        def job(name, b, more):
            bank, turn = JOBS[more][name]
            return bank, b * 4 + (PRO + 1 + turn)

        def turn(n):
            return n % 2, n // 2 + 1

        def rows(kt):
            return 128 if kt < KT - 1 else KLAST

        def max_units(kt, g):
            return 1 if 4 * kt + g < MAXU and kt < MAX_KT else 0

        def steps(engine, body):
            with engine.Fori(0, B // 2 - 1) as pair:
                for u in range(2):
                    body(pair * 2 + u, u, 2)
            body(B - 2, 0, 1)
            body(B - 1, 1, 0)

        def waits(engine, *pairs):
            for _, n in pairs:
                if not isinstance(n, int):
                    engine.lower_val(n)
            for semaphore, n in pairs:
                engine.wait_ge(semaphore, n)

        def own_register(engine, value):
            if isinstance(value, int):
                return value
            r = engine.alloc_register(f"own_{nc.next_id()}")
            engine.reg_mov(r, value)
            return engine.snap(r)

        def loads_until(b, u, n):
            return (b - u) * (n // 2) + n

        def pe_k(c, u, bank, free):
            at, n = KC[c]
            nc.tensor.wait_ge(job_free[bank], free)
            nc.tensor.matmul(PS[:, 6 + bank, 0:n], wts["l0_wk"][:, :], CT[u][:, at:at + n], start=True, stop=True).then_inc(k_mm, 1)

        def pe_v(c, u, bank, free):
            nc.tensor.wait_ge(job_free[bank], free)
            for i in range(4):
                n = rows(4 * c + i)
                at = (4 * c + i) * 128
                m = nc.tensor.matmul(PS[0:n, 6 + bank, i * 128:i * 128 + 128], CT[u][:, at:at + n], wts["l0_wv"][:, :], start=True, stop=True)
            m.then_inc(v_mm, 1)

        def pe_max(unit, u, b):
            t, c = unit // 3, unit % 3
            at, n = KC[c]
            m = 128 if t < TILES - 1 else TLAST
            if unit < 3:
                nc.tensor.wait_ge(k_high, b * 3 + c + 1)
            if unit == 0:
                nc.tensor.wait_ge(qm_ready, b + 1)
            nc.tensor.wait_ge(mx_read, b * MAXU + unit + 1)
            nc.tensor.matmul(PS[0:m, 3 + unit % 2, 0:n], QM[u][:, t * 128:t * 128 + m], KH[u][:, at:at + n], start=True, stop=True).then_inc(mx_mm, 1)

        def pe_mt(b, bank, free):
            nc.tensor.wait_ge(mxc_ready, b + 1)
            nc.tensor.wait_ge(job_free[bank], free)
            nc.tensor.transpose(PS[0:TILES, 6 + bank, 0:128], MXC, wts["ident"][:, :]).then_inc(mt_mm, 1)

        def pe_xattn0():
            pe_x(1)
            nc.tensor.wait_ge(ld["l0x"], 16 * LOADS["l0x"])
            for j in range(2):
                nc.tensor.matmul(PS[:, 4 + j, 0:HT], wts["l0_wq"][:, :], half(X[1], j), start=True, stop=True).then_inc(q_mm, 1)
            nc.tensor.wait_ge(ctx_ld[0], 16)
            for c in range(3):
                pe_k(c, 0, *turn(c))
            nc.tensor.wait_ge(q_cut, 2)
            for unit in range(MAXU):
                pe_max(unit, 0, 0)
            pe_mt(0, *turn(3))
            for c in range(3):
                pe_v(c, 0, *turn(4 + c))
            nc.tensor.wait_ge(ctx_ld[1], 16)
            for c in range(3):
                pe_k(c, 1, *turn(7 + c))
            nc.tensor.wait_ge(ones_ld, 32)

            def pv(b, u, kt, r):
                if kt == 0 and r == 0:
                    nc.tensor.wait_ge(acc_free, b + 1)
                nc.tensor.wait_ge(exp_done, b * UNITS + (4 * kt + 2 * r + 2 + 3))
                for j in range(4):
                    p = 4 * r + j
                    m = nc.tensor.matmul(PS[32 * j:32 * j + 32, 5, 2 * L * r:2 * L * (r + 1)], VA[u][:, kt, p, :], PT[kt % 2][:, p * 2 * L:(p + 1) * 2 * L],
                                         start=(kt == 0 and r == 0), stop=(kt == KT - 1), skip_group_check=True)
                if r == 1:
                    m.then_inc(pt_free, 1)

            def body(b, u, more):
                nxt = 0
                following = own_register(nc.tensor, b + 1)
                nc.tensor.wait_ge(qs_ld, b * QDMA + QDMA)
                nc.tensor.wait_ge(mrow_ld, b * 32 + 32)
                for kt in range(KT):
                    n = rows(kt)
                    if kt % 4 == 0:
                        nc.tensor.wait_ge(kst_ld[u][kt // 4], loads_until(b, u, 96))
                    for g in range(4):
                        unit = 4 * kt + g
                        nc.tensor.wait_ge(exp_done, b * UNITS + unit + 1)
                        for i in range(2):
                            p = 2 * g + i
                            m = nc.tensor.matmul(PS[0:n, unit % 3, i * 2 * L:(i + 1) * 2 * L], KST[u][0:97, p, kt * 128:kt * 128 + n], QS[u][0:97, p * 2 * L:(p + 1) * 2 * L],
                                                 start=(i == 0), stop=True, skip_group_check=True)
                        m.then_inc(unit_done, 1)
                        if more:
                            for _ in range(max_units(kt, g)):
                                pe_max(nxt, 1 - u, following)
                                nxt += 1
                        if kt > 0 and g % 2 == 1:
                            pv(b, u, kt - 1, g // 2)
                    if more and kt in V_AT:
                        pe_v(V_AT.index(kt), 1 - u, *job(f"V{V_AT.index(kt)}", b, more))
                    if more == 2 and kt in K_AT:
                        if kt == K_AT[0]:
                            nc.tensor.wait_ge(ctx_ld[u], ctx_count(b, u) + 16)
                        pe_k(K_AT.index(kt), u, *job(f"K{K_AT.index(kt)}", b, more))
                    if more and kt == M_AT:
                        pe_mt(b + 1, *job("M", b, more))
                for r in range(2):
                    pv(b, u, KT - 1, r)
                bank, free = job("D", b, more)
                nc.tensor.wait_ge(acc_free, b + 2)
                nc.tensor.wait_ge(job_free[bank], free)
                nc.tensor.matmul(PS[:, 6 + bank, 0:HT], wts["seld"][:, :], AS, start=True, stop=True).then_inc(den_mm, 1)
            steps(nc.tensor, body)
            pe_out(ACC0, wts["l0_wo"], accn_ready, B + 1, 4)

        def ctx_count(b, u):
            return loads_until(b, u, 16)

        def pe_out(acc, w, ready, count, n):
            nc.tensor.wait_ge(ready, count)
            for j in range(2):
                for i in range(n):
                    m = nc.tensor.matmul(PS[:, 4 + j, 0:HT], w[:, i, :], acc[:, i, j * HT:(j + 1) * HT], start=(i == 0), stop=(i == n - 1))
                m.then_inc(op_done, 1)

        def act_kev(c, kb, u, bank, free):
            at, n = KC[c]
            nc.scalar.wait_ge(k_mm, kb * 3 + c + 1)
            if not isinstance(kb, int) or kb > 0:
                nc.scalar.wait_ge(kp_st[c], kb * 48)
                nc.scalar.wait_ge(k_cut, kb * 9 - 9 + 3 * c + 3)
            nc.scalar.activation(KH[u][:, at:at + n], PS[:, 6 + bank, 0:n], ACT.Identity, bias=wts["l0_bk"][:, 0:1]).then_inc(k_high, 1)
            nc.scalar.activation(K32[:, at:at + n], PS[:, 6 + bank, 0:n], ACT.Identity, bias=wts["l0_bk"][:, 0:1]).then_inc(job_free[bank], 1)

        def act_xattn0():
            for j in range(2):
                nc.scalar.wait_ge(q_cut, j + 1)
                nc.scalar.activation(half(QP[0], j), half(Q32, j), ACT.Copy).then_inc(q_hi, 1)
            for c in range(3):
                act_kev(c, 0, 0, *turn(c))
            nc.scalar.wait_ge(mt_mm, 1)
            nc.scalar.activation(MB[0:TILES, :], PS[0:TILES, 7, 0:128], ACT.Copy).then_inc(job_free[1], 1)
            for c in range(3):
                act_kev(c, 1, 1, *turn(7 + c))

            def body(b, u, more):
                for kt in range(KT):
                    n = rows(kt)
                    nc.scalar.wait_ge(pt_free, b * KT + kt + 1)
                    for g in range(4):
                        unit = 4 * kt + g
                        nc.scalar.wait_ge(unit_done, b * UNITS + unit + 1)
                        nc.scalar.activation(PT[kt % 2][0:n, g * HT:(g + 1) * HT], PS[0:n, unit % 3, 0:HT], ACT.Exp).then_inc(exp_done, 1)
                    if more == 2 and kt in K_AT:
                        act_kev(K_AT.index(kt), b + 2, u, *job(f"K{K_AT.index(kt)}", b, more))
                    if more and kt == M_AT:
                        bank, free = job("M", b, more)
                        nc.scalar.wait_ge(mt_mm, b + 2)
                        nc.scalar.wait_ge(mrow_ld, b * 32 + 32)
                        nc.scalar.activation(MB[0:TILES, :], PS[0:TILES, 6 + bank, 0:128], ACT.Copy).then_inc(job_free[bank], 1)
                bank, free = job("D", b, more)
                nc.scalar.wait_ge(den_mm, b + 1)
                nc.scalar.wait_ge(accn_ready, b + 1)
                nc.scalar.activation(RD, PS[:, 6 + bank, 0:HT], ACT.Ln).then_inc(job_free[bank], 1)
                nc.scalar.wait_ge(job_free[bank], free + 1)
                nc.scalar.activation(RD, RD, ACT.Exp, scale=-1.0).then_inc(rd_ready, 1)
            steps(nc.scalar, body)

        def pool_kcut(c, kb, u, bank, free):
            at, n = KC[c]
            sl = slice(at, at + n)
            nc.gpsimd.wait_ge(k_high, kb * 3 + c + 1)
            nc.gpsimd.wait_ge(job_free[bank], free + 1)
            if not isinstance(kb, int) or kb > 0:
                nc.gpsimd.wait_ge(kp_st[c], kb * 48)
                nc.gpsimd.wait_ge(k_cut, kb * 9 - 9 + 3 * c + 3)
            nc.gpsimd.tensor_tensor(KR[:, sl], K32[:, sl], KH[u][:, sl], ALU.subtract).then_inc(k_cut, 1)
            nc.gpsimd.tensor_tensor(KP[1][:, sl], K32[:, sl], KH[u][:, sl], ALU.subtract).then_inc(k_cut, 1)
            nc.gpsimd.wait_ge(k_cut, kb * 9 + 3 * c + 2)
            nc.gpsimd.tensor_tensor(KP[2][:, sl], KR[:, sl], KP[1][:, sl], ALU.subtract).then_inc(k_cut, 1)

        def pool_xattn0():
            def block_queries(b, u):
                nc.gpsimd.tensor_tensor(QM[u].rearrange("p (h n) -> p h n", h=16), QP[0][:, bass.ds(b * L, L)].unsqueeze(1).broadcast_to([128, 16, L]),
                                        wts["of_head"][:, :].unsqueeze(2).broadcast_to([128, 16, L]), ALU.mult).then_inc(qm_ready, 1)
            nc.gpsimd.wait_ge(q_hi, 2)
            block_queries(0, 0)
            for c in range(3):
                pool_kcut(c, 0, 0, *turn(c))
            block_queries(1, 1)
            for c in range(3):
                pool_kcut(c, 1, 1, *turn(7 + c))

            def body(b, u, more):
                if more == 2:
                    nc.gpsimd.wait_ge(mx_mm, b * MAXU + MAXU)
                    block_queries(b + 2, u)
                    for c in range(3):
                        pool_kcut(c, b + 2, u, *job(f"K{c}", b, more))
                nc.gpsimd.wait_ge(rd_ready, b + 1)
                nc.gpsimd.tensor_tensor(ACC0[:, :, bass.ds(b * L, L)], AS.rearrange("p (i n) -> p i n", i=4), RD.rearrange("p (i n) -> p i n", i=4), ALU.mult).then_inc(accn_ready, 1)
            steps(nc.gpsimd, body)

        def dve_vev(c, u, b, bank):
            nc.vector.wait_ge(v_mm, b * 3 + c + 1)
            bias = wts["l0_bv"][:, :].rearrange("p (g n) -> p g n", g=8)
            last = c == 2
            for i in range(4):
                n = rows(4 * c + i)
                m = nc.vector.tensor_tensor(VA[u][0:n, 4 * c + i, :, 0:16], PS[0:n, 6 + bank, i * 128:i * 128 + 128].rearrange("p (g n) -> p g n", g=8), bias[0:n], ALU.add)
            m.then_inc(job_free[bank], 1)

        def dve_max(unit, b):
            t, c = unit // 3, unit % 3
            m = 128 if t < TILES - 1 else TLAST
            nc.vector.wait_ge(mx_mm, b * MAXU + unit + 1)
            nc.vector.tensor_reduce(MX[0:m, t, c:c + 1], PS[0:m, 3 + unit % 2, 0:KC[c][1]], X_AXIS, ALU.max).then_inc(mx_read, 1)
            if unit == MAXU - 1:
                nc.vector.wait_ge(mx_read, b * MAXU + MAXU + 2)
                if not isinstance(b, int) or b > 0:
                    nc.vector.wait_ge(mt_mm, b)
                nc.vector.tensor_reduce(MXC, MX, X_AXIS, ALU.max, negate=True).then_inc(mxc_ready, 1)

        def dve_xattn0():
            nc.vector.wait_ge(ld["l0x"], 16 * LOADS["l0x"])
            for j in range(2):
                nc.vector.wait_ge(q_mm, j + 1)
                nc.vector.tensor_scalar(half(Q32, j), PS[:, 4 + j, 0:HT], wts["l0_bq"][:, 0:1], DH0, ALU.add, ALU.mult).then_inc(q_cut, 1)
            nc.vector.wait_ge(q_hi, 2)
            nc.vector.wait_ge(q_cut, 2)
            nc.vector.tensor_tensor(QR, Q32, QP[0], ALU.subtract).then_inc(q_cut, 1)
            nc.vector.wait_ge(q_cut, 3)
            nc.vector.tensor_copy(QP[1], QR).then_inc(q_cut, 1)
            nc.vector.wait_ge(q_cut, 4)
            nc.vector.tensor_tensor(QP[2], QR, QP[1], ALU.subtract).then_inc(q_cut, 1)
            nc.vector.memset(ONE_ROW[0:1, :].bitcast(F32), TWO_ONES).then_inc(one_row, 1)
            nc.vector.memset(MX, 0.0).then_inc(va_init, 1)
            nc.vector.memset(QS[0][0:96, :].bitcast(F32), 0.0).then_inc(qs_zero, 1)
            nc.vector.memset(VA[0], 0.0).then_inc(va_init, 1)
            nc.vector.memset(QS[1][0:96, :].bitcast(F32), 0.0).then_inc(qs_zero, 1)
            nc.vector.wait_ge(va_init, 2)
            for unit in range(MAXU):
                dve_max(unit, 0)
            nc.vector.memset(VA[1], 0.0).then_inc(va_init, 1)
            nc.vector.wait_ge(va_init, 3)
            for u in range(2):
                nc.vector.memset(VA[u][:, 0:KT - 1, :, 16:17], 1.0).then_inc(va_init, 1)
                nc.vector.memset(VA[u][0:KLAST, KT - 1, :, 16:17], 1.0).then_inc(va_init, 1)
            nc.vector.wait_ge(va_init, 7)
            for c in range(3):
                dve_vev(c, 0, 0, turn(4 + c)[0])

            def body(b, u, more):
                nxt = 0
                for kt in range(KT):
                    if more:
                        for g in range(4):
                            for _ in range(max_units(kt, g)):
                                dve_max(nxt, b + 1)
                                nxt += 1
                        if kt in V_AT:
                            dve_vev(V_AT.index(kt), 1 - u, b + 1, job(f"V{V_AT.index(kt)}", b, more)[0])
                nc.vector.wait_ge(pt_free, b * KT + (KT + 2))
                nc.vector.wait_ge(accn_ready, b + 1)
                nc.vector.tensor_copy(AS, PS[:, 5, 0:HT]).then_inc(acc_free, 1)
            steps(nc.vector, body)
            dve_residual(2, wts["l0_bo"][:, 0:1])

        def sp_queries(dst, done, b):
            for t, (pq, _) in enumerate(TERMS):
                for s in range(2):
                    r0 = 16 * t + 8 * s
                    nc.sync.dma_start(dst[r0:r0 + 8, :].rearrange("d (p s q) -> d p s q", p=8, s=2)[:, :, s, :],
                                      a["q_parts"][pq].rearrange("(p s d) n -> s d p n", s=2, d=8)[s][:, :, bass.ds(b * L, L)]).then_inc(done, 16)

        def sp_kstore(c, kb, u, after=()):
            at, n = KC[c]
            again = [(kst_ld[u][c], loads_until(kb, u, 96) - 96)] if not isinstance(kb, int) or kb > 1 else []
            waits(nc.sync, *after, (k_cut, kb * 9 + 3 * c + 3), *again)
            for i in range(3):
                nc.sync.dma_start(a["k_parts"][u, i, :, at:at + n], (KP[i] if i else KH[u])[:, at:at + n]).then_inc(kp_st[c], 16)

        def sp_kload(c, kb, u):
            at, n = KC[c]
            nc.sync.wait_ge(kp_st[c], kb * 48 + 48)
            for t, (_, pk) in enumerate(TERMS):
                nc.sync.dma_start(KST[u][16 * t:16 * t + 16, :, at:at + n],
                                  a["k_parts"][u, pk, :, at:at + n].rearrange("(p i) n -> i p n", i=16)).then_inc(kst_ld[u][c], 16)

        def sp_mrow(b, u, free):
            nc.sync.wait_ge(job_free[free[0]], free[1] + 1)
            nc.sync.dma_start(QS[u][96:97, 0:128 * (TILES - 1)], MB[0:TILES - 1, :]).then_inc(mrow_ld, 16)
            nc.sync.dma_start(QS[u][96:97, 128 * (TILES - 1):16 * L], MB[TILES - 1:TILES, 0:TLAST]).then_inc(mrow_ld, 16)

        def sp_ctx(b, u):
            nc.sync.dma_start(CT[u][:, :], a["ctx_t"][bass.ds(b, 1)].rearrange("b p n -> (b p) n")).then_inc(ctx_ld[u], 16)

        def sp_xattn0():
            nc.sync.wait_ge(x_ready, 2)
            nc.sync.wait_ge(one_row, 1)
            for u in range(2):
                nc.sync.dma_start(KST[u][96:97, :, :], ONE_ROW[0:1, :].unsqueeze(1).broadcast_to([1, 8, S])).then_inc(ones_ld, 16)
            nc.sync.wait_ge(q_cut, 5)
            for i in range(3):
                nc.sync.dma_start(a["q_parts"][i], QP[i]).then_inc(qp_st, 16)
            nc.sync.wait_ge(qp_st, 48)
            nc.sync.wait_ge(qs_zero, 2)
            sp_queries(QS[0], qs_ld, 0)
            for b in range(2):
                for c in range(3):
                    sp_kstore(c, b, b)
                    sp_kload(c, b, b)
                if b == 0:
                    sp_mrow(0, 0, turn(3))

            def body(b, u, more):
                if more:
                    nc.sync.wait_ge(unit_done, b * UNITS + 1)
                    if more == 2:
                        sp_ctx(b + 2, u)
                    sp_queries(QS[1 - u], qs_ld, b + 1)
                for c in range(2):
                    if more == 2:
                        sp_kstore(c, b + 2, u, [(unit_done, b * UNITS + 16 * (c + 1))])
                        sp_kload(c, b + 2, u)
                if more:
                    sp_mrow(b + 1, 1 - u, job("M", b, more))
                if more == 2:
                    sp_kstore(2, b + 2, u, [(unit_done, b * UNITS + UNITS)])
                    sp_kload(2, b + 2, u)
            steps(nc.sync, body)

        f32, _ = carve(STAGE5_HIGH + 6 * 1024)
        PT_F, QT_F, MIX = f32(128), f32(128), f32(128)
        ft_mm, ft_ev = sem("ft_mm"), sem("ft_ev")

        def pe_fourier_matrix():
            nc.tensor.wait_ge(ld["late"], 16 * LOADS["late"])
            w = wts
            nc.tensor.matmul(PS[:, 6, 0:128], w["ft_wr"][:, :], w["ft_c"][:, :], start=True, stop=False)
            nc.tensor.matmul(PS[:, 6, 0:128], w["ft_wi"][:, :], w["ft_s"][:, :], start=False, stop=True).then_inc(ft_mm, 1)
            nc.tensor.matmul(PS[:, 7, 0:128], w["ft_wi"][:, :], w["ft_c"][:, :], start=True, stop=False)
            nc.tensor.matmul(PS[:, 7, 0:128], w["ft_wr"][:, :], w["ft_ns"][:, :], start=False, stop=True).then_inc(ft_mm, 1)
            nc.tensor.wait_ge(ft_ev, 2)
            nc.tensor.matmul(PS[:, 6, 0:128], PT_F, w["ft_cd"][:, :], start=True, stop=False)
            nc.tensor.matmul(PS[:, 6, 0:128], QT_F, w["ft_nsd"][:, :], start=False, stop=True).then_inc(ft_mm, 1)

        def dve_fourier_matrix():
            for i, m in enumerate((PT_F, QT_F, MIX)):
                nc.vector.wait_ge(ft_mm, i + 1)
                nc.vector.tensor_copy(m, PS[:, 6 + i % 2, 0:128]).then_inc(ft_ev, 1)

        def pe_fourier():
            pe_x(2)
            nc.tensor.wait_ge(ft_ev, 3)
            for j in range(2):
                nc.tensor.matmul(PS[:, 4 + j, 0:HT], MIX, half(X[0], j), start=True, stop=True).then_inc(op_done, 1)

        KB_DVE = 5
        SMALL_SEMS = {s: sem("small_" + s) for s in (
            "qk_mm", "v_mm", "q_ready", "k_ready", "va_zero", "va_one", "v_ready", "kb_dve", "kb_act", "qb_loaded0", "qb_loaded1",
            "vb_loaded0", "vb_loaded1", "s_mm", "max_ready", "subtracted", "exp_done", "t_mm", "pt_ready", "pv_done", "as_ready",
            "den_mm", "ln_done", "rd_ready", "acc_ready")}

        class Small:

            def __init__(self, first, heads, scale, w, src, src_ready, src_count):
                self.heads, self.scale, self.R, self.w = heads, scale, heads // 8, w
                self.src, self.src_ready, self.src_count = src, src_ready, src_count
                f32, _ = carve(0)
                self.KB = f32(B * heads * L).rearrange("p (b n) -> p b n", b=B)
                self.KF, self.QF = f32(T), f32(T)
                self.VA = f32(B * 256).rearrange("p (b g n) -> p b g n", b=B, g=8)
                self.QB = [f32(L) for _ in range(2)]
                self.VB = [f32(256) for _ in range(2)]
                self.SS = [f32(8 * L) for _ in range(2)]
                self.PT = [f32(8 * L) for _ in range(2)]
                self.NM = [f32(8) for _ in range(2)]
                self.AS = [f32(2 * L) for _ in range(2)]
                self.RD = [f32(2 * L) for _ in range(2)]
                self.ACC = f32(2 * self.R * T).rearrange("p (i n) -> p i n", i=2 * self.R)
                self.end = f32
                self.s = SMALL_SEMS
                self.first = first
                self.at_x = 6 if first is None else 10
                self.mask = wts["of_head"] if heads == 16 else wts["of_head8"]

            def before(self, name):
                once = dict(qk_mm=2, v_mm=2, q_ready=1, k_ready=1, va_zero=1, va_one=1, v_ready=2)
                if self.first is None:
                    return 0
                if name in once:
                    return once[name]
                if name in ("kb_dve", "kb_act"):
                    return self.first.R * (KB_DVE if name == "kb_dve" else 8 - KB_DVE)
                return 16 * B // 2 if "loaded" in name else B * self.first.R

        def scores_view(v):
            return v.rearrange("p j (h n) -> p j h n", h=4)

        SMALL_CREDITS = dict(subtracted=2, t_mm=2, pt_ready=1, pv_done=2, as_ready=1, ln_done=1, acc_ready=2)

        def pe_small(q):
            s = q.s
            nc.tensor.wait_ge(q.src_ready, q.src_count)
            nc.tensor.wait_ge(ld["late"], 16 * LOADS["late"])
            for i, n in enumerate(("wq", "wk")):
                for j in range(2):
                    m = nc.tensor.matmul(PS[:, 2 * i + j, 0:HT], wts[q.w + n][:, :], half(q.src, j), start=True, stop=True)
                m.then_inc(s["qk_mm"], 1)
            for b in range(B):
                m = nc.tensor.matmul(PS[0:L, 4 + b // 4, b % 4 * 128:b % 4 * 128 + 128], q.src[:, b * L:(b + 1) * L], wts[q.w + "wv"][:, :], start=True, stop=True)
                if b % 4 == 3:
                    m.then_inc(s["v_mm"], 1)

            def scores(b, par, r, i, qpar, qcount):
                nc.tensor.wait_ge(s[f"qb_loaded{qpar}"], qcount)
                nc.tensor.wait_ge(s["subtracted"], q.before("subtracted") + i + 1)
                for j in range(2):
                    m = nc.tensor.matmul(PS[0:L, 2 * par + j, 0:HT], q.QB[qpar], q.KB[:, b, bass.ds((8 * r + 4 * j) * L, 4 * L)] if isinstance(b, int)
                                         else q.KB_FLAT[:, bass.ds(b * (q.heads * L) + (8 * r + 4 * j) * L, 4 * L)], start=True, stop=True)
                m.then_inc(s["s_mm"], 1)

            def transposes(i, par):
                nc.tensor.wait_ge(s["exp_done"], q.before("exp_done") + i + 1)
                nc.tensor.wait_ge(s["pt_ready"], q.before("pt_ready") + i + 1)
                for h in range(8):
                    m = nc.tensor.transpose(PS[0:L, 4 + h // 4, h % 4 * L:(h % 4 + 1) * L], q.SS[par][0:L, h * L:(h + 1) * L], wts["ident"][0:L, 0:L])
                m.then_inc(s["t_mm"], 1)

            nc.tensor.wait_ge(s["q_ready"], q.before("q_ready") + 1)
            for i in range(2):
                b, r = i // q.R, i % q.R
                nc.tensor.wait_ge(s["kb_dve"], q.before("kb_dve") + (r + 1) * KB_DVE)
                nc.tensor.wait_ge(s["kb_act"], q.before("kb_act") + (r + 1) * (8 - KB_DVE))
                scores(b, i, r, i, b, q.before(f"qb_loaded{b}") + 16)
                if i == 0:
                    nc.tensor.wait_ge(s["v_ready"], q.before("v_ready") + 2)
                    transposes(0, 0)

            def body(b, u, more):
                for r in range(q.R):
                    i, par = b * q.R + r, (u * q.R + r) % 2
                    if more:
                        nb, nu = (b + 1, 1 - u) if q.R == 2 else (b + 2, u)
                        scores(nb, par, r, i + 2, nu, q.before(f"qb_loaded{nu}") + ctx_count(nb, nu))
                    if r == 0:
                        nc.tensor.wait_ge(s[f"vb_loaded{u}"], q.before(f"vb_loaded{u}") + ctx_count(b, u))
                    nc.tensor.wait_ge(s["pt_ready"], q.before("pt_ready") + i + 2)
                    nc.tensor.wait_ge(s["as_ready"], q.before("as_ready") + i + 1)
                    groups = 4 * (2 // q.R)
                    w = 8 * L // groups
                    for g in range(groups):
                        j, c = g % 4, g // 4
                        at = (4 * r + g) * 32
                        m = nc.tensor.matmul(PS[32 * j:32 * j + 32, 6, c * w:(c + 1) * w], q.VB[u][0:L, at:at + 32], q.PT[par][0:L, g * w:(g + 1) * w],
                                             start=(c == 0), stop=True, skip_group_check=True)
                    m.then_inc(s["pv_done"], 1)
                    if not isinstance(i, int) or i < B * q.R - 1:
                        transposes(i + 1, 1 - par)
                    nc.tensor.wait_ge(s["as_ready"], q.before("as_ready") + i + 2)
                    nc.tensor.wait_ge(s["ln_done"], q.before("ln_done") + i + 1)
                    nc.tensor.matmul(PS[:, 7, 0:2 * L], wts["seld"][:, :], q.AS[par], start=True, stop=True).then_inc(s["den_mm"], 1)
            steps_small(nc.tensor, q, body)

        def steps_small(engine, q, body):
            with engine.Fori(0, B // 2 - 1) as pair:
                for u in range(2):
                    body(pair * 2 + u, u, True)
            body(B - 2, 0, q.R == 2)
            body(B - 1, 1, False)

        def dve_small(q):
            s = q.s
            nc.vector.wait_ge(s["qk_mm"], q.before("qk_mm") + 1)
            nc.vector.tensor_scalar(two(q.QF), PS[:, 0:2, 0:HT], wts[q.w + "bq"][:, 0:1], q.scale, ALU.add, ALU.mult).then_inc(s["q_ready"], 1)
            def block_keys(r):
                for h in range(8 * r, 8 * r + KB_DVE):
                    nc.vector.tensor_scalar(q.KB[:, :, h * L:(h + 1) * L], by_batch(q.KF), q.mask[:, h:h + 1], None, ALU.mult).then_inc(s["kb_dve"], 1)
            nc.vector.wait_ge(s["k_ready"], q.before("k_ready") + 1)
            block_keys(0)
            bias = wts[q.w + "bv"][0:L, :].rearrange("p (g n) -> p g n", g=8)
            for c in range(2):
                nc.vector.wait_ge(s["v_mm"], q.before("v_mm") + c + 1)
                for b in range(4 * c, 4 * c + 4):
                    m = nc.vector.tensor_tensor(q.VA[0:L, b, :, 0:16], PS[0:L, 4 + c, b % 4 * 128:b % 4 * 128 + 128].rearrange("p (g n) -> p g n", g=8), bias, ALU.add)
                m.then_inc(s["v_ready"], 1)

            def views(par):
                return scores_view(PS[0:L, 2 * par:2 * par + 2, 0:HT]), q.NM[par][0:L, :].rearrange("p (j h) -> p j h", j=2)

            def maxima(i, par):
                nc.vector.wait_ge(s["s_mm"], q.before("s_mm") + i + 1)
                nc.vector.tensor_reduce(views(par)[1], views(par)[0], X_AXIS, ALU.max).then_inc(s["max_ready"], 1)

            def subtract(i, par):
                sc, nm = views(par)
                nc.vector.wait_ge(s["max_ready"], q.before("max_ready") + i + 1)
                nc.vector.wait_ge(s["t_mm"], q.before("t_mm") + i + 1)
                nc.vector.tensor_tensor(q.SS[par][0:L, :].rearrange("p (j h n) -> p j h n", j=2, h=4), sc,
                                        nm.unsqueeze(3).broadcast_to([L, 2, 4, L]), ALU.subtract).then_inc(s["subtracted"], 1)
            for i in range(2):
                if i == 1 and q.R == 2:
                    block_keys(1)
                maxima(i, i)
                subtract(i, i)

            def body(b, u, more):
                for r in range(q.R):
                    i, par = b * q.R + r, (u * q.R + r) % 2
                    if more:
                        maxima(i + 2, par)
                    nc.vector.wait_ge(s["pv_done"], q.before("pv_done") + i + 3)
                    nc.vector.wait_ge(s["acc_ready"], q.before("acc_ready") + i + 1)
                    nc.vector.tensor_copy(q.AS[par], PS[:, 6, 0:2 * L]).then_inc(s["as_ready"], 1)
                    if more:
                        subtract(i + 2, par)
            steps_small(nc.vector, q, body)

        def act_small(q):
            s = q.s
            nc.scalar.wait_ge(s["qk_mm"], q.before("qk_mm") + 2)
            nc.scalar.activation(two(q.KF), PS[:, 2:4, 0:HT], ACT.Identity, bias=wts[q.w + "bk"][:, 0:1]).then_inc(s["k_ready"], 1)
            nc.scalar.wait_ge(s["k_ready"], q.before("k_ready") + 1)
            for r in range(q.R):
                for h in range(8 * r + KB_DVE, 8 * r + 8):
                    nc.scalar.activation(q.KB[:, :, h * L:(h + 1) * L], by_batch(q.KF), ACT.Copy, scale=q.mask[:, h:h + 1]).then_inc(s["kb_act"], 1)

            def expo(i, par):
                nc.scalar.wait_ge(s["subtracted"], q.before("subtracted") + i + 3)
                nc.scalar.activation(q.SS[par][0:L, :], q.SS[par][0:L, :], ACT.Exp).then_inc(s["exp_done"], 1)
            def turned(i, par):
                nc.scalar.wait_ge(s["t_mm"], q.before("t_mm") + i + 3)
                nc.scalar.wait_ge(s["pv_done"], q.before("pv_done") + i + 1)
                nc.scalar.activation(two(q.PT[par][0:L, :]), PS[0:L, 4:6, 0:HT], ACT.Copy).then_inc(s["pt_ready"], 1)
            expo(0, 0)
            expo(1, 1)
            turned(0, 0)

            def body(b, u, more):
                for r in range(q.R):
                    i, par = b * q.R + r, (u * q.R + r) % 2
                    if not isinstance(i, int) or i < B * q.R - 1:
                        turned(i + 1, 1 - par)
                    nc.scalar.wait_ge(s["den_mm"], q.before("den_mm") + i + 1)
                    nc.scalar.wait_ge(s["acc_ready"], q.before("acc_ready") + i + 1)
                    nc.scalar.activation(q.RD[par], PS[:, 7, 0:2 * L], ACT.Ln).then_inc(s["ln_done"], 1)
                    nc.scalar.wait_ge(s["ln_done"], q.before("ln_done") + i + 2)
                    nc.scalar.activation(q.RD[par], q.RD[par], ACT.Exp, scale=-1.0).then_inc(s["rd_ready"], 1)
                    if more:
                        expo(i + 2, par)
            steps_small(nc.scalar, q, body)

        def pool_small(q):
            s = q.s
            nc.gpsimd.wait_ge(x_ready, q.at_x)
            nc.gpsimd.memset(q.VA[0:L, :, :, 17:32], 0.0).then_inc(s["va_zero"], 1)
            nc.gpsimd.memset(q.VA[0:L, :, :, 16:17], 1.0).then_inc(s["va_one"], 1)

            def body(b, u, more):
                for r in range(q.R):
                    i, par = b * q.R + r, (u * q.R + r) % 2
                    nc.gpsimd.wait_ge(s["rd_ready"], q.before("rd_ready") + i + 1)
                    nc.gpsimd.tensor_tensor(q.ACC[:, 2 * r:2 * r + 2, bass.ds(b * L, L)], q.AS[par].rearrange("p (c n) -> p c n", c=2),
                                            q.RD[par].rearrange("p (c n) -> p c n", c=2), ALU.mult).then_inc(s["acc_ready"], 1)
            steps_small(nc.gpsimd, q, body)

        def sp_small(q):
            s = q.s
            def queries(b, u):
                nc.sync.dma_start(q.QB[u], q.QF[:, bass.ds(b * L, L)]).then_inc(s[f"qb_loaded{u}"], 16)

            def values(b, u):
                nc.sync.dma_start(q.VB[u][0:L, :], q.VA_FLAT[0:L, bass.ds(b * 256, 256)]).then_inc(s[f"vb_loaded{u}"], 16)
            nc.sync.wait_ge(s["q_ready"], q.before("q_ready") + 1)
            for b in range(2):
                queries(b, b)
            nc.sync.wait_ge(s["v_ready"], q.before("v_ready") + 2)
            nc.sync.wait_ge(s["va_zero"], q.before("va_zero") + 1)
            nc.sync.wait_ge(s["va_one"], q.before("va_one") + 1)
            for b in range(2):
                values(b, b)
            with nc.sync.Fori(0, B // 2 - 1) as pair:
                for u in range(2):
                    b = pair * 2 + u
                    nc.sync.wait_ge(s["s_mm"], q.before("s_mm") + b * q.R + q.R)
                    queries(b + 2, u)
                    nc.sync.wait_ge(s["pv_done"], q.before("pv_done") + b * q.R + (q.R + 2))
                    values(b + 2, u)

        f32, b16 = carve(0)
        QPJ = f32(8 * T)
        CN = [f32(KT * 128).rearrange("p (t d) -> p t d", t=KT) for _ in range(2)]
        CH = b16(S)
        QB5 = [f32(8 * L) for _ in range(2)]
        QH5 = [b16(8 * L) for _ in range(2)]
        SHIFT5 = [f32(8 * L) for _ in range(2)]
        DIAG5 = b16(8 * L)
        PT5 = [f32(8 * L) for _ in range(2)]
        DS, RD5, ZERO = f32(8 * L), f32(8 * L), f32(8 * L)
        MX5, MXC5 = f32(8 * 3).rearrange("p (h c) -> p h c", c=3), f32(8)
        ONES5 = b16(128)
        f32, _ = carve(STAGE5_HIGH)
        GQK = f32(1024).rearrange("p (h n) -> p h n", h=8)
        GVO = f32(1024).rearrange("p (h n) -> p h n", h=8)
        W5 = {n: f32(1024).rearrange("p (h n) -> p h n", h=8) for n in ("x_wq", "x_wk", "x_wv", "x_wo")}
        CO = f32(8 * T).rearrange("p (h n) -> p h n", h=8)
        U5 = 2 * KT
        MAX5 = (3, 9)
        w5_ld, g_mm, g_ev, q5_mm, q5_ev = sem("w5_ld"), sem("g_mm"), sem("g_ev"), sem("q5_mm"), sem("q5_ev")
        c5_ld, cn_ld, qb5_ld = ([sem(f"{n}{u}") for u in range(2)] for n in ("c5_ld", "cn_ld", "qb5_ld"))
        ch_ready, qh_ready, mx5_mm, mx5_read, mxc5, diag5, shift_mm, shift5, sub5 = (sem(n) for n in ("ch_ready", "qh_ready", "mx5_mm", "mx5_read", "mxc5", "diag5", "shift_mm", "shift5", "sub5"))
        unit5, exp5, pv5, ds5, den5, ln5, rd5, co5, init5, initp5 = (sem(n) for n in ("unit5", "exp5", "pv5", "ds5", "den5", "ln5", "rd5", "co5", "init5", "initp5"))

        def pe_products5():
            nc.tensor.wait_ge(w5_ld, 64)
            for i, (l, r) in enumerate((("x_wq", "x_wk"), ("x_wv", "x_wo"))):
                if i:
                    nc.tensor.wait_ge(g_ev, 1)
                for h in range(8):
                    m = nc.tensor.matmul(PS[:, 6 + h // 4, h % 4 * 128:h % 4 * 128 + 128], W5[l][0:64, h, :], W5[r][0:64, h, :], start=True, stop=True)
                m.then_inc(g_mm, 1)

        def dve_products5():
            for i, g in enumerate((GQK, GVO)):
                nc.vector.wait_ge(g_mm, i + 1)
                nc.vector.tensor_copy(g.rearrange("p (j h) n -> p j (h n)", j=2), PS[:, 6:8, :]).then_inc(g_ev, 1)

        def pe_max5(unit, u, b):
            c, h = unit // 8, unit % 8
            at, n = KC[c]
            if unit == 0:
                nc.tensor.wait_ge(ch_ready, b + 1)
                nc.tensor.wait_ge(qh_ready, b + 1)
            nc.tensor.wait_ge(mx5_read, b * U5 + unit + 1)
            nc.tensor.matmul(PS[0:L, 2 + unit % 2, 0:n], QH5[u][:, h * L:(h + 1) * L], CH[:, at:at + n], start=True, stop=True).then_inc(mx5_mm, 1)

        def pe_shift5(b):
            nc.tensor.wait_ge(diag5, b + 1)
            nc.tensor.wait_ge(ln5, b if not isinstance(b, int) else max(b, 1))
            for g in range(2):
                m = nc.tensor.matmul(PS[:, 6 + g, 0:HT], ONES5[0:L, :], DIAG5[0:L, g * HT:(g + 1) * HT], start=True, stop=True)
            m.then_inc(shift_mm, 1)

        def pe_xattn5():
            pe_x(4)
            nc.tensor.wait_ge(g_ev, 2)
            for h in range(8):
                for j in range(2):
                    n = 2 * h + j
                    if n >= 4:
                        nc.tensor.wait_ge(q5_ev, n - 3)
                    nc.tensor.matmul(PS[:, n % 4, 0:HT], GQK[:, h, :], half(X[0], j), start=True, stop=True).then_inc(q5_mm, 1)
            nc.tensor.wait_ge(q5_ev, 16)
            for unit in range(U5):
                pe_max5(unit, 0, 0)
            pe_shift5(0)

            def pv(b, u, kt, g):
                n = rows(kt)
                if kt == 0 and g == 0:
                    nc.tensor.wait_ge(cn_ld[u], ctx_count(b, u) * 2)
                    nc.tensor.wait_ge(co5, b + 1)
                nc.tensor.wait_ge(exp5, b * U5 + (2 * kt + g + 1 + 2))
                m = nc.tensor.matmul(PS[:, 4 + g, 0:HT], CN[u][0:n, kt, :], PT5[kt % 2][0:n, g * HT:(g + 1) * HT], start=(kt == 0), stop=(kt == KT - 1))
                if g == 1:
                    m.then_inc(pv5, 1)

            def body(b, u, more):
                nxt = 0

                def maxima():
                    nonlocal nxt
                    if more and MAX5[0] <= kt < MAX5[1]:
                        pe_max5(nxt, 1 - u, b + 1)
                        nxt += 1
                nc.tensor.wait_ge(c5_ld[u], ctx_count(b, u))
                nc.tensor.wait_ge(qb5_ld[u], ctx_count(b, u))
                for kt in range(KT):
                    n = rows(kt)
                    for g in range(2):
                        unit = 2 * kt + g
                        nc.tensor.wait_ge(sub5, b * U5 + unit + 1)
                        nc.tensor.matmul(PS[0:n, unit % 2, 0:HT], CT[u][:, kt * 128:kt * 128 + n], QB5[u][:, g * HT:(g + 1) * HT], start=True, stop=True).then_inc(unit5, 1)
                        maxima()
                    for g in range(2):
                        if kt > 0:
                            pv(b, u, kt - 1, g)
                        maxima()
                    if more and kt == 10:
                        pe_shift5(b + 1)
                for g in range(2):
                    pv(b, u, KT - 1, g)
                nc.tensor.wait_ge(ds5, b * KT + (KT + 2))
                nc.tensor.wait_ge(ln5, b + 1)
                nc.tensor.wait_ge(shift5, b + 1 + (1 if more else 0))
                for g in range(2):
                    m = nc.tensor.matmul(PS[:, 6 + g, 0:HT], wts["ones"][:, :], DS[:, g * HT:(g + 1) * HT], start=True, stop=True)
                m.then_inc(den5, 1)
            steps(nc.tensor, body)
            pe_out(CO, GVO, co5, B + 1, 8)

        def act_xattn5():
            for n in range(16):
                h, j = n // 2, n % 2
                nc.scalar.wait_ge(q5_mm, n + 1)
                nc.scalar.activation(QPJ.rearrange("p (b h n) -> p b h n", b=B, h=8)[:, 4 * j:4 * j + 4, h, :],
                                     PS[:, n % 4, 0:HT].rearrange("p (b n) -> p b n", b=4), ACT.Copy, scale=64.0 ** -0.5).then_inc(q5_ev, 1)

            def shift(b, u):
                nc.scalar.wait_ge(shift_mm, b + 1)
                nc.scalar.activation(two(SHIFT5[u]), PS[:, 6:8, 0:HT], ACT.Copy).then_inc(shift5, 1)
            shift(0, 0)

            def body(b, u, more):
                for kt in range(KT):
                    n = rows(kt)
                    for g in range(2):
                        unit = 2 * kt + g
                        nc.scalar.wait_ge(sub5, b * U5 + (unit + 3))
                        nc.scalar.activation(PT5[kt % 2][0:n, g * HT:(g + 1) * HT], PT5[kt % 2][0:n, g * HT:(g + 1) * HT], ACT.Exp).then_inc(exp5, 1)
                    if more and kt == 10:
                        shift(b + 1, 1 - u)
                nc.scalar.wait_ge(den5, b + 2)
                nc.scalar.wait_ge(co5, b + 1)
                nc.scalar.activation(two(RD5), PS[:, 6:8, 0:HT], ACT.Ln).then_inc(ln5, 1)
                nc.scalar.wait_ge(ln5, b + 2)
                nc.scalar.activation(RD5, RD5, ACT.Exp, scale=-1.0).then_inc(rd5, 1)
            steps(nc.scalar, body)

        def pool_xattn5():
            nc.gpsimd.wait_ge(x_ready, 8)
            nc.gpsimd.memset(ZERO, 0.0).then_inc(initp5, 1)
            nc.gpsimd.wait_ge(initp5, 1)

            def body(b, u, more):
                for kt in range(KT):
                    n = rows(kt)
                    nc.gpsimd.wait_ge(exp5, b * U5 + (2 * kt + 2 + 2))
                    if kt == 0:
                        nc.gpsimd.wait_ge(den5, b + 1)
                    nc.gpsimd.wait_ge(ds5, b * KT + (kt + 2))
                    nc.gpsimd.tensor_tensor(DS[0:n, :], PT5[kt % 2][0:n, :], (ZERO if kt == 0 else DS)[0:n, :], ALU.add).then_inc(ds5, 1)
            steps(nc.gpsimd, body)

        def dve_xattn5():
            nc.vector.wait_ge(x_ready, 8)
            nc.vector.memset(ONES5, 1.0).then_inc(init5, 1)

            def casts(b, u):
                nc.vector.wait_ge(c5_ld[u], ctx_count(b, u))
                if not isinstance(b, int) or b > 0:
                    nc.vector.wait_ge(mx5_mm, b * U5)
                nc.vector.tensor_copy(CH, CT[u][:, :]).then_inc(ch_ready, 1)
                nc.vector.wait_ge(qb5_ld[u], ctx_count(b, u))
                nc.vector.tensor_copy(QH5[u], QB5[u]).then_inc(qh_ready, 1)

            def maximum(unit, b):
                c, h = unit // 8, unit % 8
                nc.vector.wait_ge(mx5_mm, b * U5 + unit + 1)
                nc.vector.tensor_reduce(MX5[0:L, h, c:c + 1], PS[0:L, 2 + unit % 2, 0:KC[c][1]], X_AXIS, ALU.max).then_inc(mx5_read, 1)

            def diagonals(b):
                nc.vector.wait_ge(mx5_read, b * U5 + (U5 + 2))
                nc.vector.tensor_reduce(MXC5[0:L, 0:8], MX5[0:L, :, :], X_AXIS, ALU.max, negate=True).then_inc(mxc5, 1)
                nc.vector.wait_ge(mxc5, b + 1)
                if not isinstance(b, int) or b > 0:
                    nc.vector.wait_ge(shift_mm, b)
                nc.vector.tensor_tensor(DIAG5[0:L, :].rearrange("p (h n) -> p h n", h=8), wts["ident"][0:L, 0:L].unsqueeze(1).broadcast_to([L, 8, L]),
                                        MXC5[0:L, 0:8].unsqueeze(2).broadcast_to([L, 8, L]), ALU.mult).then_inc(diag5, 1)
            def subtract(b, u, kt, g):
                n, unit = rows(kt), 2 * kt + g
                if kt == 0 and g == 0:
                    nc.vector.wait_ge(shift5, b + 1)
                if g == 0:
                    nc.vector.wait_ge(pv5, b * KT + kt + 1)
                    nc.vector.wait_ge(ds5, b * KT + kt + 1)
                nc.vector.wait_ge(unit5, b * U5 + unit + 1)
                nc.vector.tensor_tensor(PT5[kt % 2][0:n, g * HT:(g + 1) * HT], PS[0:n, unit % 2, 0:HT], SHIFT5[u][0:n, g * HT:(g + 1) * HT], ALU.add).then_inc(sub5, 1)
            casts(0, 0)
            for unit in range(U5):
                maximum(unit, 0)
            nc.vector.wait_ge(init5, 1)
            diagonals(0)
            for g in range(2):
                subtract(0, 0, 0, g)

            def body(b, u, more):
                nxt = 0

                def maxima(b_):
                    nonlocal nxt
                    if more and MAX5[0] <= kt < MAX5[1]:
                        maximum(nxt, b_)
                        nxt += 1
                if more:
                    following = own_register(nc.vector, b + 1)
                for kt in range(1, KT):
                    for g in range(2):
                        subtract(b, u, kt, g)
                        if more:
                            maxima(following)
                    for g in range(2):
                        if more:
                            maxima(following)
                    if more and kt == MAX5[0] - 1:
                        casts(b + 1, 1 - u)
                    if more and kt == MAX5[1] - 1:
                        diagonals(b + 1)
                if more:
                    for g in range(2):
                        subtract(b + 1, 1 - u, 0, g)
                nc.vector.wait_ge(pv5, b * KT + (KT + 2))
                nc.vector.wait_ge(rd5, b + 1)
                for g in range(2):
                    m = nc.vector.tensor_tensor(CO[:, 4 * g:4 * g + 4, bass.ds(b * L, L)], PS[:, 4 + g, 0:HT].rearrange("p (h n) -> p h n", h=4),
                                                RD5[:, g * HT:(g + 1) * HT].rearrange("p (h n) -> p h n", h=4), ALU.mult)
                m.then_inc(co5, 1)
            steps(nc.vector, body)
            dve_residual(5, wts["x_bo"][:, 0:1])

        def sp_context(b, u):
            nc.sync.dma_start(QB5[u], QPJ[:, bass.ds(b * (8 * L), 8 * L)]).then_inc(qb5_ld[u], 16)
            nc.sync.dma_start(CT[u][:, :], a["ctx_t"][bass.ds(b, 1)].rearrange("b p n -> (b p) n")).then_inc(c5_ld[u], 16)
            flat = a["ctx"].rearrange("b s d -> (b s) d")
            nc.sync.dma_start(CN[u][:, 0:KT - 1, :], flat[bass.ds(b * S, 128 * (KT - 1)), :].rearrange("(t p) d -> p t d", p=128)).then_inc(cn_ld[u], 16)
            nc.sync.dma_start(CN[u][0:KLAST, KT - 1, :], flat[bass.ds(b * S + 128 * (KT - 1), KLAST), :]).then_inc(cn_ld[u], 16)

        def sp_xattn5():
            nc.sync.wait_ge(q5_ev, 16)
            sp_context(0, 0)

            def body(b, u, more):
                if more:
                    waits(nc.sync, (unit5, b * U5 + 1), (pv5, b * KT + 2))
                    sp_context(b + 1, 1 - u)
            steps(nc.sync, body)

        xn_core, xn_ready, x_twice = sem("xn_core"), sem("xn_ready"), sem("x_twice")
        XN = CT[0][:, 0:T]
        gqa = Small(None, 16, 8.0 ** -0.5, "g_", X[1], x_ready, 6)
        mha = Small(gqa, 8, 128.0 ** -0.5, "f_", XN, xn_ready, 4)
        for q in (gqa, mha):
            q.KB_FLAT = q.KB.rearrange("p b n -> p (b n)")
            q.VA_FLAT = q.VA.rearrange("p b g n -> p (b g n)")

        def by_expert(v, e):
            return v.rearrange("p (b e n) -> p b e n", e=4, n=L // 4)[:, :, e, :]

        def dve_expert_input():
            for e in range(4):
                if e == 0:
                    nc.vector.wait_ge(xn_core, 2)
                nc.vector.tensor_scalar(by_expert(XN, e), by_expert(CEN, e), wts["f_nw"][:, e:e + 1], wts["f_nb"][:, e:e + 1], ALU.mult, ALU.add).then_inc(xn_ready, 1)

        def pe_experts_out():
            nc.tensor.wait_ge(mha.s["acc_ready"], mha.before("acc_ready") + B + 2)
            for j in range(2):
                for e in range(4):
                    for r in range(2):
                        m = nc.tensor.matmul(by_expert(PS[:, 4 + j, 0:HT], e), wts["f_wo"][:, 2 * e + r, :], by_expert(mha.ACC[:, r, j * HT:(j + 1) * HT], e),
                                             start=(e == 0 and r == 0), stop=(e == 3 and r == 1), skip_group_check=True)
                m.then_inc(op_done, 1)

        def dve_twice_x():
            nc.vector.tensor_scalar(Z, X[1], 2.0, None, ALU.mult).then_inc(x_twice, 1)

        def dve_experts_residual():
            nc.vector.wait_ge(x_twice, 1)
            for j in range(2):
                nc.vector.wait_ge(op_done, 10 + j + 1)
                for e in range(4):
                    m = nc.vector.scalar_tensor_tensor(out=by_expert(half(Z, j), e), in0=by_expert(PS[:, 4 + j, 0:HT], e), scalar=wts["f_bo"][:, e:e + 1],
                                                       in1=by_expert(half(Z, j), e), op0=ALU.add, op1=ALU.add)
                m.then_inc(z_ready, 1)

        block = ctx.enter_context(nc.Block())

        @block.sync
        def _(sp):
            for s, n in [(scanned, 4), (g_ready, 2), (exp_done, 3), (pt_free, 2), (acc_free, 1), (mx_read, 2), (accn_ready, 1), (job_free[0], 1), (job_free[1], 1),
                         (exp5, 2), (sub5, 2), (pv5, 2), (ds5, 2), (mx5_read, 2), (co5, 1), (ln5, 1), (den5, 1)]:
                sp.sem_inc(s, n)
            for s, n in SMALL_CREDITS.items():
                sp.sem_inc(SMALL_SEMS[s], n)
            sp.dma_start(X[0], a["x_t"]).then_inc(ld["mamba"], 16)
            for g in ("mamba", "l0x", "late"):
                for n, (group, _) in W_RESIDENT.items():
                    if group == g:
                        sp.dma_start(wts[n][tuple(slice(None) for _ in wts[n].shape)], a[n]).then_inc(ld[g], 16)
                if g == "mamba":
                    for b in range(2):
                        sp_ctx(b, b)
            sp_xattn0()
            sp.wait_ge(x_ready, 4)
            for n in W5:
                sp.dma_start(W5[n][0:64], a[n]).then_inc(w5_ld, 16)
            sp_small(gqa)
            sp_xattn5()
            sp_small(mha)
            for j in range(2):
                sp.wait_ge(x_ready, 10 + j + 1)
                sp.dma_start(a["out_t"][:, j * HT:(j + 1) * HT], half(X[0], j)).then_inc(out_stored, 16)
            sp.wait_ge(out_stored, 32)

        @block.tensor
        def _(pe):
            pe_mamba()
            pe_ln(1, Z, z_ready, 0)
            pe_xattn0()
            pe_ln(2, Z, z_ready, 2)
            pe_fourier_matrix()
            pe_fourier()
            pe_ln(3, Z, z_ready, 4)
            pe_small(gqa)
            pe_out(gqa.ACC, wts["g_wo"], gqa.s["acc_ready"], 2 * B + 2, 4)
            pe_ln(4, Z, z_ready, 6)
            pe_products5()
            pe_xattn5()
            pe_ln(5, Z, z_ready, 8)
            pe_ln(6, X[1], x_ready, 8)
            pe_small(mha)
            pe_experts_out()
            pe_ln(7, Z, z_ready, 10)

        @block.vector
        def _(dve):
            dve_mamba()
            dve_ln(1, Z, X[1], x_ready)
            dve_xattn0()
            dve_ln(2, Z, X[0], x_ready)
            dve_fourier_matrix()
            dve_residual(3, wts["ft_b"][:, 0:1])
            dve_ln(3, Z, X[1], x_ready)
            dve_small(gqa)
            dve_residual(4, wts["g_bo"][:, 0:1])
            dve_ln(4, Z, X[0], x_ready)
            dve_products5()
            dve_xattn5()
            dve_ln(5, Z, X[1], x_ready)
            dve_ln(6, X[1], CEN, xn_core)
            dve_expert_input()
            dve_twice_x()
            dve_small(mha)
            dve_experts_residual()
            dve_ln(7, Z, X[0], x_ready)

        @block.scalar
        def _(act):
            act_mamba()
            act_ln(1)
            act_xattn0()
            act_ln(2)
            act_ln(3)
            act_small(gqa)
            act_ln(4)
            act_xattn5()
            act_ln(5)
            act_ln(6)
            act_small(mha)
            act_ln(7)

        @block.gpsimd
        def _(pool):
            pool_mamba()
            pool_xattn0()
            pool_small(gqa)
            pool_xattn5()
            pool_small(mha)


W_RESIDENT = {
    "ident": ("mamba", (128, 128)), "ones_d": ("mamba", (128, 128)), "ones": ("mamba", (128, 128)), "seld": ("mamba", (128, 128)),
    "eps": ("mamba", (128, 1)), "one": ("mamba", (128, 1)), "sel32": ("mamba", (128, 32)),
    "of_head": ("mamba", (128, 16)), "of_head8": ("mamba", (128, 8)), "w_in": ("mamba", (128, 512)), "conv_w": ("mamba", (128, 16)), "conv_b": ("mamba", (128, 4)), "w_xp": ("mamba", (128, 2, 2, 128)),
    "w_dt": ("mamba", (128, 2, 256)), "dt_b": ("mamba", (128, 4)), "a_log": ("mamba", (128, 64)), "d_skip": ("mamba", (128, 4)),
    "w_out": ("mamba", (128, 2, 128)),
    "l0_wq": ("l0x", (128, 128)), "l0_bq": ("l0x", (128, 1)), "l0_wk": ("l0x", (128, 128)), "l0_bk": ("l0x", (128, 1)),
    "l0_wv": ("l0x", (128, 128)), "l0_bv": ("l0x", (128, 128)), "l0_wo": ("l0x", (128, 4, 128)), "l0_bo": ("l0x", (128, 1)),
    "ft_wr": ("late", (128, 128)), "ft_wi": ("late", (128, 128)), "ft_c": ("late", (128, 128)), "ft_s": ("late", (128, 128)),
    "ft_ns": ("late", (128, 128)), "ft_cd": ("late", (128, 128)), "ft_nsd": ("late", (128, 128)), "ft_b": ("late", (128, 1)),
    "g_wq": ("late", (128, 128)), "g_bq": ("late", (128, 1)), "g_wk": ("late", (128, 128)), "g_bk": ("late", (128, 1)),
    "g_wv": ("late", (128, 128)), "g_bv": ("late", (128, 128)), "g_wo": ("late", (128, 4, 128)), "g_bo": ("late", (128, 1)),
    "x_bo": ("late", (128, 1)),
    "f_nw": ("late", (128, 4)), "f_nb": ("late", (128, 4)), "f_wq": ("late", (128, 128)), "f_bq": ("late", (128, 1)),
    "f_wk": ("late", (128, 128)), "f_bk": ("late", (128, 1)), "f_wv": ("late", (128, 128)), "f_bv": ("late", (128, 128)),
    "f_wo": ("late", (128, 8, 128)), "f_bo": ("late", (128, 4)),
}
MAMBA_ONLY = ("w_in", "w_xp", "w_dt", "w_out")
LOADS = {g: sum(x[0] == g for x in W_RESIDENT.values()) + (g == "mamba") for g in ("mamba", "l0x", "late")}


def layout(i):
    import numpy as np
    f = np.float32
    g = {k: np.asarray(v) for k, v in i.items()}
    col = lambda v: v.reshape(-1, 1)
    o = {}
    o["x_t"] = g["x"].reshape(T, D).T
    o["ctx"] = g["ctx_1024"]
    o["ctx_t"] = g["ctx_1024"].transpose(0, 2, 1)
    o["ident"] = np.eye(128, dtype=f)
    o["ones_d"] = np.full((128, 128), 1.0 / D, f)
    o["ones"] = np.ones((128, 128), f)
    o["eps"] = np.full((128, 1), EPS, f)
    o["one"] = np.ones((128, 1), f)
    sel = np.zeros((128, 32), f)
    for r in (0, 64, 96):
        sel[r:r + 32] = np.eye(32, dtype=f)
    o["sel32"] = sel
    o["of_head"] = np.repeat(np.eye(16, dtype=f), 8, axis=0)
    o["of_head8"] = np.repeat(np.eye(8, dtype=f), 16, axis=0)
    seld = np.zeros((128, 128), f)
    for j in range(4):
        seld[32 * j + 16, 32 * j:32 * j + 32] = 1.0
    o["seld"] = seld
    ang = 2 * np.pi * ((np.arange(D)[:, None] * np.arange(D)[None, :]) % D) / D
    c, s = np.cos(ang), np.sin(ang)
    o["ft_c"], o["ft_s"], o["ft_ns"], o["ft_cd"], o["ft_nsd"] = (v.astype(f) for v in (c, s, -s, c / D, -s / D))
    L0 = lambda n: g["L0_attn_" + n]
    o["w_in"] = L0("in_proj_w").T
    two_halves = lambda v, w: np.stack([v, w]).reshape(2, 2, 128, -1).transpose(2, 0, 1, 3)
    o["conv_w"] = two_halves(L0("conv_w"), L0("conv_wb")).reshape(128, 16)
    o["conv_b"] = two_halves(L0("conv_b"), L0("conv_bb")).reshape(128, 4)
    o["dt_b"] = two_halves(L0("dt_proj_b"), L0("dt_proj_bb")).reshape(128, 4)
    o["d_skip"] = two_halves(L0("D"), L0("D_b")).reshape(128, 4)
    o["a_log"] = two_halves(L0("A_log"), L0("A_b_log")).reshape(128, 64)
    w = np.zeros((128, 2, 2, 128), f)
    wd = np.zeros((128, 2, 256), f)
    for d, (xp, dp) in enumerate(((L0("x_proj_w"), L0("dt_proj_w")), (L0("x_proj_wb"), L0("dt_proj_wb")))):
        t = xp.T.reshape(2, 128, DR + 2 * NST).transpose(1, 0, 2)
        for r in (0, 64, 96):
            w[:, d, :, r:r + 32] = t[:, :, DR:]
        w[:, d, :, 32:32 + DR] = t[:, :, :DR]
        wd[32:32 + DR, d] = dp.T
    o["w_xp"], o["w_dt"] = w, wd
    o["w_out"] = L0("out_proj_w").T.reshape(2, 128, 128).transpose(1, 0, 2)

    def masked(wo, hd):
        n = 16 // hd
        r = np.zeros((128, 2 * n, 128), f)
        for p in range(8):
            for s_ in range(n):
                r[32 * (p % 4) + s_ * hd:32 * (p % 4) + (s_ + 1) * hd, n * (p // 4) + s_] = wo[(p * n + s_) * hd:(p * n + s_ + 1) * hd]
        return r
    X0 = lambda n: g["L0_xattn_" + n]
    for n in ("q", "k", "v"):
        o["l0_w" + n] = X0("W" + n)
    o["l0_bq"], o["l0_bk"], o["l0_bo"] = col(X0("bq")), col(X0("bk")), col(X0("bo"))
    o["l0_bv"] = np.broadcast_to(X0("bv"), (128, 128))
    o["l0_wo"] = masked(X0("Wo"), 8)
    o["ft_wr"], o["ft_wi"], o["ft_b"] = g["L0_ffn_w_freq_real"], g["L0_ffn_w_freq_imag"], col(g["L0_ffn_bias"])
    G = lambda n: g["L1_attn_" + n]
    rep = lambda v: np.broadcast_to(v.reshape(-1, 4, 1, 8), (v.size // 32, 4, 4, 8)).reshape(-1, 128)
    o["g_wq"], o["g_bq"], o["g_wo"], o["g_bo"] = G("Wq"), col(G("bq")), masked(G("Wo"), 8), col(G("bo"))
    o["g_wk"], o["g_bk"], o["g_wv"] = rep(G("Wk")), col(rep(G("bk"))), rep(G("Wv"))
    o["g_bv"] = np.broadcast_to(rep(G("bv")), (128, 128))
    Y = lambda n: g["L1_xattn_" + n]
    for n in ("q", "k", "v"):
        o["x_w" + n] = Y("W" + n).T.reshape(8, 64, 128).transpose(1, 0, 2)
    o["x_wo"] = Y("Wo").reshape(8, 64, 128).transpose(1, 0, 2)
    o["x_bo"] = col(Y("bo"))
    F = lambda n: g["L1_ffn_" + n]
    nw, nb, bo = (np.zeros((128, 4), f) for _ in range(3))
    wo = np.zeros((128, 8, 128), f)
    for e in range(4):
        m = D >> e
        nw[:m, e], nb[:m, e], bo[:m, e] = F("norm_w")[:m], F("norm_b")[:m], F("o_b")[:m]
        we = np.zeros((128, 128), f)
        we[:m, :m] = F("o_w")[:m, :m].T
        wo[:, 2 * e:2 * e + 2] = masked(we, 16)
    o["f_nw"], o["f_nb"], o["f_bo"], o["f_wo"] = nw, nb, bo, wo
    for n in ("q", "k", "v"):
        o["f_w" + n] = F(n + "_w").T
    o["f_bq"], o["f_bk"] = col(F("q_b")), col(F("k_b"))
    o["f_bv"] = np.broadcast_to(F("v_b"), (128, 128))
    return {k: np.ascontiguousarray(v) for k, v in o.items()}


def kernel(**inputs):
    import concourse.bacc as bacc
    from concourse.bass_utils import run_bass_kernel_spmd

    nc = bacc.Bacc("TRN2", target_bir_lowering=False, num_devices=1)
    arrays = layout(inputs)
    a = {k: nc.dram_tensor(k, v.shape, mybir.dt.from_np(v.dtype), kind="ExternalInput").ap() for k, v in arrays.items()}
    a["out_t"] = nc.dram_tensor("out_t", (D, T), F32, kind="ExternalOutput").ap()
    a["k_parts"] = nc.dram_tensor("k_parts", (2, 3, 128, S), BF16, kind="Internal").ap()
    a["q_parts"] = nc.dram_tensor("q_parts", (3, 128, T), BF16, kind="Internal").ap()
    build(nc, a)
    out = run_bass_kernel_spmd(nc, [arrays], core_ids=[0]).results[0]["out_t"]
    return out.T.reshape(B, L, D)
```

```python
from contextlib import ExitStack

import numpy as np

import concourse.bass as bass
from concourse import mybir

F32 = mybir.dt.float32
BF16 = mybir.dt.bfloat16
ALU = mybir.AluOpType
ACT = mybir.ActivationFunctionType
X_AXIS = mybir.AxisListType.X

D = 128
B, L = 8, 100
T = B * L
HT = T // 2
S = 1444
NST, DR, NC = 16, 8, 4
KT = 12
KC = [(0, 512), (512, 512), (1024, 420)]
KLAST = S - 128 * (KT - 1)
EPS = 1e-5
TWO_ONES = float(np.array([0x3F803F80], np.uint32).view(np.float32)[0])
STAGE5_HIGH = 25000
TERMS = [(0, 0), (0, 1), (0, 2), (1, 0), (1, 1), (2, 0)]


def build(nc, a):
    with ExitStack() as ctx:
        def sb(name, shape, dt=F32):
            return ctx.enter_context(nc.sbuf_tensor(name, shape, dt))

        def sem(name):
            return ctx.enter_context(nc.semaphore(name))

        X_ = [sb("x_even", [128, T]), sb("x_odd", [128, T])]
        X = [x[:, :] for x in X_]
        Z = sb("residual", [128, T])[:, :]
        NORMED = sb("normed", [128, T])[:, :]
        SQ = sb("square_then_rstd", [128, T])[:, :]
        CT = [sb("ctxT0", [128, S]), sb("ctxT1", [128, S])]

        packs, wts = {}, {}

        def unpack(group, pack):
            packs[group], at = pack, 0
            for name, (g, shape) in W_RESIDENT.items():
                if g == group:
                    n = int(np.prod(shape[1:]))
                    v = pack[:, at:at + n]
                    if len(shape) == 3:
                        v = v.rearrange("p (i n) -> p i n", i=shape[1])
                    if len(shape) == 4:
                        v = v.rearrange("p (i j n) -> p i j n", i=shape[1], j=shape[2])
                    wts[name] = v
                    at += n
        for group in ("mamba", "l0x", "late"):
            unpack(group, sb("weights_" + group, [128, WIDTH[group]])[:, :])
        ARENA_W = 39600
        arena = sb("arena", [128, ARENA_W])
        PS = ctx.enter_context(nc.psum_tensor("ps", [128, 8, 512], F32))

        def carve(at):
            pos = [at]

            def f32(n):
                pos[0] += n
                assert pos[0] <= ARENA_W, pos[0]
                return arena[:, pos[0] - n:pos[0]]

            def b16(n):
                return f32((n + 1) // 2).bitcast(BF16)
            return f32, b16

        def two(v):
            return v.rearrange("p (j n) -> p j n", j=2)

        def half(v, j):
            return v[:, j * HT:(j + 1) * HT]

        ld = {g: sem("ld_" + g) for g in LOADS}
        z_ready, cent_ready, sq_ready = sem("z_ready"), sem("cent_ready"), sem("sq_ready")
        var_ready, ln_ready, rstd_ready, x_ready = sem("var_ready"), sem("ln_ready"), sem("rstd_ready"), sem("x_ready")
        op_done = sem("op_done")
        out_stored = sem("out_stored")
        ctx_ld = [sem("ctx_loaded0"), sem("ctx_loaded1")]

        def pe_ln(n, src, ready, count):
            for j in range(2):
                nc.tensor.wait_ge(ready, count + j + 1)
                nc.tensor.matmul(PS[:, j, 0:HT], wts["centring"], half(src, j), start=True, stop=True).then_inc(cent_ready, 1)
            for j in range(2):
                nc.tensor.wait_ge(sq_ready, 2 * (n - 1) + j + 1)
                nc.tensor.matmul(PS[:, 2 + j, 0:HT], wts["ones_d"], half(SQ, j), start=True, stop=True).then_inc(var_ready, 1)

        def dve_ln(n, dst, ready):
            for j in range(2):
                nc.vector.wait_ge(rstd_ready, 2 * (n - 1) + j + 1)
                nc.vector.tensor_tensor(half(dst, j), PS[:, j, 0:HT], half(SQ, j), ALU.mult).then_inc(ready, 1)

        def act_ln(k):
            for j in range(2):
                nc.scalar.wait_ge(cent_ready, 2 * (k - 1) + j + 1)
                nc.scalar.activation(half(SQ, j), PS[:, j, 0:HT], ACT.Square).then_inc(sq_ready, 1)
            for j in range(2):
                nc.scalar.wait_ge(var_ready, 2 * (k - 1) + j + 1)
                nc.scalar.activation(half(SQ, j), PS[:, 2 + j, 0:HT], ACT.Ln, bias=wts["eps"][:, 0:1]).then_inc(ln_ready, 1)
                nc.scalar.wait_ge(ln_ready, 2 * (k - 1) + j + 1)
                nc.scalar.activation(half(SQ, j), half(SQ, j), ACT.Exp, scale=-0.5).then_inc(rstd_ready, 1)

        def dve_residual(k, bias):
            for j in range(2):
                nc.vector.wait_ge(op_done, 2 * (k - 1) + j + 1)
                if bias is None:
                    ins = nc.vector.tensor_tensor(half(Z, j), PS[:, 4 + j, 0:HT], half(X[(k - 1) % 2], j), ALU.add)
                else:
                    ins = nc.vector.scalar_tensor_tensor(out=half(Z, j), in0=PS[:, 4 + j, 0:HT], scalar=bias,
                                                         in1=half(X[(k - 1) % 2], j), op0=ALU.add, op1=ALU.add)
                ins.then_inc(z_ready, 1)

        def pe_x(k):
            nc.tensor.wait_ge(x_ready, 2 * k)

        f32, b16 = carve(0)
        PADW = L + 2 * (NC - 1)
        XP = [f32(B * PADW).rearrange("p (b l) -> p b l", b=B) for _ in range(2)]
        SZ = [f32(T) for _ in range(2)]
        CACC = [[f32(T) for _ in range(2)] for _ in range(2)]
        U = [[f32(T) for _ in range(2)] for _ in range(2)]
        DT = [[f32(T) for _ in range(2)] for _ in range(2)]
        DTU = [[f32(T) for _ in range(2)] for _ in range(2)]
        DEC = [[f32(T) for _ in range(2)] for _ in range(2)]
        WIN = [[f32(T) for _ in range(2)] for _ in range(2)]
        TAPS = [WIN[0][0], WIN[0][1], WIN[1][0]]
        BSB = [f32(T) for _ in range(2)]
        H = [f32(T) for _ in range(2)]
        G = [f32(T) for _ in range(2)]
        BC = [b16(T) for _ in range(2)]
        R1 = f32(T)
        DTR = [f32(T) for _ in range(2)]
        SEL = b16(2 * NST * 128).rearrange("p (n m) -> p n m", n=2 * NST)
        ANEG = f32(2 * 2 * NST)
        DIAG = [[f32(128) for _ in range(2)] for _ in range(2)]
        YZ = [f32(T) for _ in range(2)]
        for group in ("first", "arena"):
            unpack(group, f32(WIDTH[group]))

        inproj, xp_ready, pads, sz_ready = sem("inproj"), sem("xp_ready"), sem("pads_zero"), sem("sz_ready")
        tap0, conv_dve, u_ready = sem("tap0"), sem("conv_dve"), sem("u_ready")
        tap_products, conv_pool = sem("tap_products"), sem("conv_pool")
        xproj, bc_hi, bc_r1, bc_mid, bc_ready, dtr_ready = sem("xproj"), sem("bc_hi"), sem("bc_r1"), sem("bc_mid"), sem("bc_ready"), sem("dtr_ready")
        dtproj, sp_act, relu_ready, dt_ready, dtu_ready = sem("dtproj"), sem("sp_act"), sem("relu_ready"), sem("dt_ready"), sem("dtu_ready")
        sel_ready, aexp, aneg, diag_ready = sem("sel_ready"), sem("aexp"), sem("aneg"), sem("diag_ready")
        dec_zeroed, b_copied = sem("dec_zeroed"), sem("b_copied")
        dec_ready, win_ready, scanned, g_ready = sem("dec_ready"), sem("win_ready"), sem("scanned"), sem("g_ready")
        b_ready, c_ready, y_added, yz_ready = sem("b_bcast"), sem("c_bcast"), sem("y_added"), sem("yz_ready")

        def pe_mamba():
            nc.tensor.wait_ge(ld["first"], 32)
            for e in range(4):
                for j in range(2):
                    m = nc.tensor.matmul(PS[:, 2 * e + j, 0:HT], wts["w_in"][:, e * 128:(e + 1) * 128], half(X[0], j), start=True, stop=True)
                m.then_inc(inproj, 1)
            nc.tensor.wait_ge(ld["mamba"], 16)
            nc.tensor.wait_ge(ld["arena"], 16)
            for d in range(2):
                if d == 0:
                    nc.tensor.wait_ge(xp_ready, 2)
                nc.tensor.wait_ge(u_ready, 2 * d + 2)
                for j in range(2):
                    for h in range(2):
                        m = nc.tensor.matmul(PS[:, 2 * d + j, 0:HT], wts["w_xp"][:, d, h, :], half(U[d][h], j), start=(h == 0), stop=(h == 1))
                m.then_inc(xproj, 1)
            nc.tensor.wait_ge(sz_ready, 2)
            for d in range(2):
                nc.tensor.wait_ge(dtr_ready, d + 1)
                for h in range(2):
                    if d == 1:
                        nc.tensor.wait_ge(relu_ready, h + 1)
                    for j in range(2):
                        m = nc.tensor.matmul(PS[:, 4 + 2 * h + j, 0:HT], wts["w_dt"][32:32 + DR, d, h * 128:(h + 1) * 128],
                                             DTR[d][32:32 + DR, j * HT:(j + 1) * HT], start=True, stop=True)
                    m.then_inc(dtproj, 1)
            nc.tensor.wait_ge(sel_ready, 1)

            def bcast(bank, which, d, done):
                for j in range(2):
                    m = nc.tensor.matmul(PS[:, bank + j, 0:HT], which, BC[d][:, j * HT:(j + 1) * HT], start=True, stop=True)
                m.then_inc(done, 1)

            def sel(n, c):
                return SEL_FLAT[:, bass.ds(n * 128 + c * NST * 128, 128)] if not isinstance(n, int) else SEL[:, n + c * NST, :]

            def add_y(m_, h, last):
                nc.tensor.wait_ge(g_ready, 2 * m_ + h + 3)
                for j in range(2):
                    m = nc.tensor.matmul(PS[:, 4 + 2 * h + j, 0:HT], wts["ident"][:, :], half(G[h], j), start=False, stop=last, skip_group_check=True)
                m.then_inc(y_added, 1)

            nc.tensor.wait_ge(bc_ready, 2)
            bcast(0, sel(0, 0), 0, b_ready)
            bcast(2, sel(0, 1), 0, c_ready)
            nc.tensor.wait_ge(b_copied, 1)
            bcast(0, sel(1, 0), 0, b_ready)
            nc.tensor.wait_ge(diag_ready, 4)
            for h in range(2):
                nc.tensor.wait_ge(relu_ready, 2 + h + 1)
                for d in range(2):
                    for j in range(2):
                        m = nc.tensor.matmul(PS[:, 4 + 2 * h + j, 0:HT], DIAG[d][h], half(U[d][h], j), start=(d == 0), stop=False, skip_group_check=True)
                m.then_inc(y_added, 1)
            nc.tensor.wait_ge(b_copied, 2)
            bcast(0, sel(2, 0), 0, b_ready)

            def state(n, d, ahead, after):
                m_ = n + d * NST
                if ahead:
                    nc.tensor.wait_ge(b_copied, m_ + 3)
                    bcast(0, sel(ahead[0], 0), ahead[1], b_ready)
                last = after is None
                add_y(m_, 0, last)
                if after:
                    nc.tensor.wait_ge(g_ready, 2 * m_ + 4)
                    bcast(2, sel(after[0], 1), after[1], c_ready)
                add_y(m_, 1, last)
            for d in range(2):
                with nc.tensor.Fori(0, NST - 3) as n:
                    state(n, d, (n + 3, d), (n + 1, d))
                for k in range(3):
                    n = NST - 3 + k
                    state(n, d, None if d else (k, 1), (n + 1, d) if k < 2 else None if d else (0, 1))
            nc.tensor.wait_ge(yz_ready, 2)
            for j in range(2):
                for h in range(2):
                    m = nc.tensor.matmul(PS[:, 4 + j, 0:HT], wts["w_out"][:, h, :], half(YZ[h], j), start=(h == 0), stop=(h == 1))
                m.then_inc(op_done, 1)

        SEL_FLAT = SEL.rearrange("p n m -> p (n m)")

        def interior(h):
            return XP[h][:, :, NC - 1:NC - 1 + L]

        def tap(d, h, k):
            at = k if d == 0 else 2 * (NC - 1) - k
            return XP[h][:, :, at:at + L]

        def by_batch(v):
            return v.rearrange("p (b l) -> p b l", b=B)

        def act_mamba():
            nc.scalar.wait_ge(ld["mamba"], 16)
            for h in range(2):
                nc.scalar.wait_ge(inproj, h + 1)
                nc.scalar.wait_ge(pads, 2)
                for j in range(2):
                    i = nc.scalar.activation(interior(h)[:, 4 * j:4 * j + 4, :], PS[:, 2 * h + j, 0:HT].rearrange("p (b l) -> p b l", b=4), ACT.Copy)
                i.then_inc(xp_ready, 1)
            for h in range(2):
                nc.scalar.wait_ge(inproj, 2 + h + 1)
                nc.scalar.activation(two(SZ[h]), PS[:, 4 + 2 * h:6 + 2 * h, 0:HT], ACT.Silu).then_inc(sz_ready, 1)
            nc.scalar.wait_ge(xp_ready, 2)
            for d in range(2):
                for h in range(2):
                    nc.scalar.activation(by_batch(CACC[d][h]), tap(d, h, 0), ACT.Identity,
                                         bias=wts["conv_b"][:, 2 * d + h:2 * d + h + 1], scale=wts["conv_w"][:, 4 * (2 * d + h):4 * (2 * d + h) + 1]).then_inc(tap0, 1)
            for k in range(1, NC):
                nc.scalar.activation(by_batch(TAPS[k - 1]), tap(1, 1, k), ACT.Copy, scale=wts["conv_w"][:, 12 + k:13 + k]).then_inc(tap_products, 1)
            for d in range(2):
                for h in range(2):
                    if (d, h) == (1, 1):
                        nc.scalar.wait_ge(conv_pool, NC - 1)
                    else:
                        nc.scalar.wait_ge(conv_dve, (2 * d + h + 1) * (NC - 1))
                    nc.scalar.activation(U[d][h], CACC[d][h], ACT.Silu).then_inc(u_ready, 1)
            nc.scalar.preload_act_table_set("natural_log_exp_and_others")
            nc.scalar.activation(ANEG, wts["a_log"][:, :], ACT.Exp).then_inc(aexp, 1)
            for d in range(2):
                nc.scalar.wait_ge(xproj, d + 1)
                nc.scalar.activation(two(BC[d]), PS[:, 2 * d:2 * d + 2, 0:HT], ACT.Copy).then_inc(bc_hi, 1)
                nc.scalar.activation(two(DTR[d])[32:32 + DR], PS[32:32 + DR, 2 * d:2 * d + 2, 0:HT], ACT.Copy).then_inc(dtr_ready, 1)
            for d in range(2):
                for h in range(2):
                    n = 2 * d + h
                    v = CACC[d][h]
                    nc.scalar.wait_ge(dtproj, n + 1)
                    nc.scalar.activation(two(v), PS[:, 4 + 2 * h:6 + 2 * h, 0:HT], ACT.Abs, bias=wts["dt_b"][:, n:n + 1]).then_inc(sp_act, 1)
                    nc.scalar.wait_ge(sp_act, 3 * n + 1)
                    nc.scalar.activation(v, v, ACT.Exp, scale=-1.0).then_inc(sp_act, 1)
                    nc.scalar.wait_ge(sp_act, 3 * n + 2)
                    nc.scalar.activation(v, v, ACT.Ln, bias=wts["one"][:, 0:1]).then_inc(sp_act, 1)
            nc.scalar.wait_ge(aneg, 1)

            def copy_b(m_, k):
                nc.scalar.wait_ge(b_ready, m_ + 1)
                if not isinstance(m_, int) or m_ > 1:
                    nc.scalar.wait_ge(win_ready, 2 * m_ - 2)
                nc.scalar.activation(two(BSB[k]), PS[:, 0:2, 0:HT], ACT.Copy).then_inc(b_copied, 1)

            def decay(n, d, k, copy):
                m_ = n + d * NST
                cols = (1, L) if d == 0 else (0, L - 1)
                for h in range(2):
                    nc.scalar.wait_ge(scanned, 2 * m_ + h + 3)
                    nc.scalar.activation(by_batch(DEC[d][h])[:, :, cols[0]:cols[1]], by_batch(DT[d][h])[:, :, cols[0]:cols[1]], ACT.Exp,
                                         scale=ANEG[:, bass.ds(n + (2 * d + h) * NST, 1)]).then_inc(dec_ready, 1)
                if copy:
                    copy_b(m_ + 2, k)
            for k in range(2):
                copy_b(k, k)
            nc.scalar.wait_ge(dec_zeroed, 4)
            for d in range(2):
                nc.scalar.wait_ge(dt_ready, 2 * d + 2)
                with nc.scalar.Fori(0, NST // 2 - d) as pair:
                    for k in range(2):
                        decay(pair * 2 + k, d, k, True)
            for k in range(2):
                decay(NST - 2 + k, 1, k, False)

        def pool_mamba():
            nc.gpsimd.wait_ge(tap0, 4)
            for k in range(1, NC):
                nc.gpsimd.wait_ge(tap_products, k)
                if k > 1:
                    nc.gpsimd.wait_ge(conv_pool, k - 1)
                nc.gpsimd.tensor_tensor(CACC[1][1], CACC[1][1], TAPS[k - 1], ALU.add).then_inc(conv_pool, 1)
            nc.gpsimd.tensor_copy(SEL, wts["sel32"][:, :].unsqueeze(2).broadcast_to([128, 2 * NST, 128])).then_inc(sel_ready, 1)
            for d in range(2):
                nc.gpsimd.wait_ge(dtu_ready, 2 * d + 2)
                with nc.gpsimd.Fori(0, NST // 2) as pair:
                    for k in range(2):
                        m_ = pair * 2 + (k + d * NST)
                        nc.gpsimd.wait_ge(b_copied, m_ + 1)
                        for h in range(2):
                            nc.gpsimd.wait_ge(scanned, 2 * m_ + h + 1)
                            nc.gpsimd.tensor_tensor(WIN[k][h], DTU[d][h], BSB[k], ALU.mult).then_inc(win_ready, 1)

        def dve_mamba():
            for h in range(2):
                nc.vector.memset(XP[h], 0.0).then_inc(pads, 1)
            for d in range(2):
                for h in range(2):
                    nc.vector.memset(by_batch(DEC[d][h])[:, :, (0 if d == 0 else L - 1):(1 if d == 0 else L)], 0.0).then_inc(dec_zeroed, 1)
            nc.vector.wait_ge(ld["mamba"], 16)
            for d in range(2):
                for h in range(2):
                    nc.vector.tensor_scalar(DIAG[d][h], wts["ident"][:, :], wts["d_skip"][:, 2 * d + h:2 * d + h + 1], None, ALU.mult).then_inc(diag_ready, 1)
            for d in range(2):
                for h in range(2 - d):
                    n = 2 * d + h
                    nc.vector.wait_ge(tap0, n + 1)
                    for k in range(1, NC):
                        if k > 1:
                            nc.vector.wait_ge(conv_dve, (NC - 1) * n + k - 1)
                        c = by_batch(CACC[d][h])
                        nc.vector.scalar_tensor_tensor(out=c, in0=tap(d, h, k), scalar=wts["conv_w"][:, 4 * n + k:4 * n + k + 1],
                                                       in1=c, op0=ALU.mult, op1=ALU.add).then_inc(conv_dve, 1)
            nc.vector.wait_ge(aexp, 1)
            nc.vector.tensor_scalar(ANEG, ANEG, -1.0, None, ALU.mult).then_inc(aneg, 1)
            for d in range(2):
                nc.vector.wait_ge(bc_hi, d + 1)
                nc.vector.wait_ge(dtr_ready, d + 1)
                if d == 1:
                    nc.vector.wait_ge(bc_ready, 1)
                nc.vector.tensor_tensor(two(R1)[64:128], PS[64:128, 2 * d:2 * d + 2, 0:HT], two(BC[d])[64:128], ALU.subtract).then_inc(bc_r1, 1)
                nc.vector.wait_ge(bc_r1, d + 1)
                nc.vector.tensor_copy(BC[d][64:128], R1[64:128]).then_inc(bc_mid, 1)
                nc.vector.wait_ge(bc_mid, d + 1)
                nc.vector.tensor_tensor(BC[d][96:128], R1[96:128], BC[d][96:128], ALU.subtract).then_inc(bc_ready, 1)
            for d in range(2):
                for h in range(2):
                    n = 2 * d + h
                    nc.vector.wait_ge(sp_act, 3 * n + 1)
                    nc.vector.tensor_scalar(two(DT[d][h]), PS[:, 4 + 2 * h:6 + 2 * h, 0:HT], wts["dt_b"][:, n:n + 1], 0.0, ALU.add, ALU.max).then_inc(relu_ready, 1)
                    nc.vector.wait_ge(sp_act, 3 * n + 3)
                    nc.vector.wait_ge(relu_ready, n + 1)
                    nc.vector.tensor_tensor(DT[d][h], DT[d][h], CACC[d][h], ALU.add).then_inc(dt_ready, 1)
                    nc.vector.wait_ge(dt_ready, n + 1)
                    nc.vector.tensor_tensor(DTU[d][h], DT[d][h], U[d][h], ALU.mult).then_inc(dtu_ready, 1)
            for d in range(2):
                with nc.vector.Fori(0, NST // 2) as pair:
                    for k in range(2):
                        m_ = pair * 2 + (k + d * NST)
                        for h in range(2):
                            nc.vector.wait_ge(dec_ready, 2 * m_ + h + 1)
                            nc.vector.wait_ge(win_ready, 2 * m_ + h + 1)
                            nc.vector.wait_ge(g_ready, 2 * m_ + h + 1)
                            if d == 0:
                                i = nc.vector.tensor_tensor_scan(H[h], DEC[d][h], WIN[k][h], 0.0, ALU.mult, ALU.add)
                            else:
                                i = nc.vector.tensor_tensor_scan(H[h][:, ::-1], DEC[d][h][:, ::-1], WIN[k][h][:, ::-1], 0.0, ALU.mult, ALU.add)
                            i.then_inc(scanned, 1)
                        nc.vector.wait_ge(c_ready, m_ + 1)
                        for h in range(2):
                            nc.vector.wait_ge(y_added, 2 * m_ + h + 1)
                            nc.vector.wait_ge(scanned, 2 * m_ + h + 5)
                            nc.vector.tensor_tensor(two(G[h]), two(H[h]), PS[:, 2:4, 0:HT], ALU.mult).then_inc(g_ready, 1)
            nc.vector.wait_ge(y_added, 2 + 4 * NST)
            nc.vector.wait_ge(sz_ready, 2)
            for h in range(2):
                nc.vector.tensor_tensor(two(YZ[h]), two(SZ[h]), PS[:, 4 + 2 * h:6 + 2 * h, 0:HT], ALU.mult).then_inc(yz_ready, 1)
            dve_residual(1, None)

        f32, b16 = carve(0)
        KST = [b16(8 * S).rearrange("p (g n) -> p g n", g=8) for _ in range(2)]
        VA = [f32(KT * 256).rearrange("p (t g n) -> p t g n", t=KT, g=8) for _ in range(2)]
        PT = [f32(16 * L) for _ in range(2)]
        K32, KR = f32(S), f32(S)
        KPARTS = b16(4 * S).rearrange("p (i n) -> p i n", i=4)
        KH, KP = [KPARTS[:, 0, :], KPARTS[:, 3, :]], [None, KPARTS[:, 1, :], KPARTS[:, 2, :]]
        QM = [b16(16 * L) for _ in range(2)]
        QS = [b16(16 * L) for _ in range(2)]
        ONE_ROW = b16(S)
        Q32, QR = f32(T), f32(T)
        QP = [b16(T) for _ in range(3)]
        ACC0 = f32(4 * T).rearrange("p (i n) -> p i n", i=4)
        spare = ACC0.rearrange("p i n -> p (i n)")
        RUN = [spare[:, g * 768:(g + 1) * 768].rearrange("p (c n) -> p c n", c=3) for g in range(2)]
        HALVES = [spare[:, 1536 + u * 256:1792 + u * 256] for u in range(4)]
        AS, RD = f32(HT), f32(HT)
        TILES = -(-16 * L // 128)
        TLAST = 16 * L - 128 * (TILES - 1)
        MX, MXC = f32(TILES * 3).rearrange("p (t c) -> p t c", c=3), f32(TILES)
        MB = b16(128)
        DH0 = 8.0 ** -0.5
        QDMA = 16 * 2 * len(TERMS)
        UNITS = 4 * KT
        MAXU = 3 * TILES
        JOBS = {2: dict(V0=(0, 0), V1=(1, 0), V2=(0, 1), K0=(1, 1), K1=(0, 2), M=(1, 2), K2=(1, 3), D=(0, 3)),
                1: dict(V0=(0, 0), V1=(1, 0), V2=(0, 1), M=(1, 1), D=(0, 2)),
                0: dict(D=(1, -2))}
        PRO = 5
        V_AT, K_AT, M_AT, MAX_KT = (0, 1, 2), (3, 5, 11), 10, 10

        q_mm, q_cut, q_hi, qp_st, qs_zero = sem("q_mm"), sem("q_cut"), sem("q_hi"), sem("q_parts_stored"), sem("stack_zero")
        qs_ld, mrow_ld = sem("qs_loaded"), sem("mrow_loaded")
        qm_ready, ones_ld = sem("qm_ready"), sem("ones_loaded")
        kp_st = sem("kp_stored")
        kst_ld = [sem("kst_loaded0"), sem("kst_loaded1")]
        k_high, qs1_zero, one_row, mx_zero = sem("k_high"), sem("qs1_zero"), sem("one_row"), sem("mx_zero")
        k_mm, k_cut, v_mm, va_init = sem("k_mm"), sem("k_cut"), sem("v_mm"), sem("va_init")
        half_ready, mx_copied = sem("half_ready"), sem("mx_copied")
        job_free = [sem("job_free0"), sem("job_free1")]
        unit_done, exp_done, pt_free, acc_free = sem("unit_done"), sem("exp_done"), sem("pt_free"), sem("acc_free")
        mx_mm, mx_read, mxc_ready, mt_mm = sem("mx_mm"), sem("mx_read"), sem("mxc_ready"), sem("mt_mm")
        den_mm, rd_ready, accn_ready = sem("den_mm"), sem("rd_ready"), sem("accn_ready")

        def job(name, b, more):
            bank, turn = JOBS[more][name]
            return bank, b * 4 + (PRO + 1 + turn)

        def turn(n):
            return n % 2, n // 2 + 1

        def rows(kt):
            return 128 if kt < KT - 1 else KLAST

        def max_units(kt, g):
            return 1 if 4 * kt + g < MAXU and kt < MAX_KT else 0

        def steps(engine, body):
            with engine.Fori(0, B // 2 - 1) as pair:
                for u in range(2):
                    body(pair * 2 + u, u, 2)
            body(B - 2, 0, 1)
            body(B - 1, 1, 0)

        def waits(engine, *pairs):
            for _, n in pairs:
                if not isinstance(n, int):
                    engine.lower_val(n)
            for semaphore, n in pairs:
                engine.wait_ge(semaphore, n)

        def own_register(engine, value):
            if isinstance(value, int):
                return value
            r = engine.alloc_register(f"own_{nc.next_id()}")
            engine.reg_mov(r, value)
            return engine.snap(r)

        def loads_until(b, u, n):
            return (b - u) * (n // 2) + n

        def pe_k(c, u, bank, free):
            at, n = KC[c]
            nc.tensor.wait_ge(job_free[bank], free)
            nc.tensor.matmul(PS[:, 6 + bank, 0:n], wts["l0_wk"][:, :], CT[u][:, at:at + n], start=True, stop=True).then_inc(k_mm, 1)

        def pe_v(c, u, bank, free):
            nc.tensor.wait_ge(job_free[bank], free)
            for i in range(4):
                n = rows(4 * c + i)
                at = (4 * c + i) * 128
                m = nc.tensor.matmul(PS[0:n, 6 + bank, i * 128:i * 128 + 128], CT[u][:, at:at + n], wts["l0_wv"][:, :], start=True, stop=True)
            m.then_inc(v_mm, 1)

        FIRST_BANKS = (3, 4, 0, 1, 2)

        def pe_first_maxima(unit, read):
            if unit >= 5:
                nc.tensor.wait_ge(read, unit - 2)

        def pe_max(unit, u, b, first=False):
            t, c = unit // 3, unit % 3
            at, n = KC[c]
            m = 128 if t < TILES - 1 else TLAST
            if unit < 3:
                nc.tensor.wait_ge(k_high, b * 3 + c + 1)
            if unit == 0:
                nc.tensor.wait_ge(qm_ready, b + 1)
            if first:
                pe_first_maxima(unit, mx_read)
            else:
                nc.tensor.wait_ge(mx_read, b * MAXU + unit + 1)
            bank = FIRST_BANKS[unit % 5] if first else 3 + unit % 2
            nc.tensor.matmul(PS[0:m, bank, 0:n], QM[u][:, t * 128:t * 128 + m], KH[u][:, at:at + n], start=True, stop=True).then_inc(mx_mm, 1)

        def pe_mt(b, bank, free):
            nc.tensor.wait_ge(mxc_ready, b + 1)
            nc.tensor.wait_ge(job_free[bank], free)
            nc.tensor.transpose(PS[0:TILES, 6 + bank, 0:128], MXC, wts["ident"][:, :]).then_inc(mt_mm, 1)

        def pe_xattn0():
            pe_x(1)
            nc.tensor.wait_ge(ld["l0x"], 16)
            for j in range(2):
                nc.tensor.matmul(PS[:, 4 + j, 0:HT], wts["l0_wq"][:, :], half(X[1], j), start=True, stop=True).then_inc(q_mm, 1)
            nc.tensor.wait_ge(ctx_ld[0], 16)
            for c in range(3):
                pe_k(c, 0, *turn(c))
            nc.tensor.wait_ge(q_cut, 2)
            for unit in range(MAXU):
                pe_max(unit, 0, 0, True)
            pe_mt(0, *turn(3))
            for c in range(3):
                pe_v(c, 0, *turn(4 + c))
            nc.tensor.wait_ge(ctx_ld[1], 16)
            for c in range(3):
                pe_k(c, 1, *turn(7 + c))
            nc.tensor.wait_ge(ones_ld, 32)

            def pv(b, u, kt, r):
                if kt == 0 and r == 0:
                    nc.tensor.wait_ge(acc_free, b + 1)
                nc.tensor.wait_ge(exp_done, b * UNITS + (4 * kt + 2 * r + 2 + 3))
                for j in range(4):
                    p = 4 * r + j
                    m = nc.tensor.matmul(PS[32 * j:32 * j + 32, 5, 2 * L * r:2 * L * (r + 1)], VA[u][:, kt, p, :], PT[kt % 2][:, p * 2 * L:(p + 1) * 2 * L],
                                         start=(kt == 0 and r == 0), stop=(kt == KT - 1), skip_group_check=True)
                if r == 1:
                    m.then_inc(pt_free, 1)

            def body(b, u, more):
                nxt = 0
                following = own_register(nc.tensor, b + 1)
                nc.tensor.wait_ge(kst_ld[u], loads_until(b, u, 96))
                nc.tensor.wait_ge(qs_ld, b * QDMA + QDMA)
                nc.tensor.wait_ge(mrow_ld, b * 32 + 32)
                for kt in range(KT):
                    n = rows(kt)
                    for g in range(4):
                        unit = 4 * kt + g
                        nc.tensor.wait_ge(exp_done, b * UNITS + unit + 1)
                        for i in range(2):
                            p = 2 * g + i
                            m = nc.tensor.matmul(PS[0:n, unit % 3, i * 2 * L:(i + 1) * 2 * L], KST[u][0:97, p, kt * 128:kt * 128 + n], QS[u][0:97, p * 2 * L:(p + 1) * 2 * L],
                                                 start=(i == 0), stop=True, skip_group_check=True)
                        m.then_inc(unit_done, 1)
                        if more:
                            for _ in range(max_units(kt, g)):
                                pe_max(nxt, 1 - u, following)
                                nxt += 1
                        if kt > 0 and g % 2 == 1:
                            pv(b, u, kt - 1, g // 2)
                    if more and kt in V_AT:
                        pe_v(V_AT.index(kt), 1 - u, *job(f"V{V_AT.index(kt)}", b, more))
                    if more == 2 and kt in K_AT[0:2]:
                        if kt == K_AT[0]:
                            nc.tensor.wait_ge(ctx_ld[u], ctx_count(b, u) + 16)
                        pe_k(K_AT.index(kt), u, *job(f"K{K_AT.index(kt)}", b, more))
                    if more and kt == M_AT:
                        pe_mt(b + 1, *job("M", b, more))
                for r in range(2):
                    pv(b, u, KT - 1, r)
                if more == 2:
                    pe_k(2, u, *job("K2", b, more))
                bank, free = job("D", b, more)
                nc.tensor.wait_ge(acc_free, b + 2)
                nc.tensor.wait_ge(job_free[bank], free)
                nc.tensor.matmul(PS[:, 6 + bank, 0:HT], wts["seld"][:, :], AS, start=True, stop=True).then_inc(den_mm, 1)
            steps(nc.tensor, body)
            pe_out(ACC0, wts["l0_wo"], accn_ready, B + 1, 4)

        def ctx_count(b, u):
            return loads_until(b, u, 16)

        def pe_out(acc, w, ready, count, n):
            nc.tensor.wait_ge(ready, count)
            for j in range(2):
                for i in range(n):
                    m = nc.tensor.matmul(PS[:, 4 + j, 0:HT], w[:, i, :], acc[:, i, j * HT:(j + 1) * HT], start=(i == 0), stop=(i == n - 1))
                m.then_inc(op_done, 1)

        def act_kev(c, kb, u, bank, free):
            at, n = KC[c]
            nc.scalar.wait_ge(k_mm, kb * 3 + c + 1)
            if not isinstance(kb, int) or kb > 0:
                nc.scalar.wait_ge(kp_st, kb * 16)
                nc.scalar.wait_ge(k_cut, kb * 9 - 9 + 3 * c + 3)
            nc.scalar.activation(KH[u][:, at:at + n], PS[:, 6 + bank, 0:n], ACT.Identity, bias=wts["l0_bk"][:, 0:1]).then_inc(k_high, 1)
            nc.scalar.activation(K32[:, at:at + n], PS[:, 6 + bank, 0:n], ACT.Identity, bias=wts["l0_bk"][:, 0:1]).then_inc(job_free[bank], 1)

        def act_xattn0():
            for j in range(2):
                nc.scalar.wait_ge(q_cut, j + 1)
                nc.scalar.activation(half(QP[0], j), half(Q32, j), ACT.Copy).then_inc(q_hi, 1)
            for c in range(3):
                act_kev(c, 0, 0, *turn(c))
            for unit in range(MAXU):
                act_half(unit, FIRST_BANKS[unit % 5], tile_rows(unit), KC[unit % 3][1], mx_mm, mx_read, HALVES, half_ready)
            nc.scalar.wait_ge(mt_mm, 1)
            nc.scalar.activation(MB[0:TILES, :], PS[0:TILES, 7, 0:128], ACT.Copy).then_inc(job_free[1], 1)
            for c in range(3):
                act_kev(c, 1, 1, *turn(7 + c))

            def body(b, u, more):
                for kt in range(KT):
                    n = rows(kt)
                    nc.scalar.wait_ge(pt_free, b * KT + kt + 1)
                    for g in range(4):
                        unit = 4 * kt + g
                        nc.scalar.wait_ge(unit_done, b * UNITS + unit + 1)
                        nc.scalar.activation(PT[kt % 2][0:n, g * HT:(g + 1) * HT], PS[0:n, unit % 3, 0:HT], ACT.Exp).then_inc(exp_done, 1)
                    if more == 2 and kt == 0:
                        load_ctx(nc.scalar, b + 2, u)
                    if more == 2 and kt in K_AT:
                        act_kev(K_AT.index(kt), b + 2, u, *job(f"K{K_AT.index(kt)}", b, more))
                    if more and kt == M_AT:
                        bank, free = job("M", b, more)
                        nc.scalar.wait_ge(mt_mm, b + 2)
                        nc.scalar.wait_ge(mrow_ld, b * 32 + 32)
                        nc.scalar.activation(MB[0:TILES, :], PS[0:TILES, 6 + bank, 0:128], ACT.Copy).then_inc(job_free[bank], 1)
                bank, free = job("D", b, more)
                nc.scalar.wait_ge(den_mm, b + 1)
                nc.scalar.wait_ge(accn_ready, b + 1)
                nc.scalar.activation(RD, PS[:, 6 + bank, 0:HT], ACT.Ln).then_inc(job_free[bank], 1)
                nc.scalar.wait_ge(job_free[bank], free + 1)
                nc.scalar.activation(RD, RD, ACT.Exp, scale=-1.0).then_inc(rd_ready, 1)
            steps(nc.scalar, body)

        def pool_kcut(c, kb, u, bank, free):
            at, n = KC[c]
            sl = slice(at, at + n)
            nc.gpsimd.wait_ge(k_high, kb * 3 + c + 1)
            nc.gpsimd.wait_ge(job_free[bank], free + 1)
            if not isinstance(kb, int) or kb > 0:
                nc.gpsimd.wait_ge(kp_st, kb * 16)
                nc.gpsimd.wait_ge(k_cut, kb * 9 - 9 + 3 * c + 3)
            nc.gpsimd.tensor_tensor(KR[:, sl], K32[:, sl], KH[u][:, sl], ALU.subtract).then_inc(k_cut, 1)
            nc.gpsimd.tensor_tensor(KP[1][:, sl], K32[:, sl], KH[u][:, sl], ALU.subtract).then_inc(k_cut, 1)
            nc.gpsimd.wait_ge(k_cut, kb * 9 + 3 * c + 2)
            nc.gpsimd.tensor_tensor(KP[2][:, sl], KR[:, sl], KP[1][:, sl], ALU.subtract).then_inc(k_cut, 1)

        def pool_xattn0():
            def block_queries(b, u):
                nc.gpsimd.tensor_tensor(QM[u].rearrange("p (h n) -> p h n", h=16), QP[0][:, bass.ds(b * L, L)].unsqueeze(1).broadcast_to([128, 16, L]),
                                        wts["of_head"][:, :].unsqueeze(2).broadcast_to([128, 16, L]), ALU.mult).then_inc(qm_ready, 1)
            nc.gpsimd.wait_ge(q_hi, 2)
            block_queries(0, 0)
            for c in range(3):
                pool_kcut(c, 0, 0, *turn(c))
            nc.gpsimd.memset(QS[1][0:96, :].bitcast(F32), 0.0).then_inc(qs1_zero, 1)
            for u in range(2):
                nc.gpsimd.memset(VA[u][:, :, :, 16:32], 0.0).then_inc(va_init, 1)
                nc.gpsimd.memset(VA[u][:, KT - 1, :, 0:16], 0.0).then_inc(va_init, 1)
            block_queries(1, 1)
            nc.gpsimd.wait_ge(va_init, 4)
            for u in range(2):
                nc.gpsimd.memset(VA[u][:, 0:KT - 1, :, 16:17], 1.0).then_inc(va_init, 1)
                nc.gpsimd.memset(VA[u][0:KLAST, KT - 1, :, 16:17], 1.0).then_inc(va_init, 1)
            for c in range(3):
                pool_kcut(c, 1, 1, *turn(7 + c))

            def body(b, u, more):
                if more == 2:
                    nc.gpsimd.wait_ge(mx_mm, b * MAXU + MAXU)
                    block_queries(b + 2, u)
                    for c in range(3):
                        pool_kcut(c, b + 2, u, *job(f"K{c}", b, more))
                nc.gpsimd.wait_ge(rd_ready, b + 1)
                nc.gpsimd.tensor_tensor(ACC0[:, :, bass.ds(b * L, L)], AS.rearrange("p (i n) -> p i n", i=4), RD.rearrange("p (i n) -> p i n", i=4), ALU.mult).then_inc(accn_ready, 1)
            steps(nc.gpsimd, body)

        def dve_vev(c, u, b, bank):
            nc.vector.wait_ge(v_mm, b * 3 + c + 1)
            bias = wts["l0_bv"][:, :].rearrange("p (g n) -> p g n", g=8)
            full = 4 if c < 2 else 3
            m = nc.vector.tensor_tensor(VA[u][:, 4 * c:4 * c + full, :, 0:16], PS[:, 6 + bank, 0:full * 128].rearrange("p (t g n) -> p t g n", t=full, g=8),
                                        bias.unsqueeze(1).broadcast_to([128, full, 8, 16]), ALU.add)
            if full < 4:
                m = nc.vector.tensor_tensor(VA[u][0:KLAST, KT - 1, :, 0:16], PS[0:KLAST, 6 + bank, 384:512].rearrange("p (g n) -> p g n", g=8), bias[0:KLAST], ALU.add)
            m.then_inc(job_free[bank], 1)

        def dve_max(unit, b):
            t, c = unit // 3, unit % 3
            m = 128 if t < TILES - 1 else TLAST
            nc.vector.wait_ge(mx_mm, b * MAXU + unit + 1)
            nc.vector.tensor_reduce(MX[0:m, t, c:c + 1], PS[0:m, 3 + unit % 2, 0:KC[c][1]], X_AXIS, ALU.max).then_inc(mx_read, 1)
            if unit == MAXU - 1:
                nc.vector.wait_ge(mx_read, b * MAXU + MAXU + 2)
                if not isinstance(b, int) or b > 0:
                    nc.vector.wait_ge(mt_mm, b)
                nc.vector.tensor_reduce(MXC, MX, X_AXIS, ALU.max, negate=True).then_inc(mxc_ready, 1)

        def act_half(unit, bank, m, n, scored, read, halves, ready):
            nc.scalar.wait_ge(scored, unit + 1)
            if unit >= 4:
                nc.scalar.wait_ge(read, unit - 1)
            nc.scalar.activation(halves[unit % 4][0:m, 0:n // 2], PS[0:m, bank, n // 2:n], ACT.Copy).then_inc(ready, 1)

        def dve_running(unit, bank, m, n, ready, halves, run, read, slot, group, dst, copied):
            g = unit // group
            nc.vector.wait_ge(ready, unit + 1)
            if slot == 0 and g >= 2:
                nc.vector.wait_ge(copied, g - 1)
            nc.vector.tensor_tensor_scan(run[g % 2][0:m, slot, 256 - n // 2:256], PS[0:m, bank, 0:n // 2], halves[unit % 4][0:m, 0:n // 2],
                                         -3.0e38, ALU.max, ALU.max).then_inc(read, 1)
            if slot == group - 1:
                nc.vector.wait_ge(read, unit + 3)
                nc.vector.tensor_copy(dst, run[g % 2][0:m, :, 255]).then_inc(copied, 1)

        def tile_rows(unit):
            return 128 if unit // 3 < TILES - 1 else TLAST

        def dve_xattn0():
            nc.vector.wait_ge(ld["l0x"], 16)
            for j in range(2):
                nc.vector.wait_ge(q_mm, j + 1)
                nc.vector.tensor_scalar(half(Q32, j), PS[:, 4 + j, 0:HT], wts["l0_bq"][:, 0:1], DH0, ALU.add, ALU.mult).then_inc(q_cut, 1)
            nc.vector.wait_ge(q_hi, 2)
            nc.vector.wait_ge(q_cut, 2)
            nc.vector.tensor_tensor(QR, Q32, QP[0], ALU.subtract).then_inc(q_cut, 1)
            nc.vector.wait_ge(q_cut, 3)
            nc.vector.tensor_copy(QP[1], QR).then_inc(q_cut, 1)
            nc.vector.wait_ge(q_cut, 4)
            nc.vector.tensor_tensor(QP[2], QR, QP[1], ALU.subtract).then_inc(q_cut, 1)
            nc.vector.memset(ONE_ROW[0:1, :].bitcast(F32), TWO_ONES).then_inc(one_row, 1)
            nc.vector.memset(QS[0][0:96, :].bitcast(F32), 0.0).then_inc(qs_zero, 1)
            nc.vector.memset(MX, 0.0).then_inc(mx_zero, 1)
            nc.vector.wait_ge(mx_zero, 1)
            for unit in range(MAXU):
                m = tile_rows(unit)
                dve_running(unit, FIRST_BANKS[unit % 5], m, KC[unit % 3][1], half_ready, HALVES, RUN, mx_read, unit % 3, 3, MX[0:m, unit // 3, :], mx_copied)
            nc.vector.wait_ge(mx_copied, TILES)
            nc.vector.tensor_reduce(MXC, MX, X_AXIS, ALU.max, negate=True).then_inc(mxc_ready, 1)
            nc.vector.wait_ge(va_init, 8)
            for c in range(3):
                dve_vev(c, 0, 0, turn(4 + c)[0])

            def body(b, u, more):
                nxt = 0
                for kt in range(KT):
                    if more:
                        for g in range(4):
                            for _ in range(max_units(kt, g)):
                                dve_max(nxt, b + 1)
                                nxt += 1
                        if kt in V_AT:
                            dve_vev(V_AT.index(kt), 1 - u, b + 1, job(f"V{V_AT.index(kt)}", b, more)[0])
                nc.vector.wait_ge(pt_free, b * KT + (KT + 2))
                nc.vector.wait_ge(accn_ready, b + 1)
                nc.vector.tensor_copy(AS, PS[:, 5, 0:HT]).then_inc(acc_free, 1)
            steps(nc.vector, body)
            dve_residual(2, wts["l0_bo"][:, 0:1])

        def sp_queries(dst, done, b):
            for t, (pq, _) in enumerate(TERMS):
                for s in range(2):
                    r0 = 16 * t + 8 * s
                    nc.sync.dma_start(dst[r0:r0 + 8, :].rearrange("d (p s q) -> d p s q", p=8, s=2)[:, :, s, :],
                                      a["q_parts"][pq].rearrange("(p s d) n -> s d p n", s=2, d=8)[s][:, :, bass.ds(b * L, L)]).then_inc(done, 16)

        def sp_keys(kb, u, after=()):
            again = [(kst_ld[u], loads_until(kb, u, 96) - 96)] if not isinstance(kb, int) or kb > 1 else []
            waits(nc.sync, *after, (k_cut, kb * 9 + 9), *again)
            nc.sync.dma_start(a["k_parts"][u].rearrange("i p n -> p i n"), KPARTS[:, u:u + 3, :]).then_inc(kp_st, 16)
            nc.sync.wait_ge(kp_st, kb * 16 + 16)
            for t, (_, pk) in enumerate(TERMS):
                nc.sync.dma_start(KST[u][16 * t:16 * t + 16, :, :],
                                  a["k_parts"][u, (pk - u) % 3].rearrange("(p i) n -> i p n", i=16)).then_inc(kst_ld[u], 16)

        def sp_mrow(b, u, free):
            nc.sync.wait_ge(job_free[free[0]], free[1] + 1)
            nc.sync.dma_start(QS[u][96:97, 0:128 * (TILES - 1)], MB[0:TILES - 1, :]).then_inc(mrow_ld, 16)
            nc.sync.dma_start(QS[u][96:97, 128 * (TILES - 1):16 * L], MB[TILES - 1:TILES, 0:TLAST]).then_inc(mrow_ld, 16)

        def load_ctx(engine, b, u):
            engine.dma_start(CT[u][:, :], a["ctx_t"][bass.ds(b, 1)].rearrange("b p n -> (b p) n")).then_inc(ctx_ld[u], 16)

        def sp_xattn0():
            nc.sync.wait_ge(x_ready, 2)
            nc.sync.wait_ge(one_row, 1)
            for u in range(2):
                nc.sync.dma_start(KST[u][96:97, :, :], ONE_ROW[0:1, :].unsqueeze(1).broadcast_to([1, 8, S])).then_inc(ones_ld, 16)
            nc.sync.wait_ge(q_cut, 5)
            for i in range(3):
                nc.sync.dma_start(a["q_parts"][i], QP[i]).then_inc(qp_st, 16)
            nc.sync.wait_ge(qp_st, 48)
            nc.sync.wait_ge(qs_zero, 1)
            sp_queries(QS[0], qs_ld, 0)
            sp_keys(0, 0)
            sp_mrow(0, 0, turn(3))
            sp_keys(1, 1)
            nc.sync.wait_ge(qs1_zero, 1)

            def body(b, u, more):
                if more:
                    nc.sync.wait_ge(unit_done, b * UNITS + 1)
                    sp_queries(QS[1 - u], qs_ld, b + 1)
                if more:
                    sp_mrow(b + 1, 1 - u, job("M", b, more))
                if more == 2:
                    sp_keys(b + 2, u, [(unit_done, b * UNITS + UNITS)])
            steps(nc.sync, body)

        f32, _ = carve(STAGE5_HIGH + 6 * 1024)
        PT_F, QT_F, MIX = f32(128), f32(128), f32(128)
        ft_mm, ft_ev = sem("ft_mm"), sem("ft_ev")

        def pe_fourier_matrix():
            nc.tensor.wait_ge(ld["late"], 16)
            w = wts
            nc.tensor.matmul(PS[:, 6, 0:128], w["ft_wr"][:, :], w["ft_c"][:, :], start=True, stop=False)
            nc.tensor.matmul(PS[:, 6, 0:128], w["ft_wi"][:, :], w["ft_s"][:, :], start=False, stop=True).then_inc(ft_mm, 1)
            nc.tensor.matmul(PS[:, 7, 0:128], w["ft_wi"][:, :], w["ft_c"][:, :], start=True, stop=False)
            nc.tensor.matmul(PS[:, 7, 0:128], w["ft_wr"][:, :], w["ft_ns"][:, :], start=False, stop=True).then_inc(ft_mm, 1)
            nc.tensor.wait_ge(ft_ev, 2)
            nc.tensor.matmul(PS[:, 6, 0:128], PT_F, w["ft_cd"][:, :], start=True, stop=False)
            nc.tensor.matmul(PS[:, 6, 0:128], QT_F, w["ft_nsd"][:, :], start=False, stop=True).then_inc(ft_mm, 1)

        def dve_fourier_matrix():
            for i, m in enumerate((PT_F, QT_F, MIX)):
                nc.vector.wait_ge(ft_mm, i + 1)
                nc.vector.tensor_copy(m, PS[:, 6 + i % 2, 0:128]).then_inc(ft_ev, 1)

        def pe_fourier():
            pe_x(2)
            nc.tensor.wait_ge(ft_ev, 3)
            for j in range(2):
                nc.tensor.matmul(PS[:, 4 + j, 0:HT], MIX, half(X[0], j), start=True, stop=True).then_inc(op_done, 1)

        KB_DVE = 5
        SMALL_SEMS = {s: sem("small_" + s) for s in (
            "qk_mm", "v_mm", "q_ready", "k_ready", "va_zero", "va_one", "v_ready", "kb_dve", "kb_act", "qb_loaded0", "qb_loaded1",
            "vb_loaded0", "vb_loaded1", "s_mm", "max_ready", "subtracted", "exp_done", "t_mm", "pt_ready", "pv_done", "as_ready",
            "den_mm", "ln_done", "rd_ready", "acc_ready")}

        class Small:

            def __init__(self, first, heads, scale, w, src, src_ready, src_count):
                self.heads, self.scale, self.R, self.w = heads, scale, heads // 8, w
                self.src, self.src_ready, self.src_count = src, src_ready, src_count
                f32, _ = carve(0)
                self.KB = f32(B * heads * L).rearrange("p (b n) -> p b n", b=B)
                self.KF, self.QF = f32(T), f32(T)
                self.VA = f32(B * 256).rearrange("p (b g n) -> p b g n", b=B, g=8)
                self.QB = [f32(L) for _ in range(2)]
                self.VB = [f32(256) for _ in range(2)]
                self.SS = [f32(8 * L) for _ in range(2)]
                self.PT = [f32(8 * L) for _ in range(2)]
                self.NM = [f32(8) for _ in range(2)]
                self.AS = [f32(2 * L) for _ in range(2)]
                self.RD = [f32(2 * L) for _ in range(2)]
                self.ACC = f32(2 * self.R * T).rearrange("p (i n) -> p i n", i=2 * self.R)
                self.s = SMALL_SEMS
                self.first = first
                self.at_x = 6 if first is None else 10
                self.mask = wts["of_head"] if heads == 16 else wts["of_head8"]

            def before(self, name):
                once = dict(qk_mm=2, v_mm=2, q_ready=1, k_ready=1, va_zero=1, va_one=1, v_ready=2)
                if self.first is None:
                    return 0
                if name in once:
                    return once[name]
                if name in ("kb_dve", "kb_act"):
                    return self.first.R * (KB_DVE if name == "kb_dve" else 8 - KB_DVE)
                return 16 * B // 2 if "loaded" in name else B * self.first.R

        def scores_view(v):
            return v.rearrange("p j (h n) -> p j h n", h=4)

        SMALL_CREDITS = dict(subtracted=2, t_mm=2, pt_ready=1, pv_done=2, as_ready=1, ln_done=1, acc_ready=2)

        def pe_small(q):
            s = q.s
            nc.tensor.wait_ge(q.src_ready, q.src_count)
            nc.tensor.wait_ge(ld["late"], 16)
            for i, n in enumerate(("wq", "wk")):
                for j in range(2):
                    m = nc.tensor.matmul(PS[:, 2 * i + j, 0:HT], wts[q.w + n][:, :], half(q.src, j), start=True, stop=True)
                m.then_inc(s["qk_mm"], 1)
            for b in range(B):
                m = nc.tensor.matmul(PS[0:L, 4 + b // 4, b % 4 * 128:b % 4 * 128 + 128], q.src[:, b * L:(b + 1) * L], wts[q.w + "wv"][:, :], start=True, stop=True)
                if b % 4 == 3:
                    m.then_inc(s["v_mm"], 1)

            if q.R == 2:
                pe_product5(0)

            def scores(b, par, r, i, qpar, qcount):
                nc.tensor.wait_ge(s[f"qb_loaded{qpar}"], qcount)
                nc.tensor.wait_ge(s["subtracted"], q.before("subtracted") + i + 1)
                for j in range(2):
                    m = nc.tensor.matmul(PS[0:L, 2 * par + j, 0:HT], q.QB[qpar], q.KB[:, b, bass.ds((8 * r + 4 * j) * L, 4 * L)] if isinstance(b, int)
                                         else q.KB_FLAT[:, bass.ds(b * (q.heads * L) + (8 * r + 4 * j) * L, 4 * L)], start=True, stop=True)
                m.then_inc(s["s_mm"], 1)

            def transposes(i, par):
                nc.tensor.wait_ge(s["exp_done"], q.before("exp_done") + i + 1)
                nc.tensor.wait_ge(s["pt_ready"], q.before("pt_ready") + i + 1)
                for h in range(8):
                    m = nc.tensor.transpose(PS[0:L, 4 + h // 4, h % 4 * L:(h % 4 + 1) * L], q.SS[par][0:L, h * L:(h + 1) * L], wts["ident"][0:L, 0:L])
                m.then_inc(s["t_mm"], 1)

            nc.tensor.wait_ge(s["q_ready"], q.before("q_ready") + 1)
            for i in range(2):
                b, r = i // q.R, i % q.R
                nc.tensor.wait_ge(s["kb_dve"], q.before("kb_dve") + (r + 1) * KB_DVE)
                nc.tensor.wait_ge(s["kb_act"], q.before("kb_act") + (r + 1) * (8 - KB_DVE))
                scores(b, i, r, i, b, q.before(f"qb_loaded{b}") + 16)
                if i == 0:
                    nc.tensor.wait_ge(s["v_ready"], q.before("v_ready") + 2)
                    transposes(0, 0)

            def body(b, u, more):
                for r in range(q.R):
                    i, par = b * q.R + r, (u * q.R + r) % 2
                    if more:
                        nb, nu = (b + 1, 1 - u) if q.R == 2 else (b + 2, u)
                        scores(nb, par, r, i + 2, nu, q.before(f"qb_loaded{nu}") + ctx_count(nb, nu))
                    if r == 0:
                        nc.tensor.wait_ge(s[f"vb_loaded{u}"], q.before(f"vb_loaded{u}") + ctx_count(b, u))
                    nc.tensor.wait_ge(s["pt_ready"], q.before("pt_ready") + i + 2)
                    nc.tensor.wait_ge(s["as_ready"], q.before("as_ready") + i + 1)
                    groups = 4 * (2 // q.R)
                    w = 8 * L // groups
                    for g in range(groups):
                        j, c = g % 4, g // 4
                        at = (4 * r + g) * 32
                        m = nc.tensor.matmul(PS[32 * j:32 * j + 32, 6, c * w:(c + 1) * w], q.VB[u][0:L, at:at + 32], q.PT[par][0:L, g * w:(g + 1) * w],
                                             start=(c == 0), stop=True, skip_group_check=True)
                    m.then_inc(s["pv_done"], 1)
                    if not isinstance(i, int) or i < B * q.R - 1:
                        transposes(i + 1, 1 - par)
                    nc.tensor.wait_ge(s["as_ready"], q.before("as_ready") + i + 2)
                    nc.tensor.wait_ge(s["ln_done"], q.before("ln_done") + i + 1)
                    nc.tensor.matmul(PS[:, 7, 0:2 * L], wts["seld"][:, :], q.AS[par], start=True, stop=True).then_inc(s["den_mm"], 1)
            steps_small(nc.tensor, q, body)

        def steps_small(engine, q, body):
            with engine.Fori(0, B // 2 - 1) as pair:
                for u in range(2):
                    body(pair * 2 + u, u, True)
            body(B - 2, 0, q.R == 2)
            body(B - 1, 1, False)

        def dve_small(q):
            s = q.s
            nc.vector.wait_ge(s["qk_mm"], q.before("qk_mm") + 1)
            nc.vector.tensor_scalar(two(q.QF), PS[:, 0:2, 0:HT], wts[q.w + "bq"][:, 0:1], q.scale, ALU.add, ALU.mult).then_inc(s["q_ready"], 1)
            def block_keys(r):
                for h in range(8 * r, 8 * r + KB_DVE):
                    nc.vector.tensor_scalar(q.KB[:, :, h * L:(h + 1) * L], by_batch(q.KF), q.mask[:, h:h + 1], None, ALU.mult).then_inc(s["kb_dve"], 1)
            nc.vector.wait_ge(s["k_ready"], q.before("k_ready") + 1)
            block_keys(0)
            bias = wts[q.w + "bv"][0:L, :].rearrange("p (g n) -> p g n", g=8)
            for c in range(2):
                nc.vector.wait_ge(s["v_mm"], q.before("v_mm") + c + 1)
                m = nc.vector.tensor_tensor(q.VA[0:L, 4 * c:4 * c + 4, :, 0:16], PS[0:L, 4 + c, :].rearrange("p (b g n) -> p b g n", b=4, g=8),
                                            bias.unsqueeze(1).broadcast_to([L, 4, 8, 16]), ALU.add)
                m.then_inc(s["v_ready"], 1)

            def views(par):
                return scores_view(PS[0:L, 2 * par:2 * par + 2, 0:HT]), q.NM[par][0:L, :].rearrange("p (j h) -> p j h", j=2)

            def maxima(i, par):
                nc.vector.wait_ge(s["s_mm"], q.before("s_mm") + i + 1)
                nc.vector.tensor_reduce(views(par)[1], views(par)[0], X_AXIS, ALU.max).then_inc(s["max_ready"], 1)

            def subtract(i, par):
                sc, nm = views(par)
                nc.vector.wait_ge(s["max_ready"], q.before("max_ready") + i + 1)
                nc.vector.wait_ge(s["t_mm"], q.before("t_mm") + i + 1)
                nc.vector.tensor_tensor(q.SS[par][0:L, :].rearrange("p (j h n) -> p j h n", j=2, h=4), sc,
                                        nm.unsqueeze(3).broadcast_to([L, 2, 4, L]), ALU.subtract).then_inc(s["subtracted"], 1)
            for i in range(2):
                if i == 1 and q.R == 2:
                    block_keys(1)
                maxima(i, i)
                subtract(i, i)

            def body(b, u, more):
                for r in range(q.R):
                    i, par = b * q.R + r, (u * q.R + r) % 2
                    if more:
                        maxima(i + 2, par)
                        subtract(i + 2, par)
            steps_small(nc.vector, q, body)

        def act_small(q):
            s = q.s
            nc.scalar.wait_ge(s["qk_mm"], q.before("qk_mm") + 2)
            nc.scalar.activation(two(q.KF), PS[:, 2:4, 0:HT], ACT.Identity, bias=wts[q.w + "bk"][:, 0:1]).then_inc(s["k_ready"], 1)
            nc.scalar.wait_ge(s["k_ready"], q.before("k_ready") + 1)
            for r in range(q.R):
                for h in range(8 * r + KB_DVE, 8 * r + 8):
                    nc.scalar.activation(q.KB[:, :, h * L:(h + 1) * L], by_batch(q.KF), ACT.Copy, scale=q.mask[:, h:h + 1]).then_inc(s["kb_act"], 1)

            if q.R == 2:
                act_product5(0)

            def expo(i, par):
                nc.scalar.wait_ge(s["subtracted"], q.before("subtracted") + i + 3)
                nc.scalar.activation(q.SS[par][0:L, :], q.SS[par][0:L, :], ACT.Exp).then_inc(s["exp_done"], 1)
            def turned(i, par):
                nc.scalar.wait_ge(s["t_mm"], q.before("t_mm") + i + 3)
                nc.scalar.wait_ge(s["pv_done"], q.before("pv_done") + i + 1)
                nc.scalar.activation(two(q.PT[par][0:L, :]), PS[0:L, 4:6, 0:HT], ACT.Copy).then_inc(s["pt_ready"], 1)
            expo(0, 0)
            expo(1, 1)
            turned(0, 0)

            def body(b, u, more):
                for r in range(q.R):
                    i, par = b * q.R + r, (u * q.R + r) % 2
                    nc.scalar.wait_ge(s["pv_done"], q.before("pv_done") + i + 3)
                    nc.scalar.wait_ge(s["acc_ready"], q.before("acc_ready") + i + 1)
                    nc.scalar.activation(q.AS[par], PS[:, 6, 0:2 * L], ACT.Copy).then_inc(s["as_ready"], 1)
                    if not isinstance(i, int) or i < B * q.R - 1:
                        turned(i + 1, 1 - par)
                    nc.scalar.wait_ge(s["den_mm"], q.before("den_mm") + i + 1)
                    nc.scalar.wait_ge(s["acc_ready"], q.before("acc_ready") + i + 1)
                    nc.scalar.activation(q.RD[par], PS[:, 7, 0:2 * L], ACT.Ln).then_inc(s["ln_done"], 1)
                    nc.scalar.wait_ge(s["ln_done"], q.before("ln_done") + i + 2)
                    nc.scalar.activation(q.RD[par], q.RD[par], ACT.Exp, scale=-1.0).then_inc(s["rd_ready"], 1)
                    if more:
                        expo(i + 2, par)
            steps_small(nc.scalar, q, body)

        def pool_small(q):
            s = q.s
            nc.gpsimd.wait_ge(x_ready, q.at_x)
            nc.gpsimd.memset(q.VA[0:L, :, :, 17:32], 0.0).then_inc(s["va_zero"], 1)
            nc.gpsimd.memset(q.VA[0:L, :, :, 16:17], 1.0).then_inc(s["va_one"], 1)

            def body(b, u, more):
                for r in range(q.R):
                    i, par = b * q.R + r, (u * q.R + r) % 2
                    nc.gpsimd.wait_ge(s["rd_ready"], q.before("rd_ready") + i + 1)
                    nc.gpsimd.tensor_tensor(q.ACC[:, 2 * r:2 * r + 2, bass.ds(b * L, L)], q.AS[par].rearrange("p (c n) -> p c n", c=2),
                                            q.RD[par].rearrange("p (c n) -> p c n", c=2), ALU.mult).then_inc(s["acc_ready"], 1)
            steps_small(nc.gpsimd, q, body)

        def sp_small(q):
            s = q.s
            def queries(b, u):
                nc.sync.dma_start(q.QB[u], q.QF[:, bass.ds(b * L, L)]).then_inc(s[f"qb_loaded{u}"], 16)

            def values(b, u):
                nc.sync.dma_start(q.VB[u][0:L, :], q.VA_FLAT[0:L, bass.ds(b * 256, 256)]).then_inc(s[f"vb_loaded{u}"], 16)
            nc.sync.wait_ge(s["q_ready"], q.before("q_ready") + 1)
            for b in range(2):
                queries(b, b)
            nc.sync.wait_ge(s["v_ready"], q.before("v_ready") + 2)
            nc.sync.wait_ge(s["va_zero"], q.before("va_zero") + 1)
            nc.sync.wait_ge(s["va_one"], q.before("va_one") + 1)
            for b in range(2):
                values(b, b)
            def more_queries(b, u):
                nc.sync.wait_ge(s["s_mm"], q.before("s_mm") + (b - 1) * q.R)
                queries(b, u)

            def more_values(b, u):
                nc.sync.wait_ge(s["pv_done"], q.before("pv_done") + (b * q.R - q.R + 2))
                values(b, u)
            ahead = 2 if q.R == 1 else 0
            for b in range(2, 2 + ahead):
                more_queries(b, b % 2)
            with nc.sync.Fori(0, (B - 2 - ahead) // 2) as pair:
                for u in range(2):
                    more_queries(pair * 2 + (u + 2 + ahead), u)
                    more_values(pair * 2 + (u + 2), u)
            for b in range(B - ahead, B):
                more_values(b, b % 2)

        f32, b16 = carve(0)
        QPJ = f32(8 * T)
        CN = [f32(KT * 128).rearrange("p (t d) -> p t d", t=KT) for _ in range(2)]
        CH = b16(S)
        QB5 = [f32(8 * L) for _ in range(2)]
        QH5 = [b16(8 * L) for _ in range(2)]
        SHIFT5 = [f32(8 * L) for _ in range(2)]
        DIAG5 = b16(8 * L)
        PT5 = [f32(8 * L) for _ in range(2)]
        DS, RD5, ZERO = f32(8 * L), f32(8 * L), f32(8 * L)
        MX5, MXC5 = f32(8 * 3).rearrange("p (h c) -> p h c", c=3), f32(8)
        ONES5 = b16(128)
        f32, _ = carve(STAGE5_HIGH)
        GQK = f32(1024).rearrange("p (h n) -> p h n", h=8)
        GVO = f32(1024).rearrange("p (h n) -> p h n", h=8)
        W5 = {n: f32(1024).rearrange("p (h n) -> p h n", h=8) for n in ("x_wq", "x_wk", "x_wv", "x_wo")}
        CO = f32(8 * T).rearrange("p (h n) -> p h n", h=8)
        spare = CO.rearrange("p h n -> p (h n)")
        RUN5 = [spare[:, g * 1024:(g + 1) * 1024].rearrange("p (c n) -> p c n", c=4) for g in range(2)]
        HALVES5 = [spare[:, 2048 + u * 256:2304 + u * 256] for u in range(4)]
        half5, copied5 = sem("half5"), sem("copied5")
        U5 = 2 * KT
        MAX5 = (4, 10)
        w5_ld, g_mm, g_ev, q5_mm, q5_ev = sem("w5_ld"), sem("g_mm"), sem("g_ev"), sem("q5_mm"), sem("q5_ev")
        c5_ld, cn_ld, qb5_ld = ([sem(f"{n}{u}") for u in range(2)] for n in ("c5_ld", "cn_ld", "qb5_ld"))
        ch_ready, qh_ready, mx5_mm, mx5_read, mxc5, diag5, shift_mm, shift5, sub5 = (sem(n) for n in ("ch_ready", "qh_ready", "mx5_mm", "mx5_read", "mxc5", "diag5", "shift_mm", "shift5", "sub5"))
        unit5, exp5, pv5, ds5, den5, ln5, rd5, co5, init5, initp5 = (sem(n) for n in ("unit5", "exp5", "pv5", "ds5", "den5", "ln5", "rd5", "co5", "init5", "initp5"))

        def pe_product5(i):
            l, r = (("x_wq", "x_wk"), ("x_wv", "x_wo"))[i]
            nc.tensor.wait_ge(w5_ld, 64)
            for h in range(8):
                m = nc.tensor.matmul(PS[:, 6 + h // 4, h % 4 * 128:h % 4 * 128 + 128], W5[l][0:64, h, :], W5[r][0:64, h, :], start=True, stop=True)
            m.then_inc(g_mm, 1)

        def act_product5(i):
            nc.scalar.wait_ge(g_mm, i + 1)
            nc.scalar.activation((GQK, GVO)[i].rearrange("p (j h) n -> p j (h n)", j=2), PS[:, 6:8, :], ACT.Copy).then_inc(g_ev, 1)

        def pe_max5(unit, u, b, first=False):
            c, h = unit // 8, unit % 8
            at, n = KC[c]
            if unit == 0:
                nc.tensor.wait_ge(ch_ready, b + 1)
                nc.tensor.wait_ge(qh_ready, b + 1)
            if first:
                pe_first_maxima(unit, mx5_read)
            else:
                nc.tensor.wait_ge(mx5_read, b * U5 + unit + 1)
            bank = FIRST_BANKS[unit % 5] if first else 2 + unit % 2
            nc.tensor.matmul(PS[0:L, bank, 0:n], QH5[u][:, h * L:(h + 1) * L], CH[:, at:at + n], start=True, stop=True).then_inc(mx5_mm, 1)

        def pe_shift5(b):
            nc.tensor.wait_ge(diag5, b + 1)
            nc.tensor.wait_ge(ln5, b if not isinstance(b, int) else max(b, 1))
            for g in range(2):
                m = nc.tensor.matmul(PS[:, 6 + g, 0:HT], ONES5[0:L, :], DIAG5[0:L, g * HT:(g + 1) * HT], start=True, stop=True)
            m.then_inc(shift_mm, 1)

        def pe_xattn5():
            pe_x(4)
            nc.tensor.wait_ge(g_ev, 1)
            for j in range(2):
                for h in range(8):
                    n = 8 * j + h
                    if n >= 4:
                        nc.tensor.wait_ge(q5_ev, n - 3)
                    nc.tensor.matmul(PS[:, n % 4, 0:HT], GQK[:, h, :], half(X[0], j), start=True, stop=True).then_inc(q5_mm, 1)
            nc.tensor.wait_ge(q5_ev, 16)
            for unit in range(U5):
                pe_max5(unit, 0, 0, True)
            pe_product5(1)
            nc.tensor.wait_ge(g_ev, 2)
            pe_shift5(0)

            def pv(b, u, kt, g):
                n = rows(kt)
                if kt == 0 and g == 0:
                    nc.tensor.wait_ge(cn_ld[u], ctx_count(b, u) * 2)
                    nc.tensor.wait_ge(co5, b + 1)
                nc.tensor.wait_ge(exp5, b * U5 + (2 * kt + g + 1 + 2))
                m = nc.tensor.matmul(PS[:, 4 + g, 0:HT], CN[u][0:n, kt, :], PT5[kt % 2][0:n, g * HT:(g + 1) * HT], start=(kt == 0), stop=(kt == KT - 1))
                if g == 1:
                    m.then_inc(pv5, 1)

            def body(b, u, more):
                nxt = 0

                def maxima():
                    nonlocal nxt
                    if more and MAX5[0] <= kt < MAX5[1]:
                        pe_max5(nxt, 1 - u, b + 1)
                        nxt += 1
                nc.tensor.wait_ge(c5_ld[u], ctx_count(b, u))
                nc.tensor.wait_ge(qb5_ld[u], ctx_count(b, u))
                for kt in range(KT):
                    n = rows(kt)
                    for g in range(2):
                        unit = 2 * kt + g
                        nc.tensor.wait_ge(sub5, b * U5 + unit + 1)
                        nc.tensor.matmul(PS[0:n, unit % 2, 0:HT], CT[u][:, kt * 128:kt * 128 + n], QB5[u][:, g * HT:(g + 1) * HT], start=True, stop=True).then_inc(unit5, 1)
                        maxima()
                    for g in range(2):
                        if kt > 0:
                            pv(b, u, kt - 1, g)
                        maxima()
                    if more and kt == 10:
                        pe_shift5(b + 1)
                for g in range(2):
                    pv(b, u, KT - 1, g)
                nc.tensor.wait_ge(ds5, b * KT + (KT + 2))
                nc.tensor.wait_ge(ln5, b + 1)
                nc.tensor.wait_ge(shift5, b + 1 + (1 if more else 0))
                for g in range(2):
                    m = nc.tensor.matmul(PS[:, 6 + g, 0:HT], wts["ones"][:, :], DS[:, g * HT:(g + 1) * HT], start=True, stop=True)
                m.then_inc(den5, 1)
            steps(nc.tensor, body)
            pe_out(CO, GVO, co5, B + 1, 8)

        def act_xattn5():
            for n in range(16):
                h, j = n % 8, n // 8
                nc.scalar.wait_ge(q5_mm, n + 1)
                nc.scalar.activation(QPJ.rearrange("p (b h n) -> p b h n", b=B, h=8)[:, 4 * j:4 * j + 4, h, :],
                                     PS[:, n % 4, 0:HT].rearrange("p (b n) -> p b n", b=4), ACT.Copy, scale=64.0 ** -0.5).then_inc(q5_ev, 1)

            def shift(b, u):
                nc.scalar.wait_ge(shift_mm, b + 1)
                nc.scalar.activation(two(SHIFT5[u]), PS[:, 6:8, 0:HT], ACT.Copy).then_inc(shift5, 1)
            for unit in range(U5):
                act_half(unit, FIRST_BANKS[unit % 5], L, KC[unit // 8][1], mx5_mm, mx5_read, HALVES5, half5)
            act_product5(1)
            shift(0, 0)

            def body(b, u, more):
                for kt in range(KT):
                    n = rows(kt)
                    for g in range(2):
                        unit = 2 * kt + g
                        nc.scalar.wait_ge(sub5, b * U5 + (unit + 3))
                        nc.scalar.activation(PT5[kt % 2][0:n, g * HT:(g + 1) * HT], PT5[kt % 2][0:n, g * HT:(g + 1) * HT], ACT.Exp).then_inc(exp5, 1)
                    if more and kt == 10:
                        shift(b + 1, 1 - u)
                nc.scalar.wait_ge(den5, b + 2)
                nc.scalar.wait_ge(co5, b + 1)
                nc.scalar.activation(two(RD5), PS[:, 6:8, 0:HT], ACT.Ln).then_inc(ln5, 1)
                nc.scalar.wait_ge(ln5, b + 2)
                nc.scalar.activation(RD5, RD5, ACT.Exp, scale=-1.0).then_inc(rd5, 1)
            steps(nc.scalar, body)

        def pool_xattn5():
            nc.gpsimd.wait_ge(x_ready, 8)
            nc.gpsimd.memset(ZERO, 0.0).then_inc(initp5, 1)
            nc.gpsimd.wait_ge(initp5, 1)

            def body(b, u, more):
                for kt in range(KT):
                    n = rows(kt)
                    nc.gpsimd.wait_ge(exp5, b * U5 + (2 * kt + 2 + 2))
                    if kt == 0:
                        nc.gpsimd.wait_ge(den5, b + 1)
                    nc.gpsimd.wait_ge(ds5, b * KT + (kt + 2))
                    nc.gpsimd.tensor_tensor(DS[0:n, :], PT5[kt % 2][0:n, :], (ZERO if kt == 0 else DS)[0:n, :], ALU.add).then_inc(ds5, 1)
            steps(nc.gpsimd, body)

        def dve_xattn5():
            nc.vector.wait_ge(x_ready, 8)
            nc.vector.memset(ONES5, 1.0).then_inc(init5, 1)

            def casts(b, u):
                nc.vector.wait_ge(c5_ld[u], ctx_count(b, u))
                if not isinstance(b, int) or b > 0:
                    nc.vector.wait_ge(mx5_mm, b * U5)
                nc.vector.tensor_copy(CH, CT[u][:, :]).then_inc(ch_ready, 1)
                nc.vector.wait_ge(qb5_ld[u], ctx_count(b, u))
                nc.vector.tensor_copy(QH5[u], QB5[u]).then_inc(qh_ready, 1)

            def maximum(unit, b):
                c, h = unit // 8, unit % 8
                nc.vector.wait_ge(mx5_mm, b * U5 + unit + 1)
                nc.vector.tensor_reduce(MX5[0:L, h, c:c + 1], PS[0:L, 2 + unit % 2, 0:KC[c][1]], X_AXIS, ALU.max).then_inc(mx5_read, 1)

            def diagonals(b):
                nc.vector.wait_ge(mx5_read, b * U5 + (U5 + 2))
                nc.vector.tensor_reduce(MXC5[0:L, 0:8], MX5[0:L, :, :], X_AXIS, ALU.max, negate=True).then_inc(mxc5, 1)
                nc.vector.wait_ge(mxc5, b + 1)
                if not isinstance(b, int) or b > 0:
                    nc.vector.wait_ge(shift_mm, b)
                nc.vector.tensor_tensor(DIAG5[0:L, :].rearrange("p (h n) -> p h n", h=8), wts["ident"][0:L, 0:L].unsqueeze(1).broadcast_to([L, 8, L]),
                                        MXC5[0:L, 0:8].unsqueeze(2).broadcast_to([L, 8, L]), ALU.mult).then_inc(diag5, 1)
            def subtract(b, u, kt, g):
                n, unit = rows(kt), 2 * kt + g
                if kt == 0 and g == 0:
                    nc.vector.wait_ge(shift5, b + 1)
                if g == 0:
                    nc.vector.wait_ge(pv5, b * KT + kt + 1)
                    nc.vector.wait_ge(ds5, b * KT + kt + 1)
                nc.vector.wait_ge(unit5, b * U5 + unit + 1)
                nc.vector.tensor_tensor(PT5[kt % 2][0:n, g * HT:(g + 1) * HT], PS[0:n, unit % 2, 0:HT], SHIFT5[u][0:n, g * HT:(g + 1) * HT], ALU.add).then_inc(sub5, 1)
            casts(0, 0)
            for unit in range(U5):
                c, h = unit // 8, unit % 8
                dve_running(unit, FIRST_BANKS[unit % 5], L, KC[c][1], half5, HALVES5, RUN5, mx5_read, unit % 4, 4, MX5[0:L, h - 3:h + 1, c] if h % 4 == 3 else None, copied5)
            nc.vector.wait_ge(init5, 1)
            nc.vector.wait_ge(copied5, U5 // 4)
            diagonals(0)
            for g in range(2):
                subtract(0, 0, 0, g)

            def body(b, u, more):
                nxt = 0

                def maxima(b_):
                    nonlocal nxt
                    if more and MAX5[0] <= kt < MAX5[1]:
                        maximum(nxt, b_)
                        nxt += 1
                if more:
                    following = own_register(nc.vector, b + 1)
                for kt in range(1, KT):
                    for g in range(2):
                        subtract(b, u, kt, g)
                        if more:
                            maxima(following)
                    for g in range(2):
                        if more:
                            maxima(following)
                    if more and kt == MAX5[0] - 1:
                        casts(b + 1, 1 - u)
                    if more and kt == MAX5[1] - 1:
                        diagonals(b + 1)
                if more:
                    for g in range(2):
                        subtract(b + 1, 1 - u, 0, g)
                nc.vector.wait_ge(pv5, b * KT + (KT + 2))
                nc.vector.wait_ge(rd5, b + 1)
                for g in range(2):
                    m = nc.vector.tensor_tensor(CO[:, 4 * g:4 * g + 4, bass.ds(b * L, L)], PS[:, 4 + g, 0:HT].rearrange("p (h n) -> p h n", h=4),
                                                RD5[:, g * HT:(g + 1) * HT].rearrange("p (h n) -> p h n", h=4), ALU.mult)
                m.then_inc(co5, 1)
            steps(nc.vector, body)
            dve_residual(5, wts["x_bo"][:, 0:1])

        def sp_queries5(b, u):
            nc.sync.dma_start(QB5[u], QPJ[:, bass.ds(b * (8 * L), 8 * L)]).then_inc(qb5_ld[u], 16)

        def sp_context(b, u):
            nc.sync.dma_start(CT[u][:, :], a["ctx_t"][bass.ds(b, 1)].rearrange("b p n -> (b p) n")).then_inc(c5_ld[u], 16)
            flat = a["ctx"].rearrange("b s d -> (b s) d")
            nc.sync.dma_start(CN[u][:, 0:KT - 1, :], flat[bass.ds(b * S, 128 * (KT - 1)), :].rearrange("(t p) d -> p t d", p=128)).then_inc(cn_ld[u], 16)
            nc.sync.dma_start(CN[u][0:KLAST, KT - 1, :], flat[bass.ds(b * S + 128 * (KT - 1), KLAST), :]).then_inc(cn_ld[u], 16)

        def sp_xattn5():
            nc.sync.wait_ge(x_ready, 8)
            sp_context(0, 0)
            nc.sync.wait_ge(q5_ev, 8)
            sp_queries5(0, 0)
            nc.sync.wait_ge(q5_ev, 16)

            def body(b, u, more):
                if more:
                    waits(nc.sync, (unit5, b * U5 + 1), (pv5, b * KT + 2))
                    sp_queries5(b + 1, 1 - u)
                    sp_context(b + 1, 1 - u)
            steps(nc.sync, body)

        xn_core, xn_ready, x_twice = sem("xn_core"), sem("xn_ready"), sem("x_twice")
        XN = CT[0][:, 0:T]
        gqa = Small(None, 16, 8.0 ** -0.5, "g_", X[1], x_ready, 6)
        mha = Small(gqa, 8, 128.0 ** -0.5, "f_", XN, xn_ready, 4)
        for q in (gqa, mha):
            q.KB_FLAT = q.KB.rearrange("p b n -> p (b n)")
            q.VA_FLAT = q.VA.rearrange("p b g n -> p (b g n)")

        def by_expert(v, e):
            return v.rearrange("p (b e n) -> p b e n", e=4, n=L // 4)[:, :, e, :]

        def dve_expert_input():
            for e in range(4):
                if e == 0:
                    nc.vector.wait_ge(xn_core, 2)
                nc.vector.tensor_scalar(by_expert(XN, e), by_expert(NORMED, e), wts["f_nw"][:, e:e + 1], wts["f_nb"][:, e:e + 1], ALU.mult, ALU.add).then_inc(xn_ready, 1)

        def pe_experts_out():
            nc.tensor.wait_ge(mha.s["acc_ready"], mha.before("acc_ready") + B + 2)
            for j in range(2):
                for e in range(4):
                    for r in range(2):
                        m = nc.tensor.matmul(by_expert(PS[:, 4 + j, 0:HT], e), wts["f_wo"][:, 2 * e + r, :], by_expert(mha.ACC[:, r, j * HT:(j + 1) * HT], e),
                                             start=(e == 0 and r == 0), stop=(e == 3 and r == 1), skip_group_check=True)
                m.then_inc(op_done, 1)

        def dve_twice_x():
            nc.vector.tensor_scalar(Z, X[1], 2.0, None, ALU.mult).then_inc(x_twice, 1)

        def dve_experts_residual():
            nc.vector.wait_ge(x_twice, 1)
            for j in range(2):
                nc.vector.wait_ge(op_done, 10 + j + 1)
                for e in range(4):
                    m = nc.vector.scalar_tensor_tensor(out=by_expert(half(Z, j), e), in0=by_expert(PS[:, 4 + j, 0:HT], e), scalar=wts["f_bo"][:, e:e + 1],
                                                       in1=by_expert(half(Z, j), e), op0=ALU.add, op1=ALU.add)
                m.then_inc(z_ready, 1)

        block = ctx.enter_context(nc.Block())

        @block.sync
        def _(sp):
            for s, n in [(scanned, 4), (g_ready, 2), (exp_done, 3), (pt_free, 2), (acc_free, 1), (mx_read, 2), (accn_ready, 1), (job_free[0], 1), (job_free[1], 1),
                         (exp5, 2), (sub5, 2), (pv5, 2), (ds5, 2), (mx5_read, 2), (co5, 1), (ln5, 1), (den5, 1)]:
                sp.sem_inc(s, n)
            for s, n in SMALL_CREDITS.items():
                sp.sem_inc(SMALL_SEMS[s], n)
            sp.dma_start(X[0], a["x_t"]).then_inc(ld["first"], 16)
            for g in ("first", "mamba", "arena", "l0x"):
                sp.dma_start(packs[g], a["pack_" + g]).then_inc(ld[g], 16)
            for b in range(2):
                load_ctx(sp, b, b)
            sp.dma_start(packs["late"], a["pack_late"]).then_inc(ld["late"], 16)
            sp_xattn0()
            sp.wait_ge(x_ready, 4)
            for n in W5:
                sp.dma_start(W5[n][0:64], a[n]).then_inc(w5_ld, 16)
            sp_small(gqa)
            sp_xattn5()
            sp_small(mha)
            for j in range(2):
                sp.wait_ge(x_ready, 10 + j + 1)
                sp.dma_start(a["out_t"][:, j * HT:(j + 1) * HT], half(X[0], j)).then_inc(out_stored, 16)
            sp.wait_ge(out_stored, 32)

        @block.tensor
        def _(pe):
            pe_mamba()
            pe_ln(1, Z, z_ready, 0)
            pe_xattn0()
            pe_ln(2, Z, z_ready, 2)
            pe_fourier_matrix()
            pe_fourier()
            pe_ln(3, Z, z_ready, 4)
            pe_small(gqa)
            pe_out(gqa.ACC, wts["g_wo"], gqa.s["acc_ready"], 2 * B + 2, 4)
            pe_ln(4, Z, z_ready, 6)
            pe_xattn5()
            pe_ln(5, Z, z_ready, 8)
            pe_ln(6, X[1], x_ready, 8)
            pe_small(mha)
            pe_experts_out()
            pe_ln(7, Z, z_ready, 10)

        @block.vector
        def _(dve):
            dve_mamba()
            dve_ln(1, X[1], x_ready)
            dve_xattn0()
            dve_ln(2, X[0], x_ready)
            dve_fourier_matrix()
            dve_residual(3, wts["ft_b"][:, 0:1])
            dve_ln(3, X[1], x_ready)
            dve_small(gqa)
            dve_residual(4, wts["g_bo"][:, 0:1])
            dve_ln(4, X[0], x_ready)
            dve_xattn5()
            dve_ln(5, X[1], x_ready)
            dve_ln(6, NORMED, xn_core)
            dve_expert_input()
            dve_twice_x()
            dve_small(mha)
            dve_experts_residual()
            dve_ln(7, X[0], x_ready)

        @block.scalar
        def _(act):
            act_mamba()
            act_ln(1)
            act_xattn0()
            act_ln(2)
            act_ln(3)
            act_small(gqa)
            act_ln(4)
            act_xattn5()
            act_ln(5)
            act_ln(6)
            act_small(mha)
            act_ln(7)

        @block.gpsimd
        def _(pool):
            pool_mamba()
            pool_xattn0()
            pool_small(gqa)
            pool_xattn5()
            pool_small(mha)


W_RESIDENT = {
    "ident": ("mamba", (128, 128)), "centring": ("mamba", (128, 128)), "ones_d": ("mamba", (128, 128)), "ones": ("mamba", (128, 128)), "seld": ("mamba", (128, 128)),
    "eps": ("mamba", (128, 1)), "one": ("mamba", (128, 1)), "sel32": ("mamba", (128, 32)),
    "of_head": ("mamba", (128, 16)), "of_head8": ("mamba", (128, 8)), "w_in": ("first", (128, 512)), "conv_w": ("mamba", (128, 16)), "conv_b": ("mamba", (128, 4)), "w_xp": ("arena", (128, 2, 2, 128)),
    "w_dt": ("arena", (128, 2, 256)), "dt_b": ("mamba", (128, 4)), "a_log": ("mamba", (128, 64)), "d_skip": ("mamba", (128, 4)),
    "w_out": ("arena", (128, 2, 128)),
    "l0_wq": ("l0x", (128, 128)), "l0_bq": ("l0x", (128, 1)), "l0_wk": ("l0x", (128, 128)), "l0_bk": ("l0x", (128, 1)),
    "l0_wv": ("l0x", (128, 128)), "l0_bv": ("l0x", (128, 128)), "l0_wo": ("l0x", (128, 4, 128)), "l0_bo": ("l0x", (128, 1)),
    "ft_wr": ("late", (128, 128)), "ft_wi": ("late", (128, 128)), "ft_c": ("late", (128, 128)), "ft_s": ("late", (128, 128)),
    "ft_ns": ("late", (128, 128)), "ft_cd": ("late", (128, 128)), "ft_nsd": ("late", (128, 128)), "ft_b": ("late", (128, 1)),
    "g_wq": ("late", (128, 128)), "g_bq": ("late", (128, 1)), "g_wk": ("late", (128, 128)), "g_bk": ("late", (128, 1)),
    "g_wv": ("late", (128, 128)), "g_bv": ("late", (128, 128)), "g_wo": ("late", (128, 4, 128)), "g_bo": ("late", (128, 1)),
    "x_bo": ("late", (128, 1)),
    "f_nw": ("late", (128, 4)), "f_nb": ("late", (128, 4)), "f_wq": ("late", (128, 128)), "f_bq": ("late", (128, 1)),
    "f_wk": ("late", (128, 128)), "f_bk": ("late", (128, 1)), "f_wv": ("late", (128, 128)), "f_bv": ("late", (128, 128)),
    "f_wo": ("late", (128, 8, 128)), "f_bo": ("late", (128, 4)),
}
LOADS = ("first", "mamba", "arena", "l0x", "late")
WIDTH = {g: sum(int(np.prod(shape[1:])) for group, shape in W_RESIDENT.values() if group == g) for g in LOADS}


def layout(i):
    f = np.float32
    g = {k: np.asarray(v) for k, v in i.items()}
    col = lambda v: v.reshape(-1, 1)
    o = {}
    o["x_t"] = g["x"].reshape(T, D).T
    o["ctx"] = g["ctx_1024"]
    o["ctx_t"] = g["ctx_1024"].transpose(0, 2, 1)
    o["ident"] = np.eye(128, dtype=f)
    o["centring"] = (np.eye(128) - 1.0 / D).astype(f)
    o["ones_d"] = np.full((128, 128), 1.0 / D, f)
    o["ones"] = np.ones((128, 128), f)
    o["eps"] = np.full((128, 1), EPS, f)
    o["one"] = np.ones((128, 1), f)
    sel = np.zeros((128, 32), f)
    for r in (0, 64, 96):
        sel[r:r + 32] = np.eye(32, dtype=f)
    o["sel32"] = sel
    o["of_head"] = np.repeat(np.eye(16, dtype=f), 8, axis=0)
    o["of_head8"] = np.repeat(np.eye(8, dtype=f), 16, axis=0)
    seld = np.zeros((128, 128), f)
    for j in range(4):
        seld[32 * j + 16, 32 * j:32 * j + 32] = 1.0
    o["seld"] = seld
    ang = 2 * np.pi * ((np.arange(D)[:, None] * np.arange(D)[None, :]) % D) / D
    c, s = np.cos(ang), np.sin(ang)
    o["ft_c"], o["ft_s"], o["ft_ns"], o["ft_cd"], o["ft_nsd"] = (v.astype(f) for v in (c, s, -s, c / D, -s / D))
    L0 = lambda n: g["L0_attn_" + n]
    o["w_in"] = L0("in_proj_w").T
    two_halves = lambda v, w: np.stack([v, w]).reshape(2, 2, 128, -1).transpose(2, 0, 1, 3)
    o["conv_w"] = two_halves(L0("conv_w"), L0("conv_wb")).reshape(128, 16)
    o["conv_b"] = two_halves(L0("conv_b"), L0("conv_bb")).reshape(128, 4)
    o["dt_b"] = two_halves(L0("dt_proj_b"), L0("dt_proj_bb")).reshape(128, 4)
    o["d_skip"] = two_halves(L0("D"), L0("D_b")).reshape(128, 4)
    o["a_log"] = two_halves(L0("A_log"), L0("A_b_log")).reshape(128, 64)
    w = np.zeros((128, 2, 2, 128), f)
    wd = np.zeros((128, 2, 256), f)
    for d, (xp, dp) in enumerate(((L0("x_proj_w"), L0("dt_proj_w")), (L0("x_proj_wb"), L0("dt_proj_wb")))):
        t = xp.T.reshape(2, 128, DR + 2 * NST).transpose(1, 0, 2)
        for r in (0, 64, 96):
            w[:, d, :, r:r + 32] = t[:, :, DR:]
        w[:, d, :, 32:32 + DR] = t[:, :, :DR]
        wd[32:32 + DR, d] = dp.T
    o["w_xp"], o["w_dt"] = w, wd
    o["w_out"] = L0("out_proj_w").T.reshape(2, 128, 128).transpose(1, 0, 2)

    def masked(wo, hd):
        n = 16 // hd
        r = np.zeros((128, 2 * n, 128), f)
        for p in range(8):
            for s_ in range(n):
                r[32 * (p % 4) + s_ * hd:32 * (p % 4) + (s_ + 1) * hd, n * (p // 4) + s_] = wo[(p * n + s_) * hd:(p * n + s_ + 1) * hd]
        return r
    X0 = lambda n: g["L0_xattn_" + n]
    for n in ("q", "k", "v"):
        o["l0_w" + n] = X0("W" + n)
    o["l0_bq"], o["l0_bk"], o["l0_bo"] = col(X0("bq")), col(X0("bk")), col(X0("bo"))
    o["l0_bv"] = np.broadcast_to(X0("bv"), (128, 128))
    o["l0_wo"] = masked(X0("Wo"), 8)
    o["ft_wr"], o["ft_wi"], o["ft_b"] = g["L0_ffn_w_freq_real"], g["L0_ffn_w_freq_imag"], col(g["L0_ffn_bias"])
    G = lambda n: g["L1_attn_" + n]
    rep = lambda v: np.broadcast_to(v.reshape(-1, 4, 1, 8), (v.size // 32, 4, 4, 8)).reshape(-1, 128)
    o["g_wq"], o["g_bq"], o["g_wo"], o["g_bo"] = G("Wq"), col(G("bq")), masked(G("Wo"), 8), col(G("bo"))
    o["g_wk"], o["g_bk"], o["g_wv"] = rep(G("Wk")), col(rep(G("bk"))), rep(G("Wv"))
    o["g_bv"] = np.broadcast_to(rep(G("bv")), (128, 128))
    Y = lambda n: g["L1_xattn_" + n]
    for n in ("q", "k", "v"):
        o["x_w" + n] = Y("W" + n).T.reshape(8, 64, 128).transpose(1, 0, 2)
    o["x_wo"] = Y("Wo").reshape(8, 64, 128).transpose(1, 0, 2)
    o["x_bo"] = col(Y("bo"))
    F = lambda n: g["L1_ffn_" + n]
    nw, nb, bo = (np.zeros((128, 4), f) for _ in range(3))
    wo = np.zeros((128, 8, 128), f)
    for e in range(4):
        m = D >> e
        nw[:m, e], nb[:m, e], bo[:m, e] = F("norm_w")[:m], F("norm_b")[:m], F("o_b")[:m]
        we = np.zeros((128, 128), f)
        we[:m, :m] = F("o_w")[:m, :m].T
        wo[:, 2 * e:2 * e + 2] = masked(we, 16)
    o["f_nw"], o["f_nb"], o["f_bo"], o["f_wo"] = nw, nb, bo, wo
    for n in ("q", "k", "v"):
        o["f_w" + n] = F(n + "_w").T
    o["f_bq"], o["f_bk"] = col(F("q_b")), col(F("k_b"))
    o["f_bv"] = np.broadcast_to(F("v_b"), (128, 128))
    for group in LOADS:
        o["pack_" + group] = np.concatenate([o.pop(n).reshape(128, -1) for n, (g_, _) in W_RESIDENT.items() if g_ == group], axis=1)
    return {k: np.ascontiguousarray(v) for k, v in o.items()}


def kernel(**inputs):
    import concourse.bacc as bacc
    from concourse.bass_utils import run_bass_kernel_spmd

    nc = bacc.Bacc("TRN2", target_bir_lowering=False, num_devices=1)
    arrays = layout(inputs)
    a = {k: nc.dram_tensor(k, v.shape, mybir.dt.from_np(v.dtype), kind="ExternalInput").ap() for k, v in arrays.items()}
    a["out_t"] = nc.dram_tensor("out_t", (D, T), F32, kind="ExternalOutput").ap()
    a["k_parts"] = nc.dram_tensor("k_parts", (2, 3, 128, S), BF16, kind="Internal").ap()
    a["q_parts"] = nc.dram_tensor("q_parts", (3, 128, T), BF16, kind="Internal").ap()
    build(nc, a)
    out = run_bass_kernel_spmd(nc, [arrays], core_ids=[0]).results[0]["out_t"]
    return out.T.reshape(B, L, D)
```
